# Optimizing a Trainium2 kernel written in Bass

```python
import numpy as np
import jax
import jax.numpy as jnp

def _softmax(x, axis=-1):
    return jax.nn.softmax(x, axis=axis)

def _gelu(x):
    return jax.nn.gelu(x, approximate=True)

def _silu(x):
    return jax.nn.silu(x)

def _sigmoid(x):
    return jax.nn.sigmoid(x)

def _layernorm(x, axis=-1, eps=1e-05):
    m = jnp.mean(x, axis=axis, keepdims=True)
    v = jnp.var(x, axis=axis, keepdims=True)
    return (x - m) / jnp.sqrt(v + eps)

def _scatter_add(tgt, idx, src, axis=0):
    return tgt.at[idx].add(src)

def _segment_sum(src, seg, n):
    return jax.ops.segment_sum(src, seg, n)
kernel_name = 'mk_gnn_resnorm_d4_gnn_r16_6c43f1'

def setup_inputs(seed: int=0):
    np.random.seed(seed)
    _w = jnp.asarray

    def _rec_inputs():
        import jax
        import jax.numpy as jnp
        _gk = jax.random.key(seed)
        x = -0.000202 + 1 * jax.random.normal(jax.random.fold_in(_gk, 1), (6250, 64), jnp.float32)
        src = jax.random.randint(jax.random.fold_in(_gk, 2), (200000,), 0, 6250, jnp.int32)
        dst = jnp.minimum((6250 * jax.random.uniform(jax.random.fold_in(_gk, 3), (200000,)) ** 2.0).astype(jnp.int32), 99999)
        _o = jnp.argsort(dst, stable=True)
        src = src[_o]
        dst = dst[_o]
        edge_attr_16 = 0.000196303 + 1.00016 * jax.random.normal(jax.random.fold_in(_gk, 11), (200000, 16), jnp.float32)
        edge_attr_8 = jax.random.uniform(jax.random.fold_in(_gk, 12), (200000, 8), jnp.float32, 0.0, 1)
        edge_weight = jax.random.uniform(jax.random.fold_in(_gk, 14), (200000,), jnp.float32, 0.0, 0.999998)
        edge_weight1 = jax.random.uniform(jax.random.fold_in(_gk, 15), (200000, 1), jnp.float32, 0.0, 0.999999)
        return (x, src, dst, edge_attr_16, edge_attr_8, edge_weight, edge_weight1)
    x, src, dst, edge_attr_16, edge_attr_8, edge_weight, edge_weight1 = _rec_inputs()

    def _L0_gnn_setup():
        import jax, jax.numpy as jnp
        import numpy as np
        N_NODES = 6250
        N_EDGES = 100000
        C = 64

        def _spline_conv(x, src, dst, u, w, root, bias, n_nodes):
            h0 = x @ w[0]
            h1 = x @ w[1]
            uc = u[:, None]
            msg = (1.0 - uc) * h0[src] + uc * h1[src]
            agg = jax.ops.segment_sum(msg, dst, num_segments=n_nodes)
            deg = jax.ops.segment_sum(jnp.ones_like(u), dst, num_segments=n_nodes)
            agg = agg / jnp.maximum(deg, 1.0)[:, None]
            return agg + x @ root + bias
        key = jax.random.key(seed)
        ks = jax.random.split(key, 10)
        x = jax.random.normal(ks[0], (N_NODES, C), dtype=jnp.float32)
        edge_index = jax.random.randint(ks[1], (2, N_EDGES), 0, N_NODES, dtype=jnp.int64)
        edge_attr = jax.random.uniform(ks[2], (N_EDGES, 1), dtype=jnp.float32)
        s = 1.0 / np.sqrt(C)
        w1 = jax.random.uniform(ks[3], (2, C, C), jnp.float32, -s, s)
        root1 = jax.random.uniform(ks[4], (C, C), jnp.float32, -s, s)
        b1 = jnp.zeros((C,), jnp.float32)
        w2 = jax.random.uniform(ks[5], (2, C, C), jnp.float32, -s, s)
        root2 = jax.random.uniform(ks[6], (C, C), jnp.float32, -s, s)
        b2 = jnp.zeros((C,), jnp.float32)
        return {'x': x, 'edge_index': edge_index, 'edge_attr': edge_attr, 'w1': w1, 'root1': root1, 'b1': b1, 'w2': w2, 'root2': root2, 'b2': b2}
    _L0_gnn_all = _L0_gnn_setup()
    _L0_gnn_in = {k: v for k, v in _L0_gnn_all.items() if k in ('w1', 'root1', 'b1', 'w2', 'root2', 'b2')}
    del _L0_gnn_all

    def _L1_gnn_setup():
        import jax, jax.numpy as jnp
        import numpy as np
        N_NODES = 6250
        N_EDGES = 62500
        D = 64
        NUM_LABELS = 8
        IN_CH = 4 * D
        OUT_CH = 64

        def _leaky_relu(v):
            return jax.nn.leaky_relu(v, negative_slope=0.01)
        key = jax.random.key(seed)
        ks = jax.random.split(key, 8)
        x = jax.random.normal(ks[0], (N_NODES, D), dtype=jnp.float32)
        edge_index = jax.random.randint(ks[1], (2, N_EDGES), 0, N_NODES, dtype=jnp.int32)
        edge_label = jax.random.uniform(ks[2], (N_EDGES, NUM_LABELS), dtype=jnp.float32)
        weight = jax.random.normal(ks[3], (IN_CH, OUT_CH), dtype=jnp.float32) * (1.0 / np.sqrt(IN_CH))
        bias = jax.random.normal(ks[4], (OUT_CH,), dtype=jnp.float32) * 0.01
        trans_weight = jax.random.normal(ks[5], (NUM_LABELS, D), dtype=jnp.float32) * (1.0 / np.sqrt(NUM_LABELS))
        attention_weight = jax.random.normal(ks[6], (D, 1), dtype=jnp.float32) * 0.1
        edge_attention_weight = jax.random.normal(ks[7], (D, 1), dtype=jnp.float32) * 0.1
        agg_weights = jnp.full((3,), 1.0 / 3.0, dtype=jnp.float32)
        return {'x': x, 'edge_index': edge_index, 'edge_label': edge_label, 'weight': weight, 'bias': bias, 'trans_weight': trans_weight, 'attention_weight': attention_weight, 'edge_attention_weight': edge_attention_weight, 'agg_weights': agg_weights}
    _L1_gnn_all = _L1_gnn_setup()
    _L1_gnn_in = {k: v for k, v in _L1_gnn_all.items() if k in ('weight', 'bias', 'trans_weight', 'attention_weight', 'edge_attention_weight', 'agg_weights')}
    del _L1_gnn_all

    def _L2_gnn_setup():
        import jax, jax.numpy as jnp
        import numpy as np
        N = 3125
        E = 50000
        IN = 64
        OUT = 64

        def gcn_conv(x, w, b, row, col, ew, n):
            h = x @ w
            deg = jax.ops.segment_sum(ew, col, num_segments=n)
            dinv = jnp.where(deg > 0, jax.lax.rsqrt(deg), 0.0)
            norm = dinv[row] * ew * dinv[col]
            out = jax.ops.segment_sum(norm[:, None] * h[row], col, num_segments=n)
            return out + b
        key = jax.random.key(seed)
        ks = jax.random.split(key, 8)
        x = jax.random.normal(ks[0], (N, IN), dtype=jnp.float32)
        edge_index = jax.random.randint(ks[1], (2, E), 0, N)
        edge_attr = jax.random.uniform(ks[2], (E,), dtype=jnp.float32)

        def lin(k, i, o):
            return (jax.random.normal(k, (i, o), dtype=jnp.float32) / np.sqrt(i)).astype(jnp.float32)
        return {'x': x, 'edge_index': edge_index, 'edge_attr': edge_attr, 'w1': lin(ks[3], IN, 16), 'b1': jnp.zeros((16,), jnp.float32), 'w2': lin(ks[4], 16, 32), 'b2': jnp.zeros((32,), jnp.float32), 'w3': lin(ks[5], 32, IN), 'b3': jnp.zeros((IN,), jnp.float32), 'lw': lin(ks[6], 2 * IN, OUT), 'lb': jnp.zeros((OUT,), jnp.float32)}
    _L2_gnn_all = _L2_gnn_setup()
    _L2_gnn_in = {k: v for k, v in _L2_gnn_all.items() if k in ('w1', 'b1', 'w2', 'b2', 'w3', 'b3', 'lw', 'lb')}
    del _L2_gnn_all

    def _L3_gnn_setup():
        import jax, jax.numpy as jnp
        import numpy as np
        N, E, IN, OUT, ED = (6250, 100000, 64, 64, 16)
        NEG = -1000000000.0
        key = jax.random.key(seed)
        ks = jax.random.split(key, 8)
        x = jax.random.normal(ks[0], (N, IN), jnp.float32)
        edge_index = jax.random.randint(ks[1], (2, E), 0, N, dtype=jnp.int32)
        edge_attr = jax.random.normal(ks[2], (E, ED), jnp.float32)
        Wn = jax.random.normal(ks[3], (IN, OUT), jnp.float32) * (1.0 / np.sqrt(IN))
        We = jax.random.normal(ks[4], (ED, OUT), jnp.float32) * (1.0 / np.sqrt(ED))
        att_src = jax.random.normal(ks[5], (OUT,), jnp.float32) * 0.02
        att_dst = jax.random.normal(ks[6], (OUT,), jnp.float32) * 0.02
        att_edge = jax.random.normal(ks[7], (OUT,), jnp.float32) * 0.02
        return {'x': x, 'edge_index': edge_index, 'edge_attr': edge_attr, 'Wn': Wn, 'We': We, 'att_src': att_src, 'att_dst': att_dst, 'att_edge': att_edge}
    _L3_gnn_all = _L3_gnn_setup()
    _L3_gnn_in = {k: v for k, v in _L3_gnn_all.items() if k in ('Wn', 'We', 'att_src', 'att_dst', 'att_edge')}
    del _L3_gnn_all
    return {'x': x, 'src': src, 'dst': dst, 'edge_attr_16': edge_attr_16, 'edge_attr_8': edge_attr_8, 'edge_weight': edge_weight, 'edge_weight1': edge_weight1, 'L0_gnn_w1': _L0_gnn_in['w1'], 'L0_gnn_root1': _L0_gnn_in['root1'], 'L0_gnn_b1': _L0_gnn_in['b1'], 'L0_gnn_w2': _L0_gnn_in['w2'], 'L0_gnn_root2': _L0_gnn_in['root2'], 'L0_gnn_b2': _L0_gnn_in['b2'], 'L1_gnn_weight': _L1_gnn_in['weight'], 'L1_gnn_bias': _L1_gnn_in['bias'], 'L1_gnn_trans_weight': _L1_gnn_in['trans_weight'], 'L1_gnn_attention_weight': _L1_gnn_in['attention_weight'], 'L1_gnn_edge_attention_weight': _L1_gnn_in['edge_attention_weight'], 'L1_gnn_agg_weights': _L1_gnn_in['agg_weights'], 'L2_gnn_w1': _L2_gnn_in['w1'], 'L2_gnn_b1': _L2_gnn_in['b1'], 'L2_gnn_w2': _L2_gnn_in['w2'], 'L2_gnn_b2': _L2_gnn_in['b2'], 'L2_gnn_w3': _L2_gnn_in['w3'], 'L2_gnn_b3': _L2_gnn_in['b3'], 'L2_gnn_lw': _L2_gnn_in['lw'], 'L2_gnn_lb': _L2_gnn_in['lb'], 'L3_gnn_Wn': _L3_gnn_in['Wn'], 'L3_gnn_We': _L3_gnn_in['We'], 'L3_gnn_att_src': _L3_gnn_in['att_src'], 'L3_gnn_att_dst': _L3_gnn_in['att_dst'], 'L3_gnn_att_edge': _L3_gnn_in['att_edge']}

def reference(x, src, dst, edge_attr_16, edge_attr_8, edge_weight, edge_weight1, L0_gnn_w1, L0_gnn_root1, L0_gnn_b1, L0_gnn_w2, L0_gnn_root2, L0_gnn_b2, L1_gnn_weight, L1_gnn_bias, L1_gnn_trans_weight, L1_gnn_attention_weight, L1_gnn_edge_attention_weight, L1_gnn_agg_weights, L2_gnn_w1, L2_gnn_b1, L2_gnn_w2, L2_gnn_b2, L2_gnn_w3, L2_gnn_b3, L2_gnn_lw, L2_gnn_lb, L3_gnn_Wn, L3_gnn_We, L3_gnn_att_src, L3_gnn_att_dst, L3_gnn_att_edge):
    import jax
    import jax.numpy as jnp

    def _L0_gnn_ref(x, edge_index, edge_attr, w1, root1, b1, w2, root2, b2):
        import jax, jax.numpy as jnp
        import numpy as np
        N_NODES = 6250
        N_EDGES = 100000
        C = 64

        def _spline_conv(x, src, dst, u, w, root, bias, n_nodes):
            h0 = x @ w[0]
            h1 = x @ w[1]
            uc = u[:, None]
            msg = (1.0 - uc) * h0[src] + uc * h1[src]
            agg = jax.ops.segment_sum(msg, dst, num_segments=n_nodes)
            deg = jax.ops.segment_sum(jnp.ones_like(u), dst, num_segments=n_nodes)
            agg = agg / jnp.maximum(deg, 1.0)[:, None]
            return agg + x @ root + bias
        src, dst = (edge_index[0], edge_index[1])
        u = edge_attr[:, 0]
        n = x.shape[0]
        h = _spline_conv(x, src, dst, u, w1, root1, b1, n)
        h = _spline_conv(h, src, dst, u, w2, root2, b2, n)
        return h

    def _L1_gnn_ref(x, edge_index, edge_label, weight, bias, trans_weight, attention_weight, edge_attention_weight, agg_weights):
        import jax, jax.numpy as jnp
        import numpy as np
        N_NODES = 6250
        N_EDGES = 62500
        D = 64
        NUM_LABELS = 8
        IN_CH = 4 * D
        OUT_CH = 64

        def _leaky_relu(v):
            return jax.nn.leaky_relu(v, negative_slope=0.01)
        n = x.shape[0]
        row, col = (edge_index[0], edge_index[1])
        ef = edge_label @ trans_weight
        node_feat = x[row] * x[col]
        att = jax.nn.sigmoid(_leaky_relu(node_feat @ attention_weight) + _leaky_relu(ef @ edge_attention_weight))
        wef = ef * att
        wnf = x[col] * att
        wsf = x[row] * att
        aw = jax.nn.softmax(agg_weights)
        cnt_row = jax.ops.segment_sum(jnp.ones((row.shape[0],), x.dtype), row, num_segments=n)
        cnt_col = jax.ops.segment_sum(jnp.ones((col.shape[0],), x.dtype), col, num_segments=n)

        def agg3(vals, idx, cnt):
            s = jax.ops.segment_sum(vals, idx, num_segments=n)
            mean = s / jnp.maximum(cnt, 1.0)[:, None]
            mx = jax.ops.segment_max(vals, idx, num_segments=n)
            mx = jnp.where(cnt[:, None] > 0, mx, 0.0)
            return mean * aw[0] + mx * aw[1] + s * aw[2]
        opinion = agg3(wef, row, cnt_row)
        out = agg3(wnf, row, cnt_row)
        inn_opinion = agg3(wef, col, cnt_col)
        inn = agg3(wsf, col, cnt_col)
        cat = jnp.concatenate((out, opinion, inn, inn_opinion), axis=1)
        return cat @ weight + bias

    def _L2_gnn_ref(x, edge_index, edge_attr, w1, b1, w2, b2, w3, b3, lw, lb):
        import jax, jax.numpy as jnp
        import numpy as np
        N = 3125
        E = 50000
        IN = 64
        OUT = 64

        def gcn_conv(x, w, b, row, col, ew, n):
            h = x @ w
            deg = jax.ops.segment_sum(ew, col, num_segments=n)
            dinv = jnp.where(deg > 0, jax.lax.rsqrt(deg), 0.0)
            norm = dinv[row] * ew * dinv[col]
            out = jax.ops.segment_sum(norm[:, None] * h[row], col, num_segments=n)
            return out + b
        n = x.shape[0]
        loop = jnp.arange(n)
        row = jnp.concatenate([edge_index[0], loop])
        col = jnp.concatenate([edge_index[1], loop])
        ew = jnp.concatenate([edge_attr, jnp.ones((n,), edge_attr.dtype)])
        x2 = jax.nn.relu(gcn_conv(x, w1, b1, row, col, ew, n))
        x3 = jax.nn.relu(gcn_conv(x2, w2, b2, row, col, ew, n))
        x4 = jax.nn.relu(gcn_conv(x3, w3, b3, row, col, ew, n))
        h = jnp.concatenate([x, x4], axis=1)
        return h @ lw + lb

    def _L3_gnn_ref(x, edge_index, edge_attr, Wn, We, att_src, att_dst, att_edge):
        import jax, jax.numpy as jnp
        import numpy as np
        N, E, IN, OUT, ED = (6250, 100000, 64, 64, 16)
        NEG = -1000000000.0
        src, dst = (edge_index[0], edge_index[1])
        n = x.shape[0]
        z = x @ Wn
        e = edge_attr @ We
        s_src = (z @ att_src)[src]
        s_dst = (z @ att_dst)[dst]
        s_edge = e @ att_edge
        score = jax.nn.leaky_relu(s_src + s_dst + s_edge, negative_slope=0.2)
        max_per = jnp.maximum(jax.ops.segment_max(score, dst, num_segments=n), NEG)
        score_exp = jnp.exp(score - max_per[dst])
        denom = jax.ops.segment_sum(score_exp, dst, num_segments=n)
        alpha = score_exp / (denom[dst] + 1e-08)
        msg = (z[src] + e) * alpha[:, None]
        out = jax.ops.segment_sum(msg, dst, num_segments=n)
        return out + x
    edge_index = jnp.stack([src, dst])
    x = _layernorm(x + _L0_gnn_ref(x, edge_index, edge_weight1, L0_gnn_w1, L0_gnn_root1, L0_gnn_b1, L0_gnn_w2, L0_gnn_root2, L0_gnn_b2), axis=-1)
    x = _layernorm(x + _L1_gnn_ref(x, edge_index, edge_attr_8, L1_gnn_weight, L1_gnn_bias, L1_gnn_trans_weight, L1_gnn_attention_weight, L1_gnn_edge_attention_weight, L1_gnn_agg_weights), axis=-1)
    x = _layernorm(x + _L2_gnn_ref(x, edge_index, edge_weight, L2_gnn_w1, L2_gnn_b1, L2_gnn_w2, L2_gnn_b2, L2_gnn_w3, L2_gnn_b3, L2_gnn_lw, L2_gnn_lb), axis=-1)
    x = _layernorm(x + _L3_gnn_ref(x, edge_index, edge_attr_16, L3_gnn_Wn, L3_gnn_We, L3_gnn_att_src, L3_gnn_att_dst, L3_gnn_att_edge), axis=-1)
    return x

_drawn_inputs = setup_inputs


def setup_inputs(seed=0):
    import zlib

    import numpy as np

    out = dict(_drawn_inputs(seed))
    spreads = {'L0_gnn_b1': (0.0, 0.1),
     'L0_gnn_b2': (0.0, 0.1),
     'L1_gnn_agg_weights': (0.3333333432674408, 0.6),
     'L2_gnn_b1': (0.0, 0.467),
     'L2_gnn_b2': (0.0, 0.291),
     'L2_gnn_b3': (0.0, 0.1),
     'L2_gnn_lb': (0.0, 0.1)}
    factors = {'edge_weight': 7.993,
     'edge_weight1': 3.313,
     'L1_gnn_bias': 8.0,
     'L1_gnn_edge_attention_weight': 8.0,
     'L3_gnn_att_src': 6.861,
     'L3_gnn_att_dst': 8.0,
     'L3_gnn_att_edge': 2.832}
    for name, (base, spread) in spreads.items():
        noise = np.random.default_rng([zlib.crc32(name.encode()), seed]).standard_normal(out[name].shape)
        drawn = base * np.exp(spread * noise) if base else spread * noise
        out[name] = jnp.asarray(drawn.astype(out[name].dtype))
    for name, factor in factors.items():
        out[name] = (out[name] * factor).astype(out[name].dtype)
    return out
```

```python
from contextlib import ExitStack

import numpy as np

import concourse.bass as bass
from concourse import mybir
from concourse.alu_op_type import AluOpType as ALU

F32 = mybir.dt.float32
BF16 = mybir.dt.bfloat16
I32 = mybir.dt.int32
ACT = mybir.ActivationFunctionType
AX = mybir.AxisListType

P = 128
N = 6250
C = 64
E = 200000
J = -(-N // P)
NP = P * J
B = 16
T = -(-E // (P * 2 * B)) * 2 * B
EP = P * T
IT = T // (2 * B)
LAST = (N - 1) // J
REST = N - LAST * J
LABELS, EDIM = 8, 16
BIG = 1.0e30
ROUND = 12582912.0
GROUP = 4
PAIR = (0, 4, 8, 7)
PAIRS = GROUP * (GROUP + 1) // 2
RANKED = B // 2


class Chain:

    def __init__(self, eng, sem, base=0):
        self.eng, self.sem, self.n = eng, sem, base

    def __call__(self, ins):
        self.n += 1
        ins.then_inc(self.sem, 1)
        self.eng.wait_ge(self.sem, self.n)


class Signal:

    def __init__(self, sem):
        self.sem, self.base = sem, 0


def flat(ap):
    return ap.rearrange("p a b -> p (a b)")


def offsets(ap):
    return bass.IndirectOffsetOnAxis(ap=ap, axis=0)


def dense(nc, sig, xs, weights, out, width):
    G = 7
    with ExitStack() as ctx:
        uid = nc.next_id()
        k_dims = [w.shape[0] for w in weights]
        xin = [ctx.enter_context(nc.sbuf_tensor(f"xin{uid}_{k}", [P, G, d], F32)) for k, d in enumerate(k_dims)]
        xt = [ctx.enter_context(nc.sbuf_tensor(f"xt{uid}_{k}", [d, G, P], F32)) for k, d in enumerate(k_dims)]
        tp = [ctx.enter_context(nc.psum_tensor(f"tp{uid}_{k}", [P, 8, P], F32)) for k in range(len(xs))]
        slot = 64 if width <= 64 else 256
        acc = ctx.enter_context(nc.psum_tensor(f"acc{uid}", [P, 8, slot], F32))
        block = ctx.enter_context(nc.Block())
        K = len(xs)
        copied, turned, turned_sb, product, saved = (sig[n] for n in ("copied", "turned", "turned_sb", "product", "saved"))

        @block.scalar
        def _(act):
            with act.Fori(0, J // G) as i:
                act.wait_ge(turned.sem, turned.base + i)
                for k in range(K):
                    ins = nc.scalar.activation(flat(xin[k][:]), flat(xs[k][:, bass.ds(i * G, G), :]), ACT.Copy)
                ins.then_inc(copied.sem, 1)
                act.wait_ge(product.sem, product.base + i + 1)
                nc.scalar.activation(out[:, bass.ds(i * G, G), 0:width], acc[:, 0:G, 0:width], ACT.Copy).then_inc(saved.sem, 1)

        @block.tensor
        def _(pe):
            with pe.Fori(0, J // G) as i:
                pe.wait_ge(copied.sem, copied.base + i + 1)
                pe.wait_ge(turned_sb.sem, turned_sb.base + i)
                pe.sem_inc(sig["rounds"].sem, 1)
                for k in range(K):
                    for g in range(G):
                        ins = nc.tensor.transpose(tp[k][0:k_dims[k], g, :], xin[k][:, g, :], sig["ident"][:])
                ins.then_inc(turned.sem, 1)
                pe.wait_ge(turned_sb.sem, turned_sb.base + i + 1)
                pe.wait_ge(saved.sem, saved.base + i)
                for g in range(G):
                    for k in range(K):
                        ins = nc.tensor.matmul(acc[:, g, 0:width], xt[k][:, g, :], weights[k], start=(k == 0), stop=(k == K - 1))
                ins.then_inc(product.sem, 1)

        @block.vector
        def _(dve):
            with dve.Fori(0, J // G) as i:
                dve.wait_ge(turned.sem, turned.base + i + 1)
                dve.wait_ge(product.sem, product.base + i)
                for k in range(K):
                    ins = nc.vector.tensor_copy(flat(xt[k][:]), flat(tp[k][0:k_dims[k], 0:G, :]))
                ins.then_inc(turned_sb.sem, 1)

        for s in (copied, turned, turned_sb, product, saved):
            s.base += J // G


def complete_and_fetch(nc, sig, carries, final, n_sum, width, fix_at, running, ends, agg, extra=None):
    link, step_pen, use_pen = carries
    n_max = width - n_sum
    with ExitStack() as ctx:
        uid = nc.next_id()
        fixed = ctx.enter_context(nc.sbuf_tensor(f"fixed{uid}", [P, width], F32))
        ps = ctx.enter_context(nc.psum_tensor(f"pcarry{uid}", [P, 512], F32))
        pt = ctx.enter_context(nc.psum_tensor(f"pcarry_t{uid}", [P, 512], F32))
        tops = ctx.enter_context(nc.sbuf_tensor(f"tops{uid}", [P, P + 1], F32))
        run = ctx.enter_context(nc.sbuf_tensor(f"run{uid}", [P, P + 1], F32))
        block = ctx.enter_context(nc.Block())
        fetched, pe_s, dve_s = sig["fetched"], sig["pe_step"], sig["dve_step"]

        @block.gpsimd
        def _(pool):
            pool.indirect_dma_start(out=fixed[:], out_offset=None, in_=running, in_offset=offsets(fix_at[:])).then_inc(fetched.sem, 16)
            pool.wait_ge(dve_s.sem, dve_s.base + (5 if n_max else 1))
            pool.indirect_dma_start(out=running, out_offset=offsets(fix_at[:]), in_=fixed[:], in_offset=None).then_inc(fetched.sem, 16)
            pool.wait_ge(fetched.sem, fetched.base + 32)
            for j in range(J):
                pool.indirect_dma_start(out=agg[:, j, :], out_offset=None, in_=running, in_offset=offsets(ends[:, j:j + 1])).then_inc(fetched.sem, 16)
            pool.wait_ge(fetched.sem, fetched.base + 32 + 16 * J)

        @block.tensor
        def _(pe):
            nc.tensor.matmul(ps[:, 0:n_sum], link[:], final[:, 0:n_sum], start=True, stop=True).then_inc(pe_s.sem, 1)
            if n_max:
                nc.tensor.transpose(pt[0:n_max, 0:P], final[:, n_sum:width], sig["ident"][:]).then_inc(pe_s.sem, 1)
                pe.wait_ge(dve_s.sem, dve_s.base + 4)
                nc.tensor.transpose(pt[:, P:P + n_max], run[0:n_max, 0:P], sig["ident"][0:n_max, 0:n_max]).then_inc(pe_s.sem, 1)

        @block.vector
        def _(dve):
            step = Chain(dve, dve_s.sem, dve_s.base)
            if n_max:
                dve.wait_ge(pe_s.sem, pe_s.base + 2)
                step(nc.vector.memset(run[0:n_max, 0:1], -BIG))
                step(nc.vector.tensor_tensor_scan(run[0:n_max, 1:P], step_pen[0:n_max, 1:P], pt[0:n_max, 0:P - 1], -BIG, ALU.add, ALU.max))
                step(nc.vector.tensor_tensor(run[0:n_max, 1:P], run[0:n_max, 1:P], use_pen[0:n_max, 1:P], ALU.add))
                step(nc.vector.tensor_scalar(run[0:n_max, 0:P], run[0:n_max, 0:P], -BIG, None, ALU.max))
                dve.wait_ge(pe_s.sem, pe_s.base + 3)
                dve.wait_ge(fetched.sem, fetched.base + 16)
                nc.vector.tensor_tensor(fixed[:, n_sum:width], fixed[:, n_sum:width], pt[:, P:P + n_max], ALU.max)
            dve.wait_ge(pe_s.sem, pe_s.base + 1)
            dve.wait_ge(fetched.sem, fetched.base + 16)
            step(nc.vector.tensor_tensor(fixed[:, 0:n_sum], fixed[:, 0:n_sum], ps[:, 0:n_sum], ALU.add))

        fetched.base += 32 + 16 * J
        pe_s.base += 3 if n_max else 1
        dve_s.base += 5 if n_max else 1


def spread(ap, n):
    return ap.unsqueeze(2).broadcast_to([ap.shape[0], ap.shape[1], n])


def repeat(ap, n):
    return ap.unsqueeze(1).broadcast_to([ap.shape[0], n, ap.shape[1]])


def carry_masks(nc, sig, first, last, link, step_pen, use_pen):
    with ExitStack() as ctx:
        uid = nc.next_id()
        diag = ctx.enter_context(nc.sbuf_tensor(f"diag{uid}", [P, P], F32))
        near = ctx.enter_context(nc.sbuf_tensor(f"near{uid}", [P, 2 * P], F32))
        ps = ctx.enter_context(nc.psum_tensor(f"pmask{uid}", [P, 512], F32))
        block = ctx.enter_context(nc.Block())
        pe_s, dve_s = sig["pe_step"], sig["dve_step"]

        @block.tensor
        def _(pe):
            pe.wait_ge(dve_s.sem, dve_s.base + 1)
            nc.tensor.matmul(ps[:, 0:P], sig["ones"][:], diag[:], start=True, stop=True).then_inc(pe_s.sem, 1)
            pe.wait_ge(dve_s.sem, dve_s.base + 4)
            nc.tensor.matmul(ps[:, P:3 * P], sig["ones"][:], near[:], start=True, stop=True).then_inc(pe_s.sem, 1)

        @block.vector
        def _(dve):
            step = Chain(dve, dve_s.sem, dve_s.base)
            step(nc.vector.tensor_scalar(diag[:], sig["ident"][:], first, None, ALU.mult))
            dve.wait_ge(pe_s.sem, pe_s.base + 1)
            step(nc.vector.scalar_tensor_tensor(link[:], ps[:, 0:P], last, sig["upper"][:], ALU.is_equal, ALU.mult))
            step(nc.vector.tensor_tensor(near[:, 0:P], link[:], sig["shift2"][:], ALU.mult))
            step(nc.vector.tensor_tensor(near[:, P:2 * P], link[:], sig["shift1"][:], ALU.mult))
            dve.wait_ge(pe_s.sem, pe_s.base + 2)
            step(nc.vector.tensor_scalar(step_pen[:], ps[:, P:2 * P], BIG, -BIG, ALU.mult, ALU.add))
            step(nc.vector.tensor_scalar(use_pen[:], ps[:, 2 * P:3 * P], BIG, -BIG, ALU.mult, ALU.add))

        pe_s.base += 2
        dve_s.base += 6


def node_ranges(nc, sig, cnt, begin, end_row, begin_row):
    with ExitStack() as ctx:
        uid = nc.next_id()
        upto = ctx.enter_context(nc.sbuf_tensor(f"upto{uid}", [P, J], F32))
        has = ctx.enter_context(nc.sbuf_tensor(f"has{uid}", [P, J], F32))
        tmp = ctx.enter_context(nc.sbuf_tensor(f"rtmp{uid}", [P, J], F32))
        ps = ctx.enter_context(nc.psum_tensor(f"pbefore{uid}", [P, 512], F32))
        block = ctx.enter_context(nc.Block())
        pe_s, dve_s = sig["pe_step"], sig["dve_step"]

        @block.tensor
        def _(pe):
            pe.wait_ge(dve_s.sem, dve_s.base + 1)
            nc.tensor.matmul(ps[:, 0:1], sig["upper"][:], upto[:, J - 1:J], start=True, stop=True).then_inc(pe_s.sem, 1)

        @block.vector
        def _(dve):
            step = Chain(dve, dve_s.sem, dve_s.base)
            step(nc.vector.tensor_tensor_scan(upto[:], sig["ones"][:, 0:J], cnt[:], 0.0, ALU.mult, ALU.add))
            dve.wait_ge(pe_s.sem, pe_s.base + 1)
            step(nc.vector.tensor_scalar(upto[:], upto[:], ps[:, 0:1], None, ALU.add))
            step(nc.vector.tensor_tensor(begin[:], upto[:], cnt[:], ALU.subtract))
            step(nc.vector.tensor_scalar(has[:], cnt[:], 0.0, None, ALU.is_gt))
            for ahead, rows, offset in ((upto, end_row, -1.0), (begin, begin_row, 0.0)):
                if rows is not None:
                    step(nc.vector.scalar_tensor_tensor(tmp[:], ahead[:], offset - EP, has[:], ALU.add, ALU.mult))
                    step(nc.vector.tensor_scalar(rows[:], tmp[:], float(EP), None, ALU.add))

        pe_s.base += 1
        dve_s.base += 4 + 2 * ((end_row is not None) + (begin_row is not None))


def layer_norm(nc, sig, x, y, out):
    with ExitStack() as ctx:
        uid = nc.next_id()
        s = ctx.enter_context(nc.sbuf_tensor(f"lnsum{uid}", [P, J], F32))
        sq = ctx.enter_context(nc.sbuf_tensor(f"lnsq{uid}", [P, J, C], F32))
        std = ctx.enter_context(nc.sbuf_tensor(f"lnstd{uid}", [P, J], F32))
        block = ctx.enter_context(nc.Block())
        act_s, dve_s = sig["act_step"], sig["dve_step"]

        @block.vector
        def _(dve):
            step = Chain(dve, dve_s.sem, dve_s.base)
            step(nc.vector.tensor_tensor(flat(y[:]), flat(x[:]), flat(y[:]), ALU.add))
            step(nc.vector.tensor_reduce(s[:], y[:], AX.X, ALU.add))
            step(nc.vector.tensor_scalar(s[:], s[:], 1.0 / C, None, ALU.mult))
            step(nc.vector.tensor_tensor(y[:], y[:], spread(s[:], C), ALU.subtract))
            step(nc.vector.tensor_tensor(flat(sq[:]), flat(y[:]), flat(y[:]), ALU.mult))
            step(nc.vector.tensor_reduce(s[:], sq[:], AX.X, ALU.add))
            step(nc.vector.tensor_scalar(s[:], s[:], 1.0 / C, 1e-5, ALU.mult, ALU.add))
            dve.wait_ge(act_s.sem, act_s.base + 1)
            step(nc.vector.reciprocal(s[:], std[:]))
            step(nc.vector.tensor_tensor(out[:], y[:], spread(s[:], C), ALU.mult))

        @block.scalar
        def _(act):
            act.wait_ge(dve_s.sem, dve_s.base + 7)
            nc.scalar.activation(std[:], s[:], ACT.Sqrt).then_inc(act_s.sem, 1)

        act_s.base += 1
        dve_s.base += 9


def weighted_pass(nc, sig, kind, table, width, table_width, edge, running, final, zeros, cleared=()):
    count, ranked, extra = "count" in edge, edge.get("ranked"), "extra" in edge
    rank = ranked is not None
    per = {"spline": 2, "gcn": 1}[kind] + B + 2 * count + 4 * rank
    with ExitStack() as ctx:
        uid = nc.next_id()

        def sb(name, shape, dt=F32):
            return ctx.enter_context(nc.sbuf_tensor(f"{name}{uid}", shape, dt))

        def pair(name, shape, dt=F32):
            return [sb(f"{name}{h}_", shape, dt) for h in range(2)]

        def sem(name):
            return ctx.enter_context(nc.semaphore(f"{name}{uid}"))

        index = pair("index", [P, B], I32)
        weight = pair("weight", [P, B])
        keep = pair("keep", [P, B])
        rows = pair("rows", [P, B, table_width])
        msg = pair("msg", [P, B, width])
        run = pair("run", [P, B, width])
        gathered = [sem(f"gathered{h}_") for h in range(2)]
        stored = [sem(f"stored{h}_") for h in range(2)]
        staged = [sem(f"staged{h}_") for h in range(2)]
        stepped = sem("stepped")
        if count:
            dst_lo, dst_hi = pair("dst_lo", [P, B]), pair("dst_hi", [P, B])
            at_lo, at_hi = pair("at_lo", [P, B, P], BF16), pair("at_hi", [P, B, J], BF16)
            blank = sb("blank", [P, P], BF16)
            p_count = ctx.enter_context(nc.psum_tensor(f"p_count{uid}", [P, 512], F32))
            counted = sem("counted")
        if rank:
            lo, hi = pair("lo", [P, RANKED]), pair("hi", [P, RANKED])
            one_lo, one_hi = pair("one_lo", [P, RANKED, P], BF16), pair("one_hi", [P, RANKED, J], BF16)
            lo_t, lo_tf = pair("lo_t", [P, GROUP, P], BF16), pair("lo_tf", [P, GROUP, P])
            earlier = pair("earlier", [P, PAIRS, P], BF16)
            seen = pair("seen", [P, J])
            picked = sb("picked", [P, RANKED, J])
            p_seen = ctx.enter_context(nc.psum_tensor(f"p_seen{uid}", [P, 512], F32))
            p_turn = ctx.enter_context(nc.psum_tensor(f"p_turn{uid}", [P, 8, P], BF16))
            p_same = ctx.enter_context(nc.psum_tensor(f"p_same{uid}", [P, 12, P], F32))
            p_look = ctx.enter_context(nc.psum_tensor(f"p_look{uid}", [P, RANKED, C], F32))
            turned, turned_sb, same, same_sb, summed, seen_sb, looked = (sem(n) for n in ("turned", "turned_sb", "same", "same_sb", "summed", "seen_sb", "looked"))
        block = ctx.enter_context(nc.Block())
        running_v = running[0:EP, :].rearrange("(p t) c -> p t c", p=P)
        INIT = 1 + 3 * count + 3 * rank
        Q = RANKED // GROUP

        @block.sync
        def _(sp):
            sp.dma_start(running[EP:EP + 1, :], zeros[0:1, 0:width]).then_inc(stored[0], 16)
            with sp.Fori(0, IT) as i:
                for h in range(2):
                    sp.wait_ge(stepped, INIT + per * (2 * i + h + 1))
                    sp.dma_start(running_v[:, bass.ds((2 * i + h) * B, B), :], run[h][:]).then_inc(stored[h], 16)
                    for dst in cleared:
                        sp.dma_start(dst[:, bass.ds((2 * i + h) * B, B), :], zeros[:, 0:B * dst.shape[2]].rearrange("p (t c) -> p t c", t=B)).then_inc(stored[h], 16)
            for h in range(2):
                sp.wait_ge(stored[h], 16 * IT * (1 + len(cleared)) + 16 * (h == 0))

        @block.gpsimd
        def _(pool):
            with pool.Fori(0, IT) as i:
                for h in range(2):
                    pool.wait_ge(staged[h], i + 1)
                    pool.sem_inc(sig["rounds"].sem, 1)
                    for k in range(B):
                        pool.indirect_dma_start(out=rows[h][:, k, :], out_offset=None, in_=table,
                                                in_offset=offsets(index[h][:, k:k + 1])).then_inc(gathered[h], 16)

        @block.scalar
        def _(act):
            def stage(h, at):
                nc.scalar.activation(weight[h][:], edge["weight"][:, bass.ds(at, B)], ACT.Copy)
                nc.scalar.activation(keep[h][:], edge["keep"][:, bass.ds(at, B)], ACT.Copy)
                if extra:
                    nc.scalar.activation(msg[h][:, :, C], edge["extra"][:, bass.ds(at, B)], ACT.Copy)
                if count:
                    nc.scalar.activation(dst_lo[h][:], edge["dst_lo"][:, bass.ds(at, B)], ACT.Copy)
                    nc.scalar.activation(dst_hi[h][:], edge["dst_hi"][:, bass.ds(at, B)], ACT.Copy)
                if rank:
                    nc.scalar.activation(lo[h][:], edge["src_lo"][:, bass.ds(at + ranked, RANKED)], ACT.Copy)
                    nc.scalar.activation(hi[h][:], edge["src_hi"][:, bass.ds(at + ranked, RANKED)], ACT.Copy)
                nc.scalar.copy(index[h][:], edge["src"][:, bass.ds(at, B)]).then_inc(staged[h], 1)

            def ranks(i, h):
                n = (2 * i + h) * Q
                turn_out(n, 0)
                for q in range(Q):
                    act.wait_ge(same, n + q + 1)
                    nc.scalar.activation(flat(earlier[q % 2][:]), flat(p_same[:, 0:PAIRS, :]), ACT.Relu).then_inc(same_sb, 1)
                    if q + 1 < Q:
                        turn_out(n + q + 1, q + 1)
                    act.wait_ge(summed, n + q + 1)
                    nc.scalar.activation(seen[(q + 1) % 2][:], p_seen[:, 0:J], ACT.Copy).then_inc(seen_sb, 1)

            def turn_out(n, q):
                act.wait_ge(turned, n + 1)
                nc.scalar.activation(flat(lo_t[q % 2][:]), flat(p_turn[:, 0:GROUP, :]), ACT.Copy)
                nc.scalar.activation(flat(lo_tf[q % 2][:]), flat(p_turn[:, 0:GROUP, :]), ACT.Copy).then_inc(turned_sb, 1)

            stage(0, 0)
            with act.Fori(0, IT) as i:
                act.wait_ge(stepped, INIT + per * (2 * i))
                stage(1, (2 * i + 1) * B)
                if rank:
                    ranks(i, 0)
                act.wait_ge(stepped, INIT + per * (2 * i + 1))
                stage(0, (2 * i + 2) * B)
                if rank:
                    ranks(i, 1)
            if count:
                act.wait_ge(counted, T + 1)
                nc.scalar.activation(edge["count"][:], p_count[:, 0:J], ACT.Copy).then_inc(staged[0], 1)
            if rank:
                act.wait_ge(summed, 2 * IT * Q)
                nc.scalar.activation(edge["seen"][:], p_seen[:, 0:J], ACT.Copy).then_inc(staged[0], 1)

        if count or rank:
            @block.tensor
            def _(pe):
                pe.wait_ge(stepped, INIT)
                if count:
                    nc.tensor.matmul(p_count[:, 0:J], blank[:], blank[:, 0:J], start=True, stop=False)

                def turn(n, h, q):
                    pe.wait_ge(turned_sb, n)
                    for k in range(GROUP):
                        ins = nc.tensor.transpose(p_turn[:, k, :], one_lo[h][:, q * GROUP + k, :], sig["ident_b"][:])
                    ins.then_inc(turned, 1)

                def ranks(i, h):
                    n = (2 * i + h) * Q
                    turn(n, h, 0)
                    for q in range(Q):
                        pe.wait_ge(turned_sb, n + q + 1)
                        pe.wait_ge(same_sb, n + q)
                        low = lo_t[q % 2]
                        for j in range(GROUP):
                            nc.tensor.matmul(p_same[:, PAIR[j], :], low[:, j, :], low[:, j, :], start=True, stop=False)
                            ins = nc.tensor.matmul(p_same[:, PAIR[j], :], sig["ident_b"][:], sig["not_earlier"][:], start=False, stop=True)
                            if j + 1 < GROUP:
                                ins = nc.tensor.matmul(p_same[:, PAIR[j] + 1:PAIR[j] + GROUP - j, :], low[:, j, :], low[:, j + 1:GROUP, :], start=True, stop=True)
                        ins.then_inc(same, 1)
                        if q + 1 < Q:
                            turn(n + q + 1, h, q + 1)
                        pe.wait_ge(seen_sb, n + q)
                        nc.tensor.matmul(p_seen[:, 0:J], sig["ident"][:], seen[q % 2][:], start=True, stop=False)
                        for k in range(GROUP):
                            kk = q * GROUP + k
                            ins = nc.tensor.matmul(p_seen[:, 0:J], one_lo[h][:, kk, :], one_hi[h][:, kk, :], start=False, stop=k == GROUP - 1)
                        ins.then_inc(summed, 1)
                        pe.wait_ge(same_sb, n + q + 1)
                        for k in range(GROUP):
                            kk = q * GROUP + k
                            nc.tensor.matmul(p_look[:, kk, 0:J], lo_tf[q % 2][:, k, :], seen[q % 2][:], start=True, stop=False)
                            for j in range(k + 1):
                                ins = nc.tensor.matmul(p_look[:, kk, 0:J], earlier[q % 2][:, PAIR[j] + k - j, :], one_hi[h][:, q * GROUP + j, :], start=False, stop=j == k)
                        ins.then_inc(looked, 1)

                with pe.Fori(0, IT) as i:
                    for h in range(2):
                        pe.wait_ge(stepped, INIT + per * (2 * i + h))
                        if rank:
                            ranks(i, h)
                        if count:
                            for k in range(B):
                                nc.tensor.matmul(p_count[:, 0:J], at_lo[h][:, k, :], at_hi[h][:, k, :], start=False, stop=False).then_inc(counted, 1)
                if count:
                    nc.tensor.matmul(p_count[:, 0:J], blank[:], blank[:, 0:J], start=False, stop=True).then_inc(counted, 1)

        @block.vector
        def _(dve):
            def one_hots(h, step):
                if count:
                    step(nc.vector.tensor_tensor(at_lo[h][:], repeat(sig["iota"][:], B), spread(dst_lo[h][:], P), ALU.is_equal))
                    step(nc.vector.tensor_tensor(at_hi[h][:], repeat(sig["iota"][:, 0:J], B), spread(dst_hi[h][:], J), ALU.is_equal))
                if rank:
                    step(nc.vector.tensor_tensor(one_lo[h][:], repeat(sig["iota"][:], RANKED), spread(lo[h][:], P), ALU.is_equal))
                    step(nc.vector.tensor_tensor(one_hi[h][:], repeat(sig["iota"][:, 0:J], RANKED), spread(hi[h][:], J), ALU.is_equal))

            nc.vector.memset(run[1][:, B - 1, :], 0.0).then_inc(stepped, 1)
            if count:
                nc.vector.memset(blank[:], 0.0).then_inc(stepped, 1)
            if rank:
                nc.vector.tensor_copy(seen[0][:], edge["seen"][:]).then_inc(stepped, 1)
            if count or rank:
                dve.wait_ge(staged[0], 1)
                one_hots(0, lambda ins: ins.then_inc(stepped, 1))
            with dve.Fori(0, IT) as i:
                for h in range(2):
                    n = [0]

                    def step(ins):
                        ins.then_inc(stepped, 1)
                        n[0] += 1

                    def after():
                        dve.wait_ge(stepped, INIT + per * (2 * i + h) + n[0])

                    dve.wait_ge(staged[h], i + 1)
                    dve.wait_ge(gathered[h], 16 * B * (i + 1))
                    if kind == "spline":
                        step(nc.vector.tensor_tensor(msg[h][:, :, 0:C], rows[h][:, :, C:2 * C], spread(weight[h][:], C), ALU.mult))
                        after()
                        step(nc.vector.tensor_tensor(msg[h][:, :, 0:C], msg[h][:, :, 0:C], rows[h][:, :, 0:C], ALU.add))
                    else:
                        step(nc.vector.tensor_tensor(msg[h][:], rows[h][:], spread(weight[h][:], width), ALU.mult))
                    dve.wait_ge(stored[h], 16 * (1 + len(cleared)) * i + 16 * (h == 0))
                    for k in range(B):
                        before = run[h][:, k - 1, :] if k else run[1 - h][:, B - 1, :]
                        after()
                        step(nc.vector.scalar_tensor_tensor(run[h][:, k, :], before, keep[h][:, k:k + 1], msg[h][:, k, :], ALU.mult, ALU.add))
                    if count or rank:
                        dve.wait_ge(staged[1 - h], i + 1 + h)
                    if count:
                        dve.wait_ge(counted, B * (2 * i + h))
                    if count or rank:
                        one_hots(1 - h, step)
                    if rank:
                        dve.wait_ge(looked, Q * (2 * i + h + 1))
                        step(nc.vector.tensor_tensor(picked[:], p_look[:, :, 0:J], one_hi[h][:], ALU.mult))
                        after()
                        step(nc.vector.tensor_reduce(edge["rank"][:, bass.ds((2 * i + h) * B + ranked, RANKED)], picked[:], AX.X, ALU.add))
                    assert n[0] == per
            dve.wait_ge(stepped, INIT + per * 2 * IT)
            nc.vector.tensor_copy(final[:, 0:width], run[1][:, B - 1, :]).then_inc(stepped, 1)


def spread_to_edges(nc, sig, node_rows, begin_row, edge_rows, table, first_key, first_rows):
    with ExitStack() as ctx:
        block = ctx.enter_context(nc.Block())
        fetched = sig["fetched"]

        @block.gpsimd
        def _(pool):
            pool.indirect_dma_start(out=first_rows[:], out_offset=None, in_=table, in_offset=offsets(first_key)).then_inc(fetched.sem, 16)
            for j in range(J):
                pool.indirect_dma_start(out=edge_rows, out_offset=offsets(begin_row[:, j:j + 1]), in_=node_rows[:, j, :], in_offset=None,
                                        bounds_check=EP - 1, oob_is_err=False).then_inc(fetched.sem, 16)
            pool.wait_ge(fetched.sem, fetched.base + 16 * (J + 1))

        fetched.base += 16 * (J + 1)


def attention_pass(nc, sig, table, edge, labels, node_rows, first_rows, w_label, w_label_att, running, final, sent, zeros):
    KEY, OUT0, LABEL0, IN0, WIDE = 0, 1, 1 + C, 1 + 2 * C, 1 + 3 * C
    per = 1 + B + 10 + 2 * B
    with ExitStack() as ctx:
        def sb(name, shape, dt=F32):
            return ctx.enter_context(nc.sbuf_tensor(name, shape, dt))

        def pair(name, shape, dt=F32):
            return [sb(f"{name}{h}", shape, dt) for h in range(2)]

        def sem(name):
            return ctx.enter_context(nc.semaphore(name))

        index, place = pair("a_index", [P, B], I32), pair("a_place", [P, B], I32)
        keep, pen, rank, key = pair("a_keep", [P, B]), pair("a_pen", [P, B]), pair("a_rank", [P, B]), pair("a_key", [P, B])
        rows = pair("a_rows", [P, B, 2 * C + 1])
        begun, xdst = pair("a_begun", [P, B, C]), pair("a_xdst", [P, B, C])
        label = pair("a_label", [LABELS, B * P])
        product = sb("a_product", [P, B, C])
        score = pair("a_score", [P, B])
        label_score, att = pair("a_label_score", [P, B]), pair("a_att", [P, B])
        msg = pair("a_msg", [P, B, WIDE])
        run = pair("a_run", [P, B, 4 * C])
        p_label = [ctx.enter_context(nc.psum_tensor(f"a_p_label{h}", [P, B, C], F32)) for h in range(2)]
        p_score = [ctx.enter_context(nc.psum_tensor(f"a_p_score{h}", [P, 512], F32)) for h in range(2)]
        gathered, stored, staged, loaded, scattered = ([sem(f"a_{n}{h}") for h in range(2)] for n in ("gathered", "stored", "staged", "loaded", "scattered"))
        stepped, labelled, activated = sem("a_stepped"), sem("a_labelled"), sem("a_activated")
        block = ctx.enter_context(nc.Block())
        running_v = running[0:EP, :].rearrange("(p t) c -> p t c", p=P)
        node_rows_v = node_rows[0:EP, :].rearrange("(p t) c -> p t c", p=P)
        INIT = per
        PLACED = 1 + B + 10

        @block.sync
        def _(sp):
            def load(h, n):
                sp.dma_start(begun[h][:], node_rows_v[:, bass.ds(n * B, B), :]).then_inc(loaded[h], 16)
                sp.dma_start(label[h][:], labels[:, bass.ds(n * (B * P), B * P)]).then_inc(loaded[h], 16)

            def store(h, i):
                sp.wait_ge(stepped, INIT + per * (2 * i + h + 1))
                sp.dma_start(running_v[:, bass.ds((2 * i + h) * B, B), :], run[h][:]).then_inc(stored[h], 16)

            sp.dma_start(running[EP:EP + 1, :], zeros[0:1, 0:4 * C]).then_inc(stored[0], 16)
            load(0, 0)
            load(1, 1)
            with sp.Fori(0, IT - 1) as i:
                for h in range(2):
                    store(h, i)
                    load(h, 2 * i + 2 + h)
            for h in range(2):
                store(h, IT - 1)
            for h in range(2):
                sp.wait_ge(stored[h], 16 * IT + 16 * (h == 0))

        @block.gpsimd
        def _(pool):
            def gather(h, i):
                pool.wait_ge(staged[h], i + 1)
                pool.sem_inc(sig["rounds"].sem, 1)
                for k in range(B):
                    pool.indirect_dma_start(out=rows[h][:, k, :], out_offset=None, in_=table,
                                            in_offset=offsets(index[h][:, k:k + 1])).then_inc(gathered[h], 16)

            def scatter(h, i):
                pool.wait_ge(stepped, INIT + per * (2 * i + h) + PLACED)
                pool.sem_inc(sig["rounds"].sem, 1)
                for k in range(B):
                    pool.indirect_dma_start(out=sent, out_offset=offsets(place[h][:, k:k + 1]), in_=msg[h][:, k, KEY:IN0],
                                            in_offset=None).then_inc(scattered[h], 16)

            gather(0, 0)
            with pool.Fori(0, IT - 1) as i:
                gather(1, i)
                scatter(0, i)
                gather(0, i + 1)
                scatter(1, i)
            gather(1, IT - 1)
            scatter(0, IT - 1)
            scatter(1, IT - 1)
            for h in range(2):
                pool.wait_ge(scattered[h], 16 * B * IT)

        @block.scalar
        def _(act):
            def stage(h, at):
                nc.scalar.activation(keep[h][:], edge["keep"][:, bass.ds(at, B)], ACT.Copy)
                nc.scalar.activation(rank[h][:], edge["rank"][:, bass.ds(at, B)], ACT.Copy)
                nc.scalar.activation(key[h][:], edge["src"][:, bass.ds(at, B)], ACT.Copy)
                nc.scalar.copy(index[h][:], edge["src"][:, bass.ds(at, B)]).then_inc(staged[h], 1)

            def attention(h, i):
                act.wait_ge(labelled, 2 * i + h + 1)
                nc.scalar.activation(label_score[h][:], p_score[h][:, 0:B], ACT.Copy).then_inc(activated, 1)
                act.wait_ge(stepped, INIT + per * (2 * i + h) + 1 + B + 5)
                nc.scalar.activation(att[h][:], score[h][:], ACT.Sigmoid).then_inc(activated, 1)

            stage(0, 0)
            with act.Fori(0, IT) as i:
                act.wait_ge(stepped, INIT + per * (2 * i))
                stage(1, (2 * i + 1) * B)
                attention(0, i)
                act.wait_ge(stepped, INIT + per * (2 * i + 1))
                stage(0, (2 * i + 2) * B)
                attention(1, i)

        @block.tensor
        def _(pe):
            with pe.Fori(0, IT) as i:
                for h in range(2):
                    pe.wait_ge(loaded[h], 32 * (i + 1))
                    pe.wait_ge(stepped, per * (2 * i + h))
                    for k in range(B):
                        edges = label[h][:, k * P:(k + 1) * P]
                        nc.tensor.matmul(p_label[h][:, k, :], edges, w_label, start=True, stop=True)
                        ins = nc.tensor.matmul(p_score[h][:, k:k + 1], edges, w_label_att, start=True, stop=True)
                    ins.then_inc(labelled, 1)

        @block.vector
        def _(dve):
            nc.vector.memset(run[1][:, B - 1, 0:2 * C], 0.0).then_inc(stepped, 1)
            nc.vector.memset(run[1][:, B - 1, 2 * C:4 * C], -BIG).then_inc(stepped, 1)
            nc.vector.tensor_copy(xdst[1][:, B - 1, :], first_rows[:, C:2 * C]).then_inc(stepped, INIT - 2)
            with dve.Fori(0, IT) as i:
                for h in range(2):
                    n = [0]

                    def step(ins):
                        ins.then_inc(stepped, 1)
                        n[0] += 1

                    def after(back=0):
                        dve.wait_ge(stepped, INIT + per * (2 * i + h) + n[0] - back)

                    dve.wait_ge(staged[h], i + 1)
                    step(nc.vector.tensor_scalar(pen[h][:], keep[h][:], BIG, -BIG, ALU.mult, ALU.add))
                    dve.wait_ge(loaded[h], 32 * (i + 1))
                    for k in range(B):
                        before = xdst[h][:, k - 1, :] if k else xdst[1 - h][:, B - 1, :]
                        after()
                        step(nc.vector.scalar_tensor_tensor(xdst[h][:, k, :], before, keep[h][:, k:k + 1], begun[h][:, k, :], ALU.mult, ALU.add))
                    dve.wait_ge(gathered[h], 16 * B * (i + 1))
                    after()
                    step(nc.vector.tensor_tensor(product[:], rows[h][:, :, 0:C], xdst[h][:], ALU.mult))
                    after()
                    step(nc.vector.tensor_reduce(score[h][:], product[:], AX.X, ALU.add))
                    after()
                    step(nc.vector.scalar_tensor_tensor(score[h][:], score[h][:], 0.01, score[h][:], ALU.mult, ALU.max))
                    dve.wait_ge(activated, 2 * (2 * i + h) + 1)
                    step(nc.vector.scalar_tensor_tensor(label_score[h][:], label_score[h][:], 0.01, label_score[h][:], ALU.mult, ALU.max))
                    after()
                    step(nc.vector.tensor_tensor(score[h][:], score[h][:], label_score[h][:], ALU.add))
                    dve.wait_ge(activated, 2 * (2 * i + h) + 2)
                    dve.wait_ge(scattered[h], 16 * B * i)
                    step(nc.vector.tensor_tensor(msg[h][:, :, OUT0:LABEL0], xdst[h][:], spread(att[h][:], C), ALU.mult))
                    step(nc.vector.tensor_tensor(msg[h][:, :, LABEL0:IN0], p_label[h][:], spread(att[h][:], C), ALU.mult))
                    step(nc.vector.tensor_tensor(msg[h][:, :, IN0:WIDE], rows[h][:, :, C:2 * C], spread(att[h][:], C), ALU.mult))
                    step(nc.vector.tensor_copy(msg[h][:, :, KEY], key[h][:]))
                    step(nc.vector.tensor_tensor(place[h][:], rows[h][:, :, 2 * C], rank[h][:], ALU.add))
                    dve.wait_ge(stored[h], 16 * i + 16 * (h == 0))
                    after(1)
                    for k in range(B):
                        before = run[h][:, k - 1, :] if k else run[1 - h][:, B - 1, :]
                        if k:
                            after(1)
                        step(nc.vector.scalar_tensor_tensor(run[h][:, k, 0:2 * C], before[:, 0:2 * C], keep[h][:, k:k + 1],
                                                            msg[h][:, k, LABEL0:WIDE], ALU.mult, ALU.add))
                        if k:
                            after(1)
                        step(nc.vector.scalar_tensor_tensor(run[h][:, k, 2 * C:4 * C], before[:, 2 * C:4 * C], pen[h][:, k:k + 1],
                                                            msg[h][:, k, LABEL0:WIDE], ALU.add, ALU.max))
                    assert n[0] == per, n
            dve.wait_ge(stepped, INIT + per * 2 * IT)
            nc.vector.tensor_copy(final[:], run[1][:, B - 1, :]).then_inc(stepped, 1)


def source_pass(nc, sig, sent, running, final, first_last, zeros):
    per = 4 + 2 * B
    W = 2 * C
    with ExitStack() as ctx:
        def pair(name, shape, dt=F32):
            return [ctx.enter_context(nc.sbuf_tensor(f"{name}{h}", shape, dt)) for h in range(2)]

        def sem(name):
            return ctx.enter_context(nc.semaphore(name))

        rows = pair("s_rows", [P, B, 1 + W])
        run = pair("s_run", [P, B, 2 * W])
        keep, pen = pair("s_keep", [P, B]), pair("s_pen", [P, B])
        last_key = ctx.enter_context(nc.sbuf_tensor("s_last_key", [P, 1], F32))
        loaded, stored = ([sem(f"s_{n}{h}") for h in range(2)] for n in ("loaded", "stored"))
        stepped, ends_loaded = sem("s_stepped"), sem("s_ends_loaded")
        block = ctx.enter_context(nc.Block())
        running_v = running[0:EP, :].rearrange("(p t) c -> p t c", p=P)
        sent_v = sent.rearrange("(p t) c -> p t c", p=P)
        INIT = per

        @block.sync
        def _(sp):
            sp.dma_start(running[EP:EP + 1, :], zeros[0:1, 0:2 * W]).then_inc(stored[0], 16)
            with sp.Fori(0, IT) as i:
                for h in range(2):
                    sp.wait_ge(stepped, INIT + per * (2 * i + h + 1))
                    sp.dma_start(running_v[:, bass.ds((2 * i + h) * B, B), :], run[h][:]).then_inc(stored[h], 16)
            for h in range(2):
                sp.wait_ge(stored[h], 16 * IT + 16 * (h == 0))

        @block.scalar
        def _(act):
            act.dma_start(first_last[:, 0:2], sent_v[:, 0, 0:2]).then_inc(ends_loaded, 16)
            act.dma_start(first_last[:, 2:4], sent_v[:, T - 1, 0:2]).then_inc(ends_loaded, 16)
            with act.Fori(0, IT) as i:
                for h in range(2):
                    act.wait_ge(stepped, per * (2 * i + h))
                    act.dma_start(rows[h][:], sent_v[:, bass.ds((2 * i + h) * B, B), :]).then_inc(loaded[h], 16)
            act.wait_ge(ends_loaded, 32)

        @block.vector
        def _(dve):
            nc.vector.memset(run[1][:, B - 1, 0:W], 0.0).then_inc(stepped, 1)
            nc.vector.memset(run[1][:, B - 1, W:2 * W], -BIG).then_inc(stepped, 1)
            nc.vector.memset(last_key[:], -1.0).then_inc(stepped, INIT - 2)
            with dve.Fori(0, IT) as i:
                for h in range(2):
                    n = [0]

                    def step(ins):
                        ins.then_inc(stepped, 1)
                        n[0] += 1

                    def after(back=0):
                        dve.wait_ge(stepped, INIT + per * (2 * i + h) + n[0] - back)

                    dve.wait_ge(loaded[h], 16 * (i + 1))
                    after()
                    step(nc.vector.tensor_tensor(keep[h][:, 0:1], rows[h][:, 0, 0:1], last_key[:], ALU.is_equal))
                    step(nc.vector.tensor_tensor(keep[h][:, 1:B], rows[h][:, 1:B, 0], rows[h][:, 0:B - 1, 0], ALU.is_equal))
                    after()
                    step(nc.vector.tensor_copy(last_key[:], rows[h][:, B - 1, 0:1]))
                    step(nc.vector.tensor_scalar(pen[h][:], keep[h][:], BIG, -BIG, ALU.mult, ALU.add))
                    dve.wait_ge(stored[h], 16 * i + 16 * (h == 0))
                    after()
                    for k in range(B):
                        before = run[h][:, k - 1, :] if k else run[1 - h][:, B - 1, :]
                        if k:
                            after(1)
                        step(nc.vector.scalar_tensor_tensor(run[h][:, k, 0:W], before[:, 0:W], keep[h][:, k:k + 1], rows[h][:, k, 1:1 + W], ALU.mult, ALU.add))
                        if k:
                            after(1)
                        step(nc.vector.scalar_tensor_tensor(run[h][:, k, W:2 * W], before[:, W:2 * W], pen[h][:, k:k + 1], rows[h][:, k, 1:1 + W], ALU.add, ALU.max))
                    assert n[0] == per, n
            dve.wait_ge(stepped, INIT + per * 2 * IT)
            nc.vector.tensor_copy(final[:], run[1][:, B - 1, :]).then_inc(stepped, 1)


def softmax_pass(nc, sig, table, edge, attrs, w_edge, w_edge_att, running, final, zeros):
    per = 13 + B + 1
    S, W = C + 1, C + 2
    with ExitStack() as ctx:
        def sb(name, shape, dt=F32):
            return ctx.enter_context(nc.sbuf_tensor(name, shape, dt))

        def pair(name, shape, dt=F32):
            return [sb(f"{name}{h}", shape, dt) for h in range(2)]

        def sem(name):
            return ctx.enter_context(nc.semaphore(name))

        index = pair("e_index", [P, B], I32)
        keep, pen, at_dst = pair("e_keep", [P, B]), pair("e_pen", [P, B]), pair("e_at_dst", [P, B])
        rows = pair("e_rows", [P, B, W])
        attr = pair("e_attr", [EDIM, B * P])
        edge_score, score, bounded = pair("e_edge_score", [P, B]), pair("e_score", [P, B]), pair("e_bounded", [P, B])
        top = pair("e_top", [P, 1 + B])
        exps = pair("e_exps", [P, 2 * B])
        factor = pair("e_factor", [P, 2 * B])
        msg = pair("e_msg", [P, B, S])
        run = pair("e_run", [P, B, W])
        p_edge = [ctx.enter_context(nc.psum_tensor(f"e_p_edge{h}", [P, B, C], F32)) for h in range(2)]
        p_score = [ctx.enter_context(nc.psum_tensor(f"e_p_score{h}", [P, 512], F32)) for h in range(2)]
        gathered, stored, staged, loaded = ([sem(f"e_{n}{h}") for h in range(2)] for n in ("gathered", "stored", "staged", "loaded"))
        stepped, projected, activated = sem("e_stepped"), sem("e_projected"), sem("e_activated")
        block = ctx.enter_context(nc.Block())
        running_v = running[0:EP, :].rearrange("(p t) c -> p t c", p=P)
        INIT = per

        @block.sync
        def _(sp):
            def load(h, n):
                sp.dma_start(attr[h][:], attrs[:, bass.ds(n * (B * P), B * P)]).then_inc(loaded[h], 16)

            def store(h, i):
                sp.wait_ge(stepped, INIT + per * (2 * i + h + 1))
                sp.dma_start(running_v[:, bass.ds((2 * i + h) * B, B), :], run[h][:]).then_inc(stored[h], 16)

            sp.dma_start(running[EP:EP + 1, :], zeros[0:1, 0:W]).then_inc(stored[0], 16)
            load(0, 0)
            load(1, 1)
            with sp.Fori(0, IT - 1) as i:
                for h in range(2):
                    store(h, i)
                    load(h, 2 * i + 2 + h)
            for h in range(2):
                store(h, IT - 1)
            for h in range(2):
                sp.wait_ge(stored[h], 16 * IT + 16 * (h == 0))

        @block.gpsimd
        def _(pool):
            with pool.Fori(0, IT) as i:
                for h in range(2):
                    pool.wait_ge(staged[h], i + 1)
                    pool.sem_inc(sig["rounds"].sem, 1)
                    for k in range(B):
                        pool.indirect_dma_start(out=rows[h][:, k, :], out_offset=None, in_=table,
                                                in_offset=offsets(index[h][:, k:k + 1])).then_inc(gathered[h], 16)

        @block.scalar
        def _(act):
            def stage(h, at):
                nc.scalar.activation(keep[h][:], edge["keep"][:, bass.ds(at, B)], ACT.Copy)
                nc.scalar.activation(at_dst[h][:], edge["at_dst"][:, bass.ds(at, B)], ACT.Copy)
                nc.scalar.copy(index[h][:], edge["src"][:, bass.ds(at, B)]).then_inc(staged[h], 1)

            def activate(h, i):
                act.wait_ge(projected, 2 * i + h + 1)
                nc.scalar.activation(edge_score[h][:], p_score[h][:, 0:B], ACT.Copy).then_inc(activated, 1)
                act.wait_ge(stepped, INIT + per * (2 * i + h) + 10)
                nc.scalar.activation(factor[h][:], exps[h][:], ACT.Exp).then_inc(activated, 1)

            stage(0, 0)
            with act.Fori(0, IT) as i:
                act.wait_ge(stepped, INIT + per * (2 * i))
                stage(1, (2 * i + 1) * B)
                activate(0, i)
                act.wait_ge(stepped, INIT + per * (2 * i + 1))
                stage(0, (2 * i + 2) * B)
                activate(1, i)

        @block.tensor
        def _(pe):
            with pe.Fori(0, IT) as i:
                for h in range(2):
                    pe.wait_ge(loaded[h], 16 * (i + 1))
                    pe.wait_ge(stepped, per * (2 * i + h))
                    for k in range(B):
                        edges = attr[h][:, k * P:(k + 1) * P]
                        nc.tensor.matmul(p_edge[h][:, k, :], edges, w_edge, start=True, stop=True)
                        ins = nc.tensor.matmul(p_score[h][:, k:k + 1], edges, w_edge_att, start=True, stop=True)
                    ins.then_inc(projected, 1)

        @block.vector
        def _(dve):
            nc.vector.memset(run[1][:, B - 1, :], 0.0).then_inc(stepped, 1)
            nc.vector.memset(top[1][:, B:B + 1], -BIG).then_inc(stepped, INIT - 1)
            with dve.Fori(0, IT) as i:
                for h in range(2):
                    n = [0]

                    def step(ins):
                        ins.then_inc(stepped, 1)
                        n[0] += 1

                    def after(back=0):
                        dve.wait_ge(stepped, INIT + per * (2 * i + h) + n[0] - back)

                    dve.wait_ge(staged[h], i + 1)
                    step(nc.vector.tensor_scalar(pen[h][:], keep[h][:], BIG, -BIG, ALU.mult, ALU.add))
                    after()
                    step(nc.vector.tensor_copy(top[h][:, 0:1], top[1 - h][:, B:B + 1]))
                    dve.wait_ge(gathered[h], 16 * B * (i + 1))
                    dve.wait_ge(activated, 2 * (2 * i + h) + 1)
                    step(nc.vector.tensor_tensor(score[h][:], rows[h][:, :, C], at_dst[h][:], ALU.add))
                    after()
                    step(nc.vector.tensor_tensor(score[h][:], score[h][:], edge_score[h][:], ALU.add))
                    after()
                    step(nc.vector.scalar_tensor_tensor(score[h][:], score[h][:], 0.2, score[h][:], ALU.mult, ALU.max))
                    after()
                    step(nc.vector.tensor_scalar(bounded[h][:], score[h][:], -1.0e9, None, ALU.max))
                    after()
                    step(nc.vector.tensor_tensor_scan(top[h][:, 1:1 + B], pen[h][:], bounded[h][:], top[h][:, 0:1], ALU.add, ALU.max))
                    after()
                    step(nc.vector.tensor_tensor(exps[h][:, 0:B], score[h][:], top[h][:, 1:1 + B], ALU.subtract))
                    step(nc.vector.tensor_tensor(exps[h][:, B:2 * B], top[h][:, 0:B], top[h][:, 1:1 + B], ALU.subtract))
                    after()
                    step(nc.vector.scalar_tensor_tensor(exps[h][:, B:2 * B], exps[h][:, B:2 * B], 0.0, pen[h][:], ALU.min, ALU.add))
                    step(nc.vector.tensor_tensor(msg[h][:, :, 0:C], rows[h][:, :, 0:C], p_edge[h][:], ALU.add))
                    dve.wait_ge(activated, 2 * (2 * i + h) + 2)
                    after()
                    step(nc.vector.tensor_tensor(msg[h][:, :, 0:C], msg[h][:, :, 0:C], spread(factor[h][:, 0:B], C), ALU.mult))
                    step(nc.vector.tensor_copy(msg[h][:, :, C], factor[h][:, 0:B]))
                    dve.wait_ge(stored[h], 16 * i + 16 * (h == 0))
                    for k in range(B):
                        before = run[h][:, k - 1, 0:S] if k else run[1 - h][:, B - 1, 0:S]
                        after()
                        step(nc.vector.scalar_tensor_tensor(run[h][:, k, 0:S], before, factor[h][:, B + k:B + k + 1], msg[h][:, k, :], ALU.mult, ALU.add))
                    step(nc.vector.tensor_copy(run[h][:, :, S], top[h][:, 1:1 + B]))
                    assert n[0] == per, n
            dve.wait_ge(stepped, INIT + per * 2 * IT)
            nc.vector.tensor_copy(final[:], run[1][:, B - 1, :]).then_inc(stepped, 1)


def complete_softmax(nc, sig, link, final, fix_at, running, ends, agg):
    S, W = C + 1, C + 2
    with ExitStack() as ctx:
        def sb(name, shape):
            return ctx.enter_context(nc.sbuf_tensor(name, shape, F32))

        fixed, diag, tops, weight_t, weight = sb("m_fixed", [P, W]), sb("m_diag", [P, P]), sb("m_tops", [P, P]), sb("m_weight_t", [P, P]), sb("m_weight", [P, P])
        top, neg, scale = sb("m_top", [P, 1]), sb("m_neg", [P, 1]), sb("m_scale", [P, 1])
        ps = ctx.enter_context(nc.psum_tensor("m_ps", [P, 512], F32))
        pt = ctx.enter_context(nc.psum_tensor("m_pt", [P, 512], F32))
        block = ctx.enter_context(nc.Block())
        fetched, pe_s, act_s, dve_s = sig["fetched"], sig["pe_step"], sig["act_step"], sig["dve_step"]

        @block.gpsimd
        def _(pool):
            pool.indirect_dma_start(out=fixed[:], out_offset=None, in_=running, in_offset=offsets(fix_at[:])).then_inc(fetched.sem, 16)
            pool.wait_ge(dve_s.sem, dve_s.base + 8)
            pool.indirect_dma_start(out=running, out_offset=offsets(fix_at[:]), in_=fixed[:], in_offset=None).then_inc(fetched.sem, 16)
            pool.wait_ge(fetched.sem, fetched.base + 32)
            for j in range(J):
                pool.indirect_dma_start(out=agg[:, j, :], out_offset=None, in_=running, in_offset=offsets(ends[:, j:j + 1])).then_inc(fetched.sem, 16)
            pool.wait_ge(fetched.sem, fetched.base + 32 + 16 * J)

        @block.tensor
        def _(pe):
            nc.tensor.transpose(pt[:, 0:P], link[:], sig["ident"][:]).then_inc(pe_s.sem, 1)
            pe.wait_ge(dve_s.sem, dve_s.base + 1)
            nc.tensor.matmul(ps[:, 0:P], sig["ones"][:], diag[:], start=True, stop=True).then_inc(pe_s.sem, 1)
            pe.wait_ge(act_s.sem, act_s.base + 1)
            nc.tensor.transpose(pt[:, P:2 * P], weight_t[:], sig["ident"][:]).then_inc(pe_s.sem, 1)
            pe.wait_ge(dve_s.sem, dve_s.base + 7)
            nc.tensor.matmul(ps[:, P:P + S], weight[:], final[:, 0:S], start=True, stop=True).then_inc(pe_s.sem, 1)

        @block.scalar
        def _(act):
            act.wait_ge(dve_s.sem, dve_s.base + 6)
            nc.scalar.activation(weight_t[:], tops[:], ACT.Exp, bias=neg[:]).then_inc(act_s.sem, 1)
            nc.scalar.activation(scale[:], fixed[:, S:W], ACT.Exp, bias=neg[:]).then_inc(act_s.sem, 1)

        @block.vector
        def _(dve):
            step = Chain(dve, dve_s.sem, dve_s.base)
            step(nc.vector.tensor_scalar(diag[:], sig["ident"][:], final[:, S:W], None, ALU.mult))
            dve.wait_ge(pe_s.sem, pe_s.base + 2)
            step(nc.vector.tensor_scalar(tops[:], pt[:, 0:P], BIG, -BIG, ALU.mult, ALU.add))
            step(nc.vector.tensor_tensor(tops[:], tops[:], ps[:, 0:P], ALU.add))
            step(nc.vector.tensor_reduce(top[:], tops[:], AX.X, ALU.max))
            dve.wait_ge(fetched.sem, fetched.base + 16)
            step(nc.vector.tensor_tensor(top[:], top[:], fixed[:, S:W], ALU.max))
            step(nc.vector.tensor_scalar(neg[:], top[:], -1.0, None, ALU.mult))
            dve.wait_ge(pe_s.sem, pe_s.base + 3)
            step(nc.vector.tensor_copy(weight[:], pt[:, P:2 * P]))
            dve.wait_ge(pe_s.sem, pe_s.base + 4)
            dve.wait_ge(act_s.sem, act_s.base + 2)
            step(nc.vector.scalar_tensor_tensor(fixed[:, 0:S], fixed[:, 0:S], scale[:], ps[:, P:P + S], ALU.mult, ALU.add))

        fetched.base += 32 + 16 * J
        pe_s.base += 4
        act_s.base += 2
        dve_s.base += 8


def on_vector(nc, sig, body):
    with nc.Block() as block:
        @block.vector
        def _(dve):
            step = Chain(dve, sig["dve_step"].sem, sig["dve_step"].base)
            body(step)
            sig["dve_step"].base = step.n


def moves(nc, sig, copies):
    with nc.Block() as block:
        moved = sig["moved"]

        @block.sync
        def _(sp):
            for to, of in copies:
                sp.dma_start(to, of).then_inc(moved.sem, 16)
            sp.wait_ge(moved.sem, moved.base + 16 * len(copies))

        moved.base += 16 * len(copies)


def gnn(nc, out, x, src, dst, u, ew, labels, attrs, spline1, root1, bias01, spline2, root2, bias02,
        w_att, bias1, trans, trans_t, att, edge_att, agg_weights, gw1, gb1, gw2, gb2, gw3, gb3, lw, lb,
        wn, we, we_t, att_src, att_dst, att_edge, stop=None):
    V = nc.vector
    with ExitStack() as ctx:
        def dram(name, shape):
            return nc.dram_tensor(name, shape, F32, kind="Internal").ap()

        def sb(name, shape, dt=F32, scope=ctx):
            return scope.enter_context(nc.sbuf_tensor(name, shape, dt))

        sig = {n: Signal(ctx.enter_context(nc.semaphore(n))) for n in
               ("copied", "turned", "turned_sb", "product", "saved", "fetched", "pe_step", "act_step", "dve_step", "pool_step", "moved", "rounds")}

        spline_table = dram("spline_table", [NP, 2 * C])
        att_table = dram("att_table", [NP, 2 * C + 1])
        gcn_table = [dram(f"gcn_table{k}", [NP, c]) for k, c in enumerate((16, 16, 32))]
        soft_table = dram("soft_table", [NP, C + 2])
        range_table = dram("range_table", [NP, 1])
        running = {w: dram(f"running{w}", [EP + 1, w]) for w in (C + 1, C, 4 * C, 16, 32, C + 2)}
        begun_x, begun_s, sent = dram("begun_x", [EP, C]), dram("begun_s", [EP, 1]), dram("sent", [EP, 1 + 2 * C])

        def nodes(table):
            return table.rearrange("(p j) c -> p j c", p=P)

        def steps(rows):
            return rows.rearrange("(p t) c -> p t c", p=P)

        for name in ("ident", "ones", "upper", "shift1", "shift2", "iota"):
            sig[name] = sb(name, [P, P])
        sig["ident_b"], sig["not_earlier"] = sb("ident_b", [P, P], BF16), sb("not_earlier", [P, P], BF16)
        chunk_row = sb("chunk_row", [P, 1])
        zeros = sb("zeros", [P, max(B, J - REST) * C])
        src_i = sb("src_i", [P, T + B], I32)
        keep = sb("keep", [P, T + B])
        ew_s = sb("ew_s", [P, T + B])
        rank = sb("rank", [P, T + B])
        first_dst, first_dst_f, last_dst_f, fix_dst = sb("first_dst", [P, 1], I32), sb("first_dst_f", [P, 1]), sb("last_dst_f", [P, 1]), sb("fix_dst", [P, 1], I32)
        link, step_pen, use_pen = sb("link", [P, P]), sb("step_pen", [P, P]), sb("use_pen", [P, P])
        xs = sb("xs", [P, J, C])
        y = sb("y", [P, J, C])
        final = sb("final", [P, 4 * C])
        cnt_dst, cnt_src, begin_dst, begin_src = (sb(n, [P, J]) for n in ("cnt_dst", "cnt_src", "begin_dst", "begin_src"))
        end_dst, first_at, end_src = (sb(n, [P, J], I32) for n in ("end_dst", "first_at", "end_src"))
        r_dst, r_src, ew_sum, dinv = (sb(n, [P, J]) for n in ("r_dst", "r_src", "ew_sum", "dinv"))

        l0 = ctx.enter_context(ExitStack())
        u_s = sb("u_s", [P, T + B], F32, l0)
        dst_lo, dst_hi, src_lo, src_hi = (sb(n, [P, T + B], BF16, l0) for n in ("dst_lo", "dst_hi", "src_lo", "src_hi"))
        w0 = [sb(f"w0_{k}", [C, 3 * C], F32, l0) for k in range(2)]
        b0 = [sb(f"b0_{k}", [P, C], F32, l0) for k in range(2)]

        with ExitStack() as tmp:
            dst_i, prev_i = sb("dst_i", [P, T], I32, tmp), sb("prev_i", [P, T], I32, tmp)
            dst_f, prev_f = sb("dst_f", [P, T], F32, tmp), sb("prev_f", [P, T], F32, tmp)
            many = sb("many", [P, 1], F32, tmp)
            blank_node = zeros[0:1, 0:(J - REST) * C]
            with nc.Block() as block:
                pool_s, moved, dve_s = sig["pool_step"], sig["moved"], sig["dve_step"]
                dst_flat = dst.rearrange("p t -> (p t)")

                @block.sync
                def _(sp):
                    sp.wait_ge(dve_s.sem, 1)
                    n = 0
                    for to, of in (
                        (src_i[:, 0:T], src), (dst_i[:], dst),
                        (prev_i[1:P, :], dst_flat[T - 1:EP - 1].rearrange("(p t) -> p t", t=T)), (prev_i[0:1, 1:T], dst[0:1, 0:T - 1]),
                        (ew_s[:, 0:T], ew), (u_s[:, 0:T], u),
                        (xs[0:LAST, :, :], x[0:LAST * J, :].rearrange("(p j) c -> p j c", j=J)),
                        (xs[LAST:LAST + 1, 0:REST, :], x[LAST * J:N, :].unsqueeze(0)),
                        (xs[LAST:LAST + 1, REST:J, :], blank_node.rearrange("p (j c) -> p j c", c=C)),
                        *((w0[k][:, n0 * C:(n0 + 1) * C], w) for k, ws in enumerate(((spline1[0], spline1[1], root1), (spline2[0], spline2[1], root2)))
                          for n0, w in enumerate(ws)),
                        *((b0[k][:], b.broadcast_to([P, C])) for k, b in enumerate((bias01, bias02))),
                    ):
                        sp.dma_start(to, of).then_inc(moved.sem, 16)
                        n += 1
                    sp.wait_ge(moved.sem, 16 * n)
                    moved.base += 16 * n

                @block.gpsimd
                def _(pool):
                    step = Chain(pool, pool_s.sem)
                    step(pool.iota(sig["iota"][:], [[1, P]], base=0, channel_multiplier=0, allow_small_or_imprecise_dtypes=True))
                    step(pool.iota(chunk_row[:], [[0, 1]], base=-1, channel_multiplier=T, allow_small_or_imprecise_dtypes=True))
                    step(pool.memset(sig["ones"][:], 1.0))
                    for name in ("ident", "shift1", "shift2", "ident_b", "not_earlier"):
                        step(pool.memset(sig[name][:], 0.0))

                    def select(name, of, op, base, fill):
                        step(pool.affine_select(out=sig[name][:], in_=sig[of][:], compare_op=op, fill=fill, base=base, pattern=[[1, P]], channel_multiplier=-1))

                    select("ident", "ident", ALU.not_equal, 0, 1.0)
                    select("ident_b", "ident_b", ALU.not_equal, 0, 1.0)
                    select("shift1", "shift1", ALU.not_equal, -1, 1.0)
                    select("shift2", "shift2", ALU.not_equal, -2, 1.0)
                    select("upper", "ones", ALU.is_gt, 0, 0.0)
                    select("not_earlier", "not_earlier", ALU.is_gt, 0, -1.0)

                @block.vector
                def _(dve):
                    step = Chain(dve, dve_s.sem)
                    step(V.memset(zeros[:], 0.0))
                    step(V.memset(prev_i[0:1, 0:1], -1))
                    step(V.memset(cnt_src[:], 0.0))
                    for t in (src_i, keep, ew_s, rank, u_s, dst_lo, dst_hi, src_lo, src_hi):
                        step(V.memset(t[:, T:T + B], 0))
                    dve.wait_ge(moved.sem, 16 * 17)
                    step(V.tensor_copy(dst_f[:], dst_i[:]))
                    step(V.tensor_copy(prev_f[:], prev_i[:]))
                    step(V.tensor_tensor(keep[:, 0:T], dst_f[:], prev_f[:], ALU.is_equal))
                    step(V.tensor_copy(first_dst[:], dst_i[:, 0:1]))
                    step(V.tensor_copy(first_dst_f[:], dst_f[:, 0:1]))
                    step(V.tensor_copy(last_dst_f[:], dst_f[:, T - 1:T]))
                    step(V.tensor_scalar(prev_f[:], dst_f[:], first_dst_f[:], None, ALU.is_equal))
                    step(V.tensor_reduce(many[:], prev_f[:], AX.X, ALU.add))
                    dve.wait_ge(pool_s.sem, 2)
                    step(V.tensor_tensor(fix_dst[:], many[:], chunk_row[:], ALU.add))

                    def split(key, lo, lo_b, hi):
                        step(V.tensor_scalar(lo, key, -float(J // 2), 1.0 / J, ALU.add, ALU.mult))
                        step(V.tensor_scalar(lo, lo, ROUND, None, ALU.add))
                        step(V.tensor_scalar(lo, lo, -ROUND, None, ALU.add))
                        step(V.scalar_tensor_tensor(hi, lo, -float(J), key, ALU.mult, ALU.add))
                        step(V.tensor_copy(lo_b, lo))

                    split(dst_f[:], prev_f[:], dst_lo[:, 0:T], dst_hi[:, 0:T])
                    step(V.tensor_copy(prev_f[:], src_i[:, 0:T]))
                    split(prev_f[:], dst_f[:], src_lo[:, 0:T], src_hi[:, 0:T])
                    for k in range(2):
                        step(V.tensor_tensor(w0[k][:, C:2 * C], w0[k][:, C:2 * C], w0[k][:, 0:C], ALU.subtract))
                    dve_s.base = step.n

        carry_masks(nc, sig, first_dst_f[:], last_dst_f[:], link, step_pen, use_pen)
        carries = (link, step_pen, use_pen)

        with ExitStack() as tmp:
            d = sb("d", [P, J, 3 * C], F32, tmp)
            h = sb("h0", [P, J, C], F32, tmp)
            for k in range(2):
                width = C + 1 if k == 0 else C
                dense(nc, sig, [xs if k == 0 else h], [w0[k][:]], d, 3 * C)
                moves(nc, sig, [(nodes(spline_table), d[:, :, 0:2 * C])])
                edge = {"src": src_i, "keep": keep, "weight": u_s, "src_lo": src_lo, "src_hi": src_hi, "rank": rank, "seen": cnt_src, "ranked": k * RANKED}
                if k == 0:
                    edge |= {"extra": ew_s, "dst_lo": dst_lo, "dst_hi": dst_hi, "count": cnt_dst}
                weighted_pass(nc, sig, "spline", spline_table, width, 2 * C, edge, running[width], final, zeros,
                              cleared=() if k == 0 else (steps(begun_x), steps(begun_s)))
                if k == 0:
                    node_ranges(nc, sig, cnt_dst, begin_dst, end_dst, first_at)
                else:
                    node_ranges(nc, sig, cnt_src, begin_src, end_src, None)
                agg_scope = tmp.enter_context(ExitStack())
                agg_k = sb(f"agg0_{k}", [P, J, width], F32, agg_scope)
                complete_and_fetch(nc, sig, carries, final, width, width, fix_dst, running[width], end_dst, agg_k)

                def mean_root_bias(step):
                    if k == 0:
                        step(V.tensor_scalar(r_dst[:], cnt_dst[:], 1.0, None, ALU.max))
                        step(V.reciprocal(r_dst[:], r_dst[:]))
                        step(V.tensor_copy(ew_sum[:], agg_k[:, :, C]))
                    to = h if k == 0 else y
                    step(V.tensor_tensor(to[:], agg_k[:, :, 0:C], spread(r_dst[:], C), ALU.mult))
                    step(V.tensor_tensor(to[:], to[:], d[:, :, 2 * C:3 * C], ALU.add))
                    step(V.tensor_tensor(to[:], to[:], repeat(b0[k][:], J), ALU.add))

                on_vector(nc, sig, mean_root_bias)
                agg_scope.close()
            layer_norm(nc, sig, xs, y, xs)
        l0.close()

        def finish():
            moves(nc, sig, [(out[0:LAST * J, :].rearrange("(p j) c -> p j c", j=J), xs[0:LAST, :, :]),
                            (out[LAST * J:N, :].unsqueeze(0), xs[LAST:LAST + 1, 0:REST, :])])

        if stop == 0:
            return finish()

        with ExitStack() as tmp:
            w_top, w_bot, b1 = sb("w_top", [P, C], F32, tmp), sb("w_bot", [P, C], F32, tmp), sb("b1", [P, C], F32, tmp)
            tw, twt, ea, tw_att = sb("tw", [LABELS, C], F32, tmp), sb("twt", [C, LABELS], F32, tmp), sb("ea", [C, 1], F32, tmp), sb("tw_att", [LABELS, 1], F32, tmp)
            att_b, mix = sb("att_b", [P, C], F32, tmp), sb("mix", [P, 3], F32, tmp)
            mix_sum = sb("mix_sum", [P, 1], F32, tmp)
            share = sb("share", [P, J], F32, tmp)
            comb_dst = sb("comb_dst", [P, J, 2 * C], F32, tmp)
            first_rows = sb("first_rows", [P, 2 * C + 1], F32, tmp)
            moves(nc, sig, [(w_top[:], w_att[0:2 * C, :]), (w_bot[0:C, :], w_att[3 * C:4 * C, :]), (w_bot[C:2 * C, :], w_att[2 * C:3 * C, :]),
                            (b1[:], bias1.broadcast_to([P, C])), (tw[:], trans), (twt[:], trans_t), (ea[:], edge_att),
                            (att_b[:], att.broadcast_to([P, C])), (mix[:], agg_weights.broadcast_to([P, 3]))])
            with ExitStack() as rows:
                t1 = sb("t1", [P, J, 2 * C + 1], F32, rows)

                def table_rows(step):
                    step(V.tensor_tensor(t1[:, :, 0:C], xs[:], repeat(att_b[:], J), ALU.mult))
                    step(V.tensor_copy(t1[:, :, C:2 * C], xs[:]))
                    step(V.tensor_copy(t1[:, :, 2 * C], begin_src[:]))
                    step(V.tensor_reduce(mix_sum[:], mix[:], AX.X, ALU.max))
                    step(V.tensor_scalar(mix[:], mix[:], mix_sum[:], None, ALU.subtract))
                    step(V.tensor_copy(begin_dst[:], end_src[:]))
                    step(V.tensor_scalar(r_src[:], cnt_src[:], 1.0, None, ALU.max))
                    step(V.reciprocal(r_src[:], r_src[:]))

                on_vector(nc, sig, table_rows)
                with ExitStack() as c2:
                    ps = c2.enter_context(nc.psum_tensor("p_label_att", [P, 512], F32))
                    block = c2.enter_context(nc.Block())
                    act_s, pe_s, dve_s = sig["act_step"], sig["pe_step"], sig["dve_step"]

                    @block.scalar
                    def _(act):
                        nc.scalar.activation(mix[:], mix[:], ACT.Exp).then_inc(act_s.sem, 1)

                    @block.tensor
                    def _(pe):
                        nc.tensor.matmul(ps[0:LABELS, 0:1], twt[:], ea[:], start=True, stop=True).then_inc(pe_s.sem, 1)

                    @block.vector
                    def _(dve):
                        step = Chain(dve, dve_s.sem, dve_s.base)
                        dve.wait_ge(pe_s.sem, pe_s.base + 1)
                        step(V.tensor_copy(tw_att[:], ps[0:LABELS, 0:1]))
                        dve.wait_ge(act_s.sem, act_s.base + 1)
                        step(V.tensor_reduce(mix_sum[:], mix[:], AX.X, ALU.add))
                        step(V.reciprocal(mix_sum[:], mix_sum[:]))
                        step(V.tensor_scalar(mix[:], mix[:], mix_sum[:], None, ALU.mult))
                        dve_s.base = step.n

                    act_s.base += 1
                    pe_s.base += 1
                moves(nc, sig, [(nodes(att_table), t1[:]), (nodes(range_table), begin_dst[:].unsqueeze(2))])
            spread_to_edges(nc, sig, xs, first_at, begun_x, att_table, first_dst[:], first_rows)
            attention_pass(nc, sig, att_table, {"src": src_i, "keep": keep, "rank": rank}, labels, begun_x, first_rows, tw[:], tw_att[:],
                           running[4 * C], final, sent, zeros)

            def combine(agg, cnt_r, to):
                def body(step):
                    step(V.tensor_scalar(share[:], cnt_r[:], mix[:, 0:1], mix[:, 2:3], ALU.mult, ALU.add))
                    step(V.tensor_tensor(to[:], agg[:, :, 0:2 * C], spread(share[:], 2 * C), ALU.mult))
                    step(V.scalar_tensor_tensor(to[:], agg[:, :, 2 * C:4 * C], mix[:, 1:2], to[:], ALU.mult, ALU.add))

                on_vector(nc, sig, body)

            with ExitStack() as rows:
                agg = sb("agg_dst", [P, J, 4 * C], F32, rows)
                complete_and_fetch(nc, sig, carries, final, 2 * C, 4 * C, fix_dst, running[4 * C], end_dst, agg)
                combine(agg, r_dst, comb_dst)
            ends = sb("ends", [P, 4], F32, tmp)
            source_pass(nc, sig, sent, running[4 * C], final, ends, zeros)
            first_src, fix_src, end_first = sb("first_src", [P, 1], I32, tmp), sb("fix_src", [P, 1], I32, tmp), sb("end_first", [P, 1], F32, tmp)
            link_s, step_pen_s, use_pen_s = sb("link_s", [P, P], F32, tmp), sb("step_pen_s", [P, P], F32, tmp), sb("use_pen_s", [P, P], F32, tmp)
            carry_masks(nc, sig, ends[:, 0:1], ends[:, 2:3], link_s, step_pen_s, use_pen_s)
            chunk_end = sb("chunk_end", [P, 1], F32, tmp)
            with nc.Block() as block:
                fetched, dve_s = sig["fetched"], sig["dve_step"]

                @block.gpsimd
                def _(pool):
                    pool.wait_ge(dve_s.sem, dve_s.base + 1)
                    pool.indirect_dma_start(out=end_first[:], out_offset=None, in_=range_table, in_offset=offsets(first_src[:])).then_inc(fetched.sem, 16)

                @block.vector
                def _(dve):
                    step = Chain(dve, dve_s.sem, dve_s.base)
                    step(V.tensor_copy(first_src[:], ends[:, 0:1]))
                    step(V.tensor_scalar(chunk_end[:], chunk_row[:], float(T), None, ALU.add))
                    dve.wait_ge(fetched.sem, fetched.base + 16)
                    step(V.tensor_tensor(fix_src[:], end_first[:], chunk_end[:], ALU.min))
                    dve_s.base = step.n

                fetched.base += 16
            comb_src = sb("comb_src", [P, J, 2 * C], F32, tmp)
            with ExitStack() as rows:
                agg = sb("agg_src", [P, J, 4 * C], F32, rows)
                complete_and_fetch(nc, sig, (link_s, step_pen_s, use_pen_s), final, 2 * C, 4 * C, fix_src, running[4 * C], end_src, agg)
                combine(agg, r_src, comb_src)
            dense(nc, sig, [comb_src, comb_dst], [w_top[:], w_bot[:]], y, C)
            on_vector(nc, sig, lambda step: step(V.tensor_tensor(y[:], y[:], repeat(b1[:], J), ALU.add)))
            layer_norm(nc, sig, xs, y, xs)
        if stop == 1:
            return finish()

        with ExitStack() as tmp:
            widths = (16, 16, 32)
            w1, w2, w3 = sb("gw1s", [C, 16], F32, tmp), sb("gw2s", [16, 32], F32, tmp), sb("gw3s", [32, C], F32, tmp)
            gb = [sb(f"gb{k}", [P, c], F32, tmp) for k, c in enumerate((16, 32, C))]
            lws = [sb(f"lws{k}", [C, C], F32, tmp) for k in range(2)]
            lbs = sb("lbs", [P, C], F32, tmp)
            t = [sb(f"gt{k}", [P, J, c], F32, tmp) for k, c in enumerate(widths)]
            agg = [sb(f"gagg{k}", [P, J, c], F32, tmp) for k, c in enumerate(widths)]
            x2, x3, x4 = sb("x2", [P, J, 16], F32, tmp), sb("x3", [P, J, 32], F32, tmp), sb("x4", [P, J, C], F32, tmp)
            moves(nc, sig, [(w1[:], gw1), (w2[:], gw2), (w3[:], gw3), (gb[0][:], gb1.broadcast_to([P, 16])), (gb[1][:], gb2.broadcast_to([P, 32])),
                            (gb[2][:], gb3.broadcast_to([P, C])), (lws[0][:], lw[0:C, :]), (lws[1][:], lw[C:2 * C, :]), (lbs[:], lb.broadcast_to([P, C]))])
            some = sb("some", [P, J], F32, tmp)

            def degrees(step):
                step(V.tensor_scalar(ew_sum[:], ew_sum[:], 1.0, None, ALU.add))
                step(V.tensor_scalar(some[:], ew_sum[:], 0.0, None, ALU.is_gt))
                step(V.tensor_scalar(ew_sum[:], ew_sum[:], 1.0e-30, None, ALU.max))

            on_vector(nc, sig, degrees)
            with nc.Block() as block:
                act_s, dve_s = sig["act_step"], sig["dve_step"]

                @block.scalar
                def _(act):
                    nc.scalar.activation(dinv[:], ew_sum[:], ACT.Sqrt).then_inc(act_s.sem, 1)

                @block.vector
                def _(dve):
                    step = Chain(dve, dve_s.sem, dve_s.base)
                    dve.wait_ge(act_s.sem, act_s.base + 1)
                    step(V.reciprocal(dinv[:], dinv[:]))
                    step(V.tensor_tensor(dinv[:], dinv[:], some[:], ALU.mult))
                    dve_s.base = step.n

                act_s.base += 1

            def convolve(k):
                c = widths[k]
                moves(nc, sig, [(nodes(gcn_table[k]), t[k][:])])
                weighted_pass(nc, sig, "gcn", gcn_table[k], c, c, {"src": src_i, "keep": keep, "weight": ew_s}, running[c], final, zeros)
                complete_and_fetch(nc, sig, carries, final, c, c, fix_dst, running[c], end_dst, agg[k])

                def body(step):
                    step(V.tensor_tensor(agg[k][:], agg[k][:], t[k][:], ALU.add))
                    step(V.tensor_tensor(agg[k][:], agg[k][:], spread(dinv[:], c), ALU.mult))

                on_vector(nc, sig, body)

            def bias_relu(step, h, b):
                step(V.tensor_tensor(h[:], h[:], repeat(b[:], J), ALU.add))
                step(V.tensor_scalar(flat(h[:]), flat(h[:]), 0.0, None, ALU.max))

            def scaled(step, to, h, c):
                step(V.tensor_tensor(to[:], h[:], spread(dinv[:], c), ALU.mult))

            dense(nc, sig, [xs], [w1[:]], x2, 16)
            on_vector(nc, sig, lambda step: scaled(step, t[0], x2, 16))
            convolve(0)
            on_vector(nc, sig, lambda step: (bias_relu(step, agg[0], gb[0]), scaled(step, t[1], agg[0], 16)))
            convolve(1)
            dense(nc, sig, [agg[1]], [w2[:]], x3, 32)
            on_vector(nc, sig, lambda step: (bias_relu(step, x3, gb[1]), scaled(step, t[2], x3, 32)))
            convolve(2)
            dense(nc, sig, [agg[2]], [w3[:]], x4, C)
            on_vector(nc, sig, lambda step: bias_relu(step, x4, gb[2]))
            dense(nc, sig, [xs, x4], [lws[0][:], lws[1][:]], y, C)
            on_vector(nc, sig, lambda step: step(V.tensor_tensor(y[:], y[:], repeat(lbs[:], J), ALU.add)))
            layer_norm(nc, sig, xs, y, xs)
        if stop == 2:
            return finish()

        with ExitStack() as tmp:
            wns, wes, wet, ae, w_edge_att = sb("wns", [C, C], F32, tmp), sb("wes", [EDIM, C], F32, tmp), sb("wet", [C, EDIM], F32, tmp), sb("ae", [C, 1], F32, tmp), sb("w_edge_att", [EDIM, 1], F32, tmp)
            a_src, a_dst = sb("a_src", [P, C], F32, tmp), sb("a_dst", [P, C], F32, tmp)
            t3, prod, s_dst = sb("t3", [P, J, C + 2], F32, tmp), sb("prod", [P, J, C], F32, tmp), sb("s_dst", [P, J, 1], F32, tmp)
            first_rows = sb("first_rows3", [P, C + 2], F32, tmp)
            at_dst, begun = sb("at_dst", [P, T + B], F32, tmp), sb("begun3", [P, T], F32, tmp)
            moves(nc, sig, [(wns[:], wn), (wes[:], we), (wet[:], we_t), (ae[:], att_edge), (a_src[:], att_src.broadcast_to([P, C])), (a_dst[:], att_dst.broadcast_to([P, C]))])
            dense(nc, sig, [xs], [wns[:]], t3, C)

            def table_rows(step):
                for col, a in ((C, a_src), (C + 1, a_dst)):
                    step(V.tensor_tensor(prod[:], t3[:, :, 0:C], repeat(a[:], J), ALU.mult))
                    step(V.tensor_reduce(t3[:, :, col], prod[:], AX.X, ALU.add))
                step(V.tensor_copy(s_dst[:, :, 0], t3[:, :, C + 1]))

            on_vector(nc, sig, table_rows)
            with ExitStack() as c2:
                ps = c2.enter_context(nc.psum_tensor("p_edge_att", [P, 512], F32))
                block = c2.enter_context(nc.Block())
                pe_s, dve_s = sig["pe_step"], sig["dve_step"]

                @block.tensor
                def _(pe):
                    nc.tensor.matmul(ps[0:EDIM, 0:1], wet[:], ae[:], start=True, stop=True).then_inc(pe_s.sem, 1)

                @block.vector
                def _(dve):
                    step = Chain(dve, dve_s.sem, dve_s.base)
                    dve.wait_ge(pe_s.sem, pe_s.base + 1)
                    step(V.tensor_copy(w_edge_att[:], ps[0:EDIM, 0:1]))
                    dve_s.base = step.n

                pe_s.base += 1
            moves(nc, sig, [(nodes(soft_table), t3[:])])
            spread_to_edges(nc, sig, s_dst, first_at, begun_s, soft_table, first_dst[:], first_rows)
            moves(nc, sig, [(begun[:], begun_s.rearrange("(p t) c -> p (t c)", p=P))])

            def held(step):
                step(V.memset(at_dst[:, T:T + B], 0.0))
                step(V.tensor_tensor_scan(at_dst[:, 0:T], keep[:, 0:T], begun[:], first_rows[:, C + 1:C + 2], ALU.mult, ALU.add))

            on_vector(nc, sig, held)
            softmax_pass(nc, sig, soft_table, {"src": src_i, "keep": keep, "at_dst": at_dst}, attrs, wes[:], w_edge_att[:], running[C + 2], final[:, 0:C + 2], zeros)
            agg = sb("agg3", [P, J, C + 2], F32, tmp)
            complete_softmax(nc, sig, link, final, fix_dst, running[C + 2], end_dst, agg)

            def normalised(step):
                step(V.tensor_scalar(r_src[:], agg[:, :, C], 1.0e-8, None, ALU.add))
                step(V.reciprocal(r_src[:], r_src[:]))
                step(V.tensor_tensor(y[:], agg[:, :, 0:C], spread(r_src[:], C), ALU.mult))
                step(V.tensor_tensor(flat(y[:]), flat(y[:]), flat(xs[:]), ALU.add))

            on_vector(nc, sig, normalised)
            layer_norm(nc, sig, xs, y, xs)
        finish()


def kernel(**inputs):
    import concourse.bacc as bacc
    from concourse.bass_utils import run_bass_kernel_spmd

    def chunks(name, fill):
        a = np.asarray(inputs[name]).reshape(E)
        return np.concatenate([a, np.full(EP - E, fill, a.dtype)]).reshape(P, T)

    def steps(name):
        a = np.asarray(inputs[name])
        a = np.concatenate([a, np.zeros((EP - E, a.shape[1]), a.dtype)])
        return np.ascontiguousarray(a.reshape(P, T, -1).transpose(2, 1, 0)).reshape(a.shape[1], T * P)

    def plain(name):
        return np.ascontiguousarray(inputs[name])

    def row(name):
        return plain(name).reshape(1, -1)

    def turned(name):
        return np.ascontiguousarray(np.asarray(inputs[name]).T)

    arrays = {
        "x": plain("x"), "src": chunks("src", NP - 1), "dst": chunks("dst", NP - 1),
        "u": chunks("edge_weight1", 0), "ew": chunks("edge_weight", 0),
        "labels": steps("edge_attr_8"), "attrs": steps("edge_attr_16"),
        "spline1": plain("L0_gnn_w1"), "root1": plain("L0_gnn_root1"), "bias01": row("L0_gnn_b1"),
        "spline2": plain("L0_gnn_w2"), "root2": plain("L0_gnn_root2"), "bias02": row("L0_gnn_b2"),
        "w_att": plain("L1_gnn_weight"), "bias1": row("L1_gnn_bias"), "trans": plain("L1_gnn_trans_weight"), "trans_t": turned("L1_gnn_trans_weight"),
        "att": row("L1_gnn_attention_weight"), "edge_att": plain("L1_gnn_edge_attention_weight"), "agg_weights": row("L1_gnn_agg_weights"),
        "gw1": plain("L2_gnn_w1"), "gb1": row("L2_gnn_b1"), "gw2": plain("L2_gnn_w2"), "gb2": row("L2_gnn_b2"),
        "gw3": plain("L2_gnn_w3"), "gb3": row("L2_gnn_b3"), "lw": plain("L2_gnn_lw"), "lb": row("L2_gnn_lb"),
        "wn": plain("L3_gnn_Wn"), "we": plain("L3_gnn_We"), "we_t": turned("L3_gnn_We"),
        "att_src": row("L3_gnn_att_src"), "att_dst": row("L3_gnn_att_dst"), "att_edge": plain("L3_gnn_att_edge").reshape(C, 1),
    }
    nc = bacc.Bacc("TRN2", target_bir_lowering=False, num_devices=1)
    args = {n: nc.dram_tensor(f"in_{n}", a.shape, mybir.dt.from_np(a.dtype), kind="ExternalInput").ap() for n, a in arrays.items()}
    out = nc.dram_tensor("out", [N, C], F32, kind="ExternalOutput").ap()
    gnn(nc, out, **args)
    r = run_bass_kernel_spmd(nc, [{f"in_{n}": a for n, a in arrays.items()}], core_ids=[0])
    return r.results[0]["out"]
```

```python
from contextlib import ExitStack

import numpy as np

import concourse.bass as bass
from concourse import mybir
from concourse.alu_op_type import AluOpType as ALU

F32 = mybir.dt.float32
BF16 = mybir.dt.bfloat16
I32 = mybir.dt.int32
ACT = mybir.ActivationFunctionType
AX = mybir.AxisListType

P = 128
N = 6250
C = 64
E = 200000
J = -(-N // P)
NP = P * J
B = 16
T = -(-E // (P * 2 * B)) * 2 * B
EP = P * T
IT = T // (2 * B)
LAST = (N - 1) // J
REST = N - LAST * J
LABELS, EDIM = 8, 16
BIG = 1.0e30
ROUND = 12582912.0
GROUP = 4
PAIR = (0, 4, 8, 7)
PAIRS = GROUP * (GROUP + 1) // 2
RANKED = B // 2
SENT = 1 + C + LABELS
RUN = C + LABELS + 2 * C
SLICE = 16
PICKS = 4


class Chain:

    def __init__(self, eng, sem, base=0):
        self.eng, self.sem, self.n = eng, sem, base

    def __call__(self, ins):
        self.n += 1
        ins.then_inc(self.sem, 1)
        self.eng.wait_ge(self.sem, self.n)


class Signal:

    def __init__(self, sem):
        self.sem, self.base = sem, 0


def flat(ap):
    return ap.rearrange("p a b -> p (a b)")


def offsets(ap):
    return bass.IndirectOffsetOnAxis(ap=ap, axis=0)


def dense(nc, sig, xs, weights, out, width, store=None, bias=None, block=None):
    G = 7
    GROUPS = J // G
    with ExitStack() as ctx:
        uid = nc.next_id()
        K = len(xs)
        k_dims = [w.shape[0] for w in weights]

        def sb(name, shape):
            return [ctx.enter_context(nc.sbuf_tensor(f"{name}{uid}_{b}", shape, F32)) for b in range(2)]

        xin = [sb(f"xin{k}_", [P, G, d]) for k, d in enumerate(k_dims)]
        xt = [sb(f"xt{k}_", [d, G, P]) for k, d in enumerate(k_dims)]
        tp = [ctx.enter_context(nc.psum_tensor(f"tp{uid}_{k}", [P, 8, P], F32)) for k in range(K)]
        slot = next(s for s in (64, 128, 256) if width <= s)
        ACCS = 2 if 2 * K + slot // 32 <= 8 and block is None else 1
        acc = [ctx.enter_context(nc.psum_tensor(f"acc{uid}_{b}", [P, 8, slot], F32)) for b in range(ACCS)]
        block = block or ctx.enter_context(nc.Block())
        copied, turned, turned_sb, product, saved, moved = (sig[n] for n in ("copied", "turned", "turned_sb", "product", "saved", "moved"))

        def each_group(eng, body):
            with eng.Fori(0, GROUPS // 2) as j:
                body(2 * j, 0)
                body(2 * j + 1, 1)
            body(GROUPS - 1, 0)

        @block.scalar
        def _(act):
            def copy(i, b):
                act.wait_ge(turned.sem, turned.base + i - 1)
                for k in range(K):
                    ins = nc.scalar.activation(xin[k][b][:], xs[k][:, bass.ds(i * G, G), :], ACT.Copy)
                ins.then_inc(copied.sem, 1)

            def save(i, b):
                if bias is not None:
                    return
                act.wait_ge(product.sem, product.base + i + 1)
                nc.scalar.activation(out[:, bass.ds(i * G, G), 0:width], acc[b % ACCS][:, 0:G, 0:width], ACT.Copy).then_inc(saved.sem, 1)

            copy(0, 0)
            copy(1, 1)
            with act.Fori(0, GROUPS // 2 - 1) as j:
                for b in range(2):
                    save(2 * j + b, b)
                    copy(2 * j + b + 2, b)
            save(GROUPS - 3, 0)
            copy(GROUPS - 1, 0)
            save(GROUPS - 2, 1)
            save(GROUPS - 1, 0)

        @block.tensor
        def _(pe):
            def turn(i, b):
                pe.wait_ge(copied.sem, copied.base + i + 1)
                pe.wait_ge(turned_sb.sem, turned_sb.base + i)
                pe.sem_inc(sig["rounds"].sem, 1)
                for k in range(K):
                    for g in range(G):
                        ins = nc.tensor.transpose(tp[k][0:k_dims[k], g, :], xin[k][b][:, g, :], sig["ident"][:])
                ins.then_inc(turned.sem, 1)

            def multiply(i, b):
                pe.wait_ge(turned_sb.sem, turned_sb.base + i + 1)
                pe.wait_ge(saved.sem, saved.base + i + 1 - ACCS)
                for g in range(G):
                    for k in range(K):
                        ins = nc.tensor.matmul(acc[b % ACCS][:, g, 0:width], xt[k][b][:, g, :], weights[k], start=(k == 0), stop=(k == K - 1))
                ins.then_inc(product.sem, 1)

            turn(0, 0)
            with pe.Fori(0, GROUPS // 2) as j:
                for b in range(2):
                    turn(2 * j + b + 1, 1 - b)
                    multiply(2 * j + b, b)
            multiply(GROUPS - 1, 0)

        @block.vector
        def _(dve):
            def copy_out(i, b):
                dve.wait_ge(turned.sem, turned.base + i + 1)
                dve.wait_ge(product.sem, product.base + i - 1)
                for k in range(K):
                    ins = nc.vector.tensor_copy(flat(xt[k][b][:]), flat(tp[k][0:k_dims[k], 0:G, :]))
                ins.then_inc(turned_sb.sem, 1)

            def add_bias(i, b):
                if bias is None:
                    return
                dve.wait_ge(product.sem, product.base + i + 1)
                nc.vector.tensor_tensor(out[:, bass.ds(i * G, G), 0:width], acc[b % ACCS][:, 0:G, 0:width], repeat(bias, G), ALU.add).then_inc(saved.sem, 1)

            copy_out(0, 0)
            with dve.Fori(0, GROUPS // 2) as j:
                for b in range(2):
                    copy_out(2 * j + b + 1, 1 - b)
                    add_bias(2 * j + b, b)
            add_bias(GROUPS - 1, 0)

        if store is not None:
            @block.sync
            def _(sp):
                def send(i, b):
                    sp.wait_ge(saved.sem, saved.base + i + 1)
                    sp.dma_start(store[:, bass.ds(i * G, G), :], out[:, bass.ds(i * G, G), 0:store.shape[2]]).then_inc(moved.sem, 16)

                each_group(sp, send)
                sp.wait_ge(moved.sem, moved.base + 16 * GROUPS)

            moved.base += 16 * GROUPS

        for s in (copied, turned, turned_sb, product, saved):
            s.base += GROUPS


def complete_and_fetch(nc, sig, carries, final, n_sum, width, fix_at, running, ends, agg, beside=None):
    link, step_pen, use_pen = carries
    n_max = width - n_sum
    with ExitStack() as ctx:
        uid = nc.next_id()
        fixed = ctx.enter_context(nc.sbuf_tensor(f"fixed{uid}", [P, width], F32))
        ps = ctx.enter_context(nc.psum_tensor(f"pcarry{uid}", [P, 512], F32))
        pt = ctx.enter_context(nc.psum_tensor(f"pcarry_t{uid}", [P, 512], F32))
        run = ctx.enter_context(nc.sbuf_tensor(f"run{uid}", [P, P + 1], F32))
        block = ctx.enter_context(nc.Block())
        fetched, pe_s, dve_s = sig["fetched"], sig["pe_step"], sig["dve_step"]

        @block.gpsimd
        def _(pool):
            pool.indirect_dma_start(out=fixed[:], out_offset=None, in_=running, in_offset=offsets(fix_at[:])).then_inc(fetched.sem, 16)
            pool.wait_ge(dve_s.sem, dve_s.base + (5 if n_max else 1))
            pool.indirect_dma_start(out=running, out_offset=offsets(fix_at[:]), in_=fixed[:], in_offset=None).then_inc(fetched.sem, 16)
            pool.wait_ge(fetched.sem, fetched.base + 32)
            for j in range(J):
                pool.indirect_dma_start(out=agg[:, j, :], out_offset=None, in_=running, in_offset=offsets(ends[:, j:j + 1])).then_inc(fetched.sem, 16)
            pool.wait_ge(fetched.sem, fetched.base + 32 + 16 * J)

        @block.tensor
        def _(pe):
            nc.tensor.matmul(ps[:, 0:n_sum], link[:], final[:, 0:n_sum], start=True, stop=True).then_inc(pe_s.sem, 1)
            if n_max:
                nc.tensor.transpose(pt[0:n_max, 0:P], final[:, n_sum:width], sig["ident"][:]).then_inc(pe_s.sem, 1)
                pe.wait_ge(dve_s.sem, dve_s.base + 4)
                nc.tensor.transpose(pt[:, P:P + n_max], run[0:n_max, 0:P], sig["ident"][0:n_max, 0:n_max]).then_inc(pe_s.sem, 1)

        @block.vector
        def _(dve):
            step = Chain(dve, dve_s.sem, dve_s.base)
            if n_max:
                dve.wait_ge(pe_s.sem, pe_s.base + 2)
                step(nc.vector.memset(run[0:n_max, 0:1], -BIG))
                step(nc.vector.tensor_tensor_scan(run[0:n_max, 1:P], step_pen[0:n_max, 1:P], pt[0:n_max, 0:P - 1], -BIG, ALU.add, ALU.max))
                step(nc.vector.tensor_tensor(run[0:n_max, 1:P], run[0:n_max, 1:P], use_pen[0:n_max, 1:P], ALU.add))
                step(nc.vector.tensor_scalar(run[0:n_max, 0:P], run[0:n_max, 0:P], -BIG, None, ALU.max))
                dve.wait_ge(pe_s.sem, pe_s.base + 3)
                dve.wait_ge(fetched.sem, fetched.base + 16)
                nc.vector.tensor_tensor(fixed[:, n_sum:width], fixed[:, n_sum:width], pt[:, P:P + n_max], ALU.max)
            dve.wait_ge(pe_s.sem, pe_s.base + 1)
            dve.wait_ge(fetched.sem, fetched.base + 16)
            step(nc.vector.tensor_tensor(fixed[:, 0:n_sum], fixed[:, 0:n_sum], ps[:, 0:n_sum], ALU.add))

        fetched.base += 32 + 16 * J
        pe_s.base += 3 if n_max else 1
        dve_s.base += 5 if n_max else 1
        if beside:
            beside(block, ctx)


def spread(ap, n):
    return ap.unsqueeze(2).broadcast_to([ap.shape[0], ap.shape[1], n])


def repeat(ap, n):
    return ap.unsqueeze(1).broadcast_to([ap.shape[0], n, ap.shape[1]])


def carry_masks(nc, sig, first, last, link, step_pen, use_pen):
    with ExitStack() as ctx:
        uid = nc.next_id()
        diag = ctx.enter_context(nc.sbuf_tensor(f"diag{uid}", [P, P], F32))
        near = ctx.enter_context(nc.sbuf_tensor(f"near{uid}", [P, 2 * P], F32))
        ps = ctx.enter_context(nc.psum_tensor(f"pmask{uid}", [P, 512], F32))
        block = ctx.enter_context(nc.Block())
        pe_s, dve_s = sig["pe_step"], sig["dve_step"]

        @block.tensor
        def _(pe):
            pe.wait_ge(dve_s.sem, dve_s.base + 1)
            nc.tensor.matmul(ps[:, 0:P], sig["ones"][:], diag[:], start=True, stop=True).then_inc(pe_s.sem, 1)
            pe.wait_ge(dve_s.sem, dve_s.base + 4)
            nc.tensor.matmul(ps[:, P:3 * P], sig["ones"][:], near[:], start=True, stop=True).then_inc(pe_s.sem, 1)

        @block.vector
        def _(dve):
            step = Chain(dve, dve_s.sem, dve_s.base)
            step(nc.vector.tensor_scalar(diag[:], sig["ident"][:], first, None, ALU.mult))
            dve.wait_ge(pe_s.sem, pe_s.base + 1)
            step(nc.vector.scalar_tensor_tensor(link[:], ps[:, 0:P], last, sig["upper"][:], ALU.is_equal, ALU.mult))
            step(nc.vector.tensor_tensor(near[:, 0:P], link[:], sig["shift2"][:], ALU.mult))
            step(nc.vector.tensor_tensor(near[:, P:2 * P], link[:], sig["shift1"][:], ALU.mult))
            dve.wait_ge(pe_s.sem, pe_s.base + 2)
            step(nc.vector.tensor_scalar(step_pen[:], ps[:, P:2 * P], BIG, -BIG, ALU.mult, ALU.add))
            step(nc.vector.tensor_scalar(use_pen[:], ps[:, 2 * P:3 * P], BIG, -BIG, ALU.mult, ALU.add))

        pe_s.base += 2
        dve_s.base += 6


def node_ranges(nc, sig, cnt, begin, end_row, begin_row):
    with ExitStack() as ctx:
        uid = nc.next_id()
        upto = ctx.enter_context(nc.sbuf_tensor(f"upto{uid}", [P, J], F32))
        has = ctx.enter_context(nc.sbuf_tensor(f"has{uid}", [P, J], F32))
        tmp = ctx.enter_context(nc.sbuf_tensor(f"rtmp{uid}", [P, J], F32))
        ps = ctx.enter_context(nc.psum_tensor(f"pbefore{uid}", [P, 512], F32))
        block = ctx.enter_context(nc.Block())
        pe_s, dve_s = sig["pe_step"], sig["dve_step"]

        @block.tensor
        def _(pe):
            pe.wait_ge(dve_s.sem, dve_s.base + 1)
            nc.tensor.matmul(ps[:, 0:1], sig["upper"][:], upto[:, J - 1:J], start=True, stop=True).then_inc(pe_s.sem, 1)

        @block.vector
        def _(dve):
            step = Chain(dve, dve_s.sem, dve_s.base)
            step(nc.vector.tensor_tensor_scan(upto[:], sig["ones"][:, 0:J], cnt[:], 0.0, ALU.mult, ALU.add))
            dve.wait_ge(pe_s.sem, pe_s.base + 1)
            step(nc.vector.tensor_scalar(upto[:], upto[:], ps[:, 0:1], None, ALU.add))
            step(nc.vector.tensor_tensor(begin[:], upto[:], cnt[:], ALU.subtract))
            step(nc.vector.tensor_scalar(has[:], cnt[:], 0.0, None, ALU.is_gt))
            for ahead, rows, offset in ((upto, end_row, -1.0), (begin, begin_row, 0.0)):
                if rows is not None:
                    step(nc.vector.scalar_tensor_tensor(tmp[:], ahead[:], offset - EP, has[:], ALU.add, ALU.mult))
                    step(nc.vector.tensor_scalar(rows[:], tmp[:], float(EP), None, ALU.add))

        pe_s.base += 1
        dve_s.base += 4 + 2 * ((end_row is not None) + (begin_row is not None))


def layer_norm(nc, sig, x, y, out):
    with ExitStack() as ctx:
        uid = nc.next_id()
        s = ctx.enter_context(nc.sbuf_tensor(f"lnsum{uid}", [P, J], F32))
        sq = ctx.enter_context(nc.sbuf_tensor(f"lnsq{uid}", [P, J, C], F32))
        std = ctx.enter_context(nc.sbuf_tensor(f"lnstd{uid}", [P, J], F32))
        block = ctx.enter_context(nc.Block())
        act_s, dve_s = sig["act_step"], sig["dve_step"]

        @block.vector
        def _(dve):
            step = Chain(dve, dve_s.sem, dve_s.base)
            step(nc.vector.tensor_tensor(flat(y[:]), flat(x[:]), flat(y[:]), ALU.add))
            step(nc.vector.tensor_reduce(s[:], y[:], AX.X, ALU.add))
            step(nc.vector.tensor_scalar(s[:], s[:], 1.0 / C, None, ALU.mult))
            step(nc.vector.tensor_tensor(y[:], y[:], spread(s[:], C), ALU.subtract))
            step(nc.vector.tensor_tensor(flat(sq[:]), flat(y[:]), flat(y[:]), ALU.mult))
            step(nc.vector.tensor_reduce(s[:], sq[:], AX.X, ALU.add))
            step(nc.vector.tensor_scalar(s[:], s[:], 1.0 / C, 1e-5, ALU.mult, ALU.add))
            dve.wait_ge(act_s.sem, act_s.base + 1)
            step(nc.vector.reciprocal(s[:], std[:]))
            step(nc.vector.tensor_tensor(out[:], y[:], spread(s[:], C), ALU.mult))

        @block.scalar
        def _(act):
            act.wait_ge(dve_s.sem, dve_s.base + 7)
            nc.scalar.activation(std[:], s[:], ACT.Sqrt).then_inc(act_s.sem, 1)

        act_s.base += 1
        dve_s.base += 9


def spline_pass(nc, sig, table, width, edge, running, final, zeros, cleared=()):
    count, ranked, extra = "count" in edge, edge.get("ranked"), "extra" in edge
    rank = ranked is not None
    per = 2 + B + 2 * count + 4 * rank
    with ExitStack() as ctx:
        uid = nc.next_id()

        def sb(name, shape, dt=F32):
            return ctx.enter_context(nc.sbuf_tensor(f"{name}{uid}", shape, dt))

        def pair(name, shape, dt=F32):
            return [sb(f"{name}{h}_", shape, dt) for h in range(2)]

        def sem(name):
            return ctx.enter_context(nc.semaphore(f"{name}{uid}"))

        index = pair("index", [P, B], I32)
        weight = pair("weight", [P, B])
        keep = pair("keep", [P, B])
        rows = pair("rows", [P, B, 2 * C])
        msg = pair("msg", [P, B, width])
        run = pair("run", [P, B, width])
        gathered = [sem(f"gathered{h}_") for h in range(2)]
        stored = [sem(f"stored{h}_") for h in range(2)]
        staged = [sem(f"staged{h}_") for h in range(2)]
        stepped = sem("stepped")
        if count:
            dst_lo, dst_hi = pair("dst_lo", [P, B]), pair("dst_hi", [P, B])
            at_lo, at_hi = pair("at_lo", [P, B, P], BF16), pair("at_hi", [P, B, J], BF16)
            blank = sb("blank", [P, P], BF16)
            p_count = ctx.enter_context(nc.psum_tensor(f"p_count{uid}", [P, 512], F32))
            counted = sem("counted")
        if rank:
            lo, hi = pair("lo", [P, RANKED]), pair("hi", [P, RANKED])
            one_lo, one_hi = pair("one_lo", [P, RANKED, P], BF16), pair("one_hi", [P, RANKED, J], BF16)
            lo_t, lo_tf = pair("lo_t", [P, GROUP, P], BF16), pair("lo_tf", [P, GROUP, P])
            earlier = pair("earlier", [P, PAIRS, P], BF16)
            seen = pair("seen", [P, J])
            picked = sb("picked", [P, RANKED, J])
            p_seen = ctx.enter_context(nc.psum_tensor(f"p_seen{uid}", [P, 512], F32))
            p_turn = ctx.enter_context(nc.psum_tensor(f"p_turn{uid}", [P, 8, P], BF16))
            p_same = ctx.enter_context(nc.psum_tensor(f"p_same{uid}", [P, 12, P], F32))
            p_look = ctx.enter_context(nc.psum_tensor(f"p_look{uid}", [P, RANKED, C], F32))
            turned, turned_sb, same, same_sb, summed, seen_sb, looked = (sem(n) for n in ("turned", "turned_sb", "same", "same_sb", "summed", "seen_sb", "looked"))
        block = ctx.enter_context(nc.Block())
        running_v = running[0:EP, :].rearrange("(p t) c -> p t c", p=P)
        INIT = 1 + 3 * count + 3 * rank
        Q = RANKED // GROUP

        @block.sync
        def _(sp):
            sp.dma_start(running[EP:EP + 1, :], zeros[0:1, 0:width]).then_inc(stored[0], 16)
            with sp.Fori(0, IT) as i:
                for h in range(2):
                    sp.wait_ge(stepped, INIT + per * (2 * i + h + 1))
                    sp.dma_start(running_v[:, bass.ds((2 * i + h) * B, B), :], run[h][:]).then_inc(stored[h], 16)
                    for dst in cleared:
                        sp.dma_start(dst[:, bass.ds((2 * i + h) * B, B), :], zeros[:, 0:B * dst.shape[2]].rearrange("p (t c) -> p t c", t=B)).then_inc(stored[h], 16)
            for h in range(2):
                sp.wait_ge(stored[h], 16 * IT * (1 + len(cleared)) + 16 * (h == 0))

        @block.gpsimd
        def _(pool):
            with pool.Fori(0, IT) as i:
                for h in range(2):
                    pool.wait_ge(staged[h], i + 1)
                    pool.sem_inc(sig["rounds"].sem, 1)
                    for k in range(B):
                        pool.indirect_dma_start(out=rows[h][:, k, :], out_offset=None, in_=table,
                                                in_offset=offsets(index[h][:, k:k + 1])).then_inc(gathered[h], 16)

        @block.scalar
        def _(act):
            def stage(h, at):
                nc.scalar.activation(weight[h][:], edge["weight"][:, bass.ds(at, B)], ACT.Copy)
                nc.scalar.activation(keep[h][:], edge["keep"][:, bass.ds(at, B)], ACT.Copy)
                if extra:
                    nc.scalar.activation(msg[h][:, :, C], edge["extra"][:, bass.ds(at, B)], ACT.Copy)
                if count:
                    nc.scalar.activation(dst_lo[h][:], edge["dst_lo"][:, bass.ds(at, B)], ACT.Copy)
                    nc.scalar.activation(dst_hi[h][:], edge["dst_hi"][:, bass.ds(at, B)], ACT.Copy)
                if rank:
                    nc.scalar.activation(lo[h][:], edge["src_lo"][:, bass.ds(at + ranked, RANKED)], ACT.Copy)
                    nc.scalar.activation(hi[h][:], edge["src_hi"][:, bass.ds(at + ranked, RANKED)], ACT.Copy)
                nc.scalar.copy(index[h][:], edge["src"][:, bass.ds(at, B)]).then_inc(staged[h], 1)

            def ranks(i, h):
                n = (2 * i + h) * Q
                turn_out(n, 0)
                for q in range(Q):
                    act.wait_ge(same, n + q + 1)
                    nc.scalar.activation(flat(earlier[q % 2][:]), flat(p_same[:, 0:PAIRS, :]), ACT.Relu).then_inc(same_sb, 1)
                    if q + 1 < Q:
                        turn_out(n + q + 1, q + 1)
                    act.wait_ge(summed, n + q + 1)
                    nc.scalar.activation(seen[(q + 1) % 2][:], p_seen[:, 0:J], ACT.Copy).then_inc(seen_sb, 1)

            def turn_out(n, q):
                act.wait_ge(turned, n + 1)
                nc.scalar.activation(flat(lo_t[q % 2][:]), flat(p_turn[:, 0:GROUP, :]), ACT.Copy)
                nc.scalar.activation(flat(lo_tf[q % 2][:]), flat(p_turn[:, 0:GROUP, :]), ACT.Copy).then_inc(turned_sb, 1)

            stage(0, 0)
            with act.Fori(0, IT) as i:
                act.wait_ge(stepped, INIT + per * (2 * i))
                stage(1, (2 * i + 1) * B)
                if rank:
                    ranks(i, 0)
                act.wait_ge(stepped, INIT + per * (2 * i + 1))
                stage(0, (2 * i + 2) * B)
                if rank:
                    ranks(i, 1)
            if count:
                act.wait_ge(counted, T + 1)
                nc.scalar.activation(edge["count"][:], p_count[:, 0:J], ACT.Copy).then_inc(staged[0], 1)
            if rank:
                act.wait_ge(summed, 2 * IT * Q)
                nc.scalar.activation(edge["seen"][:], p_seen[:, 0:J], ACT.Copy).then_inc(staged[0], 1)

        if count or rank:
            @block.tensor
            def _(pe):
                pe.wait_ge(stepped, INIT)
                if count:
                    nc.tensor.matmul(p_count[:, 0:J], blank[:], blank[:, 0:J], start=True, stop=False)

                def turn(n, h, q):
                    pe.wait_ge(turned_sb, n)
                    for k in range(GROUP):
                        ins = nc.tensor.transpose(p_turn[:, k, :], one_lo[h][:, q * GROUP + k, :], sig["ident_b"][:])
                    ins.then_inc(turned, 1)

                def ranks(i, h):
                    n = (2 * i + h) * Q
                    turn(n, h, 0)
                    for q in range(Q):
                        pe.wait_ge(turned_sb, n + q + 1)
                        pe.wait_ge(same_sb, n + q)
                        low = lo_t[q % 2]
                        for j in range(GROUP):
                            nc.tensor.matmul(p_same[:, PAIR[j], :], low[:, j, :], low[:, j, :], start=True, stop=False)
                            ins = nc.tensor.matmul(p_same[:, PAIR[j], :], sig["ident_b"][:], sig["not_earlier"][:], start=False, stop=True)
                            if j + 1 < GROUP:
                                ins = nc.tensor.matmul(p_same[:, PAIR[j] + 1:PAIR[j] + GROUP - j, :], low[:, j, :], low[:, j + 1:GROUP, :], start=True, stop=True)
                        ins.then_inc(same, 1)
                        if q + 1 < Q:
                            turn(n + q + 1, h, q + 1)
                        pe.wait_ge(seen_sb, n + q)
                        nc.tensor.matmul(p_seen[:, 0:J], sig["ident"][:], seen[q % 2][:], start=True, stop=False)
                        for k in range(GROUP):
                            kk = q * GROUP + k
                            ins = nc.tensor.matmul(p_seen[:, 0:J], one_lo[h][:, kk, :], one_hi[h][:, kk, :], start=False, stop=k == GROUP - 1)
                        ins.then_inc(summed, 1)
                        pe.wait_ge(same_sb, n + q + 1)
                        for k in range(GROUP):
                            kk = q * GROUP + k
                            nc.tensor.matmul(p_look[:, kk, 0:J], lo_tf[q % 2][:, k, :], seen[q % 2][:], start=True, stop=False)
                            for j in range(k + 1):
                                ins = nc.tensor.matmul(p_look[:, kk, 0:J], earlier[q % 2][:, PAIR[j] + k - j, :], one_hi[h][:, q * GROUP + j, :], start=False, stop=j == k)
                        ins.then_inc(looked, 1)

                with pe.Fori(0, IT) as i:
                    for h in range(2):
                        pe.wait_ge(stepped, INIT + per * (2 * i + h))
                        if rank:
                            ranks(i, h)
                        if count:
                            for k in range(B):
                                nc.tensor.matmul(p_count[:, 0:J], at_lo[h][:, k, :], at_hi[h][:, k, :], start=False, stop=False).then_inc(counted, 1)
                if count:
                    nc.tensor.matmul(p_count[:, 0:J], blank[:], blank[:, 0:J], start=False, stop=True).then_inc(counted, 1)

        @block.vector
        def _(dve):
            def one_hots(h, step):
                if count:
                    step(nc.vector.tensor_tensor(at_lo[h][:], repeat(sig["iota"][:], B), spread(dst_lo[h][:], P), ALU.is_equal))
                    step(nc.vector.tensor_tensor(at_hi[h][:], repeat(sig["iota"][:, 0:J], B), spread(dst_hi[h][:], J), ALU.is_equal))
                if rank:
                    step(nc.vector.tensor_tensor(one_lo[h][:], repeat(sig["iota"][:], RANKED), spread(lo[h][:], P), ALU.is_equal))
                    step(nc.vector.tensor_tensor(one_hi[h][:], repeat(sig["iota"][:, 0:J], RANKED), spread(hi[h][:], J), ALU.is_equal))

            nc.vector.memset(run[1][:, B - 1, :], 0.0).then_inc(stepped, 1)
            if count:
                nc.vector.memset(blank[:], 0.0).then_inc(stepped, 1)
            if rank:
                nc.vector.tensor_copy(seen[0][:], edge["seen"][:]).then_inc(stepped, 1)
            if count or rank:
                dve.wait_ge(staged[0], 1)
                one_hots(0, lambda ins: ins.then_inc(stepped, 1))
            with dve.Fori(0, IT) as i:
                for h in range(2):
                    n = [0]

                    def step(ins):
                        ins.then_inc(stepped, 1)
                        n[0] += 1

                    def after():
                        dve.wait_ge(stepped, INIT + per * (2 * i + h) + n[0])

                    dve.wait_ge(staged[h], i + 1)
                    dve.wait_ge(gathered[h], 16 * B * (i + 1))
                    step(nc.vector.tensor_tensor(msg[h][:, :, 0:C], rows[h][:, :, C:2 * C], spread(weight[h][:], C), ALU.mult))
                    after()
                    step(nc.vector.tensor_tensor(msg[h][:, :, 0:C], msg[h][:, :, 0:C], rows[h][:, :, 0:C], ALU.add))
                    dve.wait_ge(stored[h], 16 * (1 + len(cleared)) * i + 16 * (h == 0))
                    for k in range(B):
                        before = run[h][:, k - 1, :] if k else run[1 - h][:, B - 1, :]
                        after()
                        step(nc.vector.scalar_tensor_tensor(run[h][:, k, :], before, keep[h][:, k:k + 1], msg[h][:, k, :], ALU.mult, ALU.add))
                    if count or rank:
                        dve.wait_ge(staged[1 - h], i + 1 + h)
                    if count:
                        dve.wait_ge(counted, B * (2 * i + h))
                    if count or rank:
                        one_hots(1 - h, step)
                    if rank:
                        dve.wait_ge(looked, Q * (2 * i + h + 1))
                        step(nc.vector.tensor_tensor(picked[:], p_look[:, :, 0:J], one_hi[h][:], ALU.mult))
                        after()
                        step(nc.vector.tensor_reduce(edge["rank"][:, bass.ds((2 * i + h) * B + ranked, RANKED)], picked[:], AX.X, ALU.add))
                    assert n[0] == per
            dve.wait_ge(stepped, INIT + per * 2 * IT)
            nc.vector.tensor_copy(final[:, 0:width], run[1][:, B - 1, :]).then_inc(stepped, 1)


def split_rows(nc, sig, rows, width, parts):
    with ExitStack() as ctx:
        rest = ctx.enter_context(nc.sbuf_tensor(f"rest{nc.next_id()}", [P, J, width], F32))

        def body(step):
            left = rows
            for k, part in enumerate(parts):
                for c in range(width // SLICE):
                    cut = slice(c * SLICE, (c + 1) * SLICE)
                    step(nc.vector.tensor_copy(part[:, c, :, :], left[:, :, cut]))
                    if k + 1 < len(parts):
                        step(nc.vector.tensor_tensor(rest[:, :, cut], left[:, :, cut], part[:, c, :, :], ALU.subtract))
                left = rest

        on_vector(nc, sig, body)


def graph_pass(nc, sig, table, width, edge, parts, running, final, zeros):
    SLICES = width // SLICE
    ON_CHIP = PICKS // SLICES
    GATHERED = B - ON_CHIP
    BANK = 512 // SLICE
    CHAIN = B // 2 + 6
    AFTER_HOT = 1 + CHAIN
    per = 2 * PICKS + 2 + AFTER_HOT
    INIT = 2 + AFTER_HOT
    PICK_READ = (1, 2, 5, 6)
    with ExitStack() as ctx:
        uid = nc.next_id()

        def sb(name, shape, dt=F32):
            return ctx.enter_context(nc.sbuf_tensor(f"{name}{uid}", shape, dt))

        def pair(name, shape, dt=F32):
            return [sb(f"{name}{h}_", shape, dt) for h in range(2)]

        def sem(name):
            return ctx.enter_context(nc.semaphore(f"{name}{uid}"))

        index = pair("index", [P, GATHERED], I32)
        weight, keep = pair("weight", [P, B]), pair("keep", [P, B])
        lo, hi = pair("lo", [P, ON_CHIP]), pair("hi", [P, ON_CHIP])
        one_lo, one_hi = pair("one_lo", [P, ON_CHIP, P], BF16), pair("one_hi", [P, ON_CHIP, J])
        lo_t = pair("lo_t", [P, ON_CHIP, P], BF16)
        rows, msg = (pair(n, [P, B, width]) for n in ("rows", "msg"))
        run = pair("run", [P, 1 + B, width])
        both, two, held = sb("both", [P, B // 2]), sb("two", [P, B // 2, width]), sb("held", [P, B // 2, width])
        picked = pair("picked", [P, SLICE, J])
        p_turn = ctx.enter_context(nc.psum_tensor(f"p_turn{uid}", [P, 8, P], BF16))
        p_slots = [ctx.enter_context(nc.psum_tensor(f"p_slots{k}_{uid}", [P, 2 * BANK, SLICE], F32)) for k in range(2)]
        gathered, stored, indexed, staged = ([sem(f"{n}{h}_") for h in range(2)] for n in ("gathered", "stored", "indexed", "staged"))
        stepped, turned, turned_sb, looked = (sem(n) for n in ("stepped", "turned", "turned_sb", "looked"))
        block = ctx.enter_context(nc.Block())
        running_v = running[0:EP, :].rearrange("(p t) c -> p t c", p=P)

        @block.sync
        def _(sp):
            for h in range(2):
                cut = slice(h * width // 2, (h + 1) * width // 2)
                sp.dma_start(running[EP:EP + 1, cut], zeros[0:1, cut]).then_inc(stored[h], 16)
            with sp.Fori(0, IT) as i:
                for h in range(2):
                    sp.wait_ge(stepped, INIT + per * (2 * i + h + 1))
                    sp.dma_start(running_v[:, bass.ds((2 * i + h) * B, B), :], run[h][:, 1:1 + B, :]).then_inc(stored[h], 16)
            for h in range(2):
                sp.wait_ge(stored[h], 16 * (IT + 1))

        @block.gpsimd
        def _(pool):
            with pool.Fori(0, IT) as i:
                for h in range(2):
                    pool.wait_ge(indexed[h], i + 1)
                    pool.sem_inc(sig["rounds"].sem, 1)
                    for k in range(GATHERED):
                        pool.indirect_dma_start(out=rows[h][:, ON_CHIP + k, :], out_offset=None, in_=table,
                                                in_offset=offsets(index[h][:, k:k + 1])).then_inc(gathered[h], 16)

        @block.scalar
        def _(act):
            def stage_index(h, at):
                nc.scalar.copy(index[h][:], edge["src"][:, bass.ds(at + ON_CHIP, GATHERED)]).then_inc(indexed[h], 1)

            def stage(h, at):
                nc.scalar.activation(lo[h][:], edge["src_lo"][:, bass.ds(at, ON_CHIP)], ACT.Copy)
                nc.scalar.activation(hi[h][:], edge["src_hi"][:, bass.ds(at, ON_CHIP)], ACT.Copy)
                nc.scalar.activation(weight[h][:], edge["weight"][:, bass.ds(at, B)], ACT.Copy)
                nc.scalar.activation(keep[h][:], edge["keep"][:, bass.ds(at, B)], ACT.Copy).then_inc(staged[h], 1)

            def turn_out(n, h):
                act.wait_ge(turned, n + 1)
                nc.scalar.activation(flat(lo_t[h][:]), flat(p_turn[:, 0:ON_CHIP, :]), ACT.Copy).then_inc(turned_sb, 1)

            stage_index(0, 0)
            stage(0, 0)
            turn_out(0, 0)
            with act.Fori(0, IT) as i:
                for h in range(2):
                    n = 2 * i + h
                    act.wait_ge(stepped, INIT + per * n - CHAIN)
                    stage_index(1 - h, (n + 1) * B)
                    act.wait_ge(stepped, INIT + per * n)
                    stage(1 - h, (n + 1) * B)
                    turn_out(n + 1, 1 - h)

        @block.tensor
        def _(pe):
            def turn(n, h):
                pe.wait_ge(stepped, INIT + per * n - AFTER_HOT)
                pe.sem_inc(sig["rounds"].sem, 1)
                for k in range(ON_CHIP):
                    ins = nc.tensor.transpose(p_turn[:, k, :], one_lo[h][:, k, :], sig["ident_b"][:])
                ins.then_inc(turned, 1)

            with pe.Fori(0, IT) as i:
                for h in range(2):
                    n = 2 * i + h
                    turn(n, h)
                    pe.wait_ge(turned_sb, n + 1)
                    for m in range(PICKS):
                        if m >= 2:
                            pe.wait_ge(stepped, INIT + per * n + PICK_READ[m - 2])
                        to = p_slots[m % 2]
                        for j0, j1 in ((0, BANK), (BANK, J)):
                            for k, part in enumerate(parts):
                                ins = nc.tensor.matmul(flat(to[:, j0:j1, :]), lo_t[h][:, m // SLICES, :], flat(part[:, m % SLICES, j0:j1, :]),
                                                       start=k == 0, stop=k == len(parts) - 1)
                        ins.then_inc(looked, 1)
            turn(2 * IT, 0)

        @block.vector
        def _(dve):
            def one_hots(h, step):
                step(nc.vector.tensor_tensor(one_lo[h][:], repeat(sig["iota"][:], ON_CHIP), spread(lo[h][:], P), ALU.is_equal))
                step(nc.vector.tensor_tensor(one_hi[h][:], repeat(sig["iota"][:, 0:J], ON_CHIP), spread(hi[h][:], J), ALU.is_equal))

            dve.wait_ge(staged[0], 1)
            one_hots(0, lambda ins: ins.then_inc(stepped, 1))
            nc.vector.memset(run[1][:, B, :], 0.0).then_inc(stepped, AFTER_HOT)
            with dve.Fori(0, IT) as i:
                for h in range(2):
                    n = [0]

                    def step(ins):
                        ins.then_inc(stepped, 1)
                        n[0] += 1

                    def after(back=0):
                        dve.wait_ge(stepped, INIT + per * (2 * i + h) + n[0] - back)

                    for m0 in range(0, PICKS, 2):
                        for m in (m0, m0 + 1):
                            dve.wait_ge(looked, PICKS * (2 * i + h) + m + 1)
                            if m0:
                                after(1)
                            k = m // SLICES
                            step(nc.vector.tensor_tensor(picked[m % 2][:], p_slots[m % 2][:, 0:J, :].rearrange("p j c -> p c j"),
                                                         one_hi[h][:, k:k + 1, :].broadcast_to([P, SLICE, J]), ALU.mult))
                        for m in (m0, m0 + 1):
                            k, c = m // SLICES, m % SLICES
                            after(1)
                            step(nc.vector.tensor_reduce(rows[h][:, k, c * SLICE:(c + 1) * SLICE], picked[m % 2][:], AX.X, ALU.add))
                    dve.wait_ge(staged[1 - h], i + 1 + h)
                    one_hots(1 - h, step)
                    dve.wait_ge(gathered[h], 16 * GATHERED * (i + 1))
                    after(2)
                    step(nc.vector.tensor_tensor(msg[h][:], rows[h][:], spread(weight[h][:], width), ALU.mult))
                    step(nc.vector.tensor_tensor(both[:], keep[h][:, 0:B:2], keep[h][:, 1:B:2], ALU.mult))
                    after(1)
                    step(nc.vector.tensor_tensor(two[:], msg[h][:, 0:B:2, :], spread(keep[h][:, 1:B:2], width), ALU.mult))
                    dve.wait_ge(stored[h], 16 * (i + 1))
                    step(nc.vector.tensor_copy(run[h][:, 0, :], run[1 - h][:, B, :]))
                    after(1)
                    step(nc.vector.tensor_tensor(two[:], two[:], msg[h][:, 1:B:2, :], ALU.add))
                    for k in range(B // 2):
                        after()
                        step(nc.vector.scalar_tensor_tensor(run[h][:, 2 * k + 2, :], run[h][:, 2 * k, :], both[:, k:k + 1], two[:, k, :], ALU.mult, ALU.add))
                    after(1)
                    step(nc.vector.tensor_tensor(held[:], run[h][:, 0:B:2, :], spread(keep[h][:, 0:B:2], width), ALU.mult))
                    after()
                    step(nc.vector.tensor_tensor(run[h][:, 1:B:2, :], held[:], msg[h][:, 0:B:2, :], ALU.add))
                    assert n[0] == per
            dve.wait_ge(stepped, INIT + per * 2 * IT)
            nc.vector.tensor_copy(final[:, 0:width], run[1][:, B, :]).then_inc(stepped, 1)


def spread_to_edges(nc, sig, node_rows, begin_row, edge_rows, table, first_key, first_rows):
    with ExitStack() as ctx:
        block = ctx.enter_context(nc.Block())
        fetched = sig["fetched"]

        @block.gpsimd
        def _(pool):
            pool.indirect_dma_start(out=first_rows[:], out_offset=None, in_=table, in_offset=offsets(first_key)).then_inc(fetched.sem, 16)
            for j in range(J):
                pool.indirect_dma_start(out=edge_rows, out_offset=offsets(begin_row[:, j:j + 1]), in_=node_rows[:, j, :], in_offset=None,
                                        bounds_check=EP - 1, oob_is_err=False).then_inc(fetched.sem, 16)
            pool.wait_ge(fetched.sem, fetched.base + 16 * (J + 1))

        fetched.base += 16 * (J + 1)


def attention_pass(nc, sig, table, edge, labels, label_rows, node_rows, first_rows, w_label, w_label_att, running, final, sent, zeros):
    KEY, OUT0, LABEL0, IN0, EF0, WIDE = 0, 1, 1 + C, SENT, SENT + C, SENT + 2 * C
    SUMS = LABELS + C
    per = 1 + B + 11 + 2 * B
    with ExitStack() as ctx:
        def sb(name, shape, dt=F32):
            return ctx.enter_context(nc.sbuf_tensor(name, shape, dt))

        def pair(name, shape, dt=F32):
            return [sb(f"{name}{h}", shape, dt) for h in range(2)]

        def sem(name):
            return ctx.enter_context(nc.semaphore(name))

        index, place = pair("a_index", [P, B], I32), pair("a_place", [P, B], I32)
        keep, pen, rank, key = pair("a_keep", [P, B]), pair("a_pen", [P, B]), pair("a_rank", [P, B]), pair("a_key", [P, B])
        rows = pair("a_rows", [P, B, 2 * C + 1])
        begun, xdst = pair("a_begun", [P, B, C]), pair("a_xdst", [P, B, C])
        label, label_row = pair("a_label", [LABELS, B * P]), pair("a_label_row", [P, B, LABELS])
        product = sb("a_product", [P, B, C])
        score = pair("a_score", [P, B])
        label_score, att = pair("a_label_score", [P, B]), pair("a_att", [P, B])
        msg = pair("a_msg", [P, B, WIDE])
        run = pair("a_run", [P, B, RUN])
        p_label = [ctx.enter_context(nc.psum_tensor(f"a_p_label{h}", [P, B, C], F32)) for h in range(2)]
        p_score = [ctx.enter_context(nc.psum_tensor(f"a_p_score{h}", [P, 512], F32)) for h in range(2)]
        gathered, stored, staged, loaded, scattered = ([sem(f"a_{n}{h}") for h in range(2)] for n in ("gathered", "stored", "staged", "loaded", "scattered"))
        stepped, labelled, activated = sem("a_stepped"), sem("a_labelled"), sem("a_activated")
        block = ctx.enter_context(nc.Block())
        running_v = running[0:EP, :].rearrange("(p t) c -> p t c", p=P)
        node_rows_v = node_rows[0:EP, :].rearrange("(p t) c -> p t c", p=P)
        INIT = 2 * per
        PLACED = 1 + B + 11

        @block.sync
        def _(sp):
            def load(h, n):
                sp.dma_start(begun[h][:], node_rows_v[:, bass.ds(n * B, B), :]).then_inc(loaded[h], 16)
                sp.dma_start(label[h][:], labels[:, bass.ds(n * (B * P), B * P)]).then_inc(loaded[h], 16)
                sp.dma_start(label_row[h][:], label_rows[:, bass.ds(n * B, B), :]).then_inc(loaded[h], 16)

            def store(h, i):
                sp.wait_ge(stepped, INIT + per * (2 * i + h + 1))
                sp.dma_start(running_v[:, bass.ds((2 * i + h) * B, B), :], run[h][:]).then_inc(stored[h], 16)

            for h in range(2):
                cut = slice(h * RUN // 2, (h + 1) * RUN // 2)
                sp.dma_start(running[EP:EP + 1, cut], zeros[0:1, cut]).then_inc(stored[h], 16)
            load(0, 0)
            load(1, 1)
            with sp.Fori(0, IT - 1) as i:
                for h in range(2):
                    store(h, i)
                    load(h, 2 * i + 2 + h)
            for h in range(2):
                store(h, IT - 1)
            for h in range(2):
                sp.wait_ge(stored[h], 16 * (IT + 1))

        @block.gpsimd
        def _(pool):
            def gather(h, i):
                pool.wait_ge(staged[h], i + 1)
                pool.sem_inc(sig["rounds"].sem, 1)
                for k in range(B):
                    pool.indirect_dma_start(out=rows[h][:, k, :], out_offset=None, in_=table,
                                            in_offset=offsets(index[h][:, k:k + 1])).then_inc(gathered[h], 16)

            def scatter(h, i):
                pool.wait_ge(stepped, INIT + per * (2 * i + h) + PLACED)
                pool.sem_inc(sig["rounds"].sem, 1)
                for k in range(B):
                    pool.indirect_dma_start(out=sent, out_offset=offsets(place[h][:, k:k + 1]), in_=msg[h][:, k, 0:SENT],
                                            in_offset=None).then_inc(scattered[h], 16)

            gather(0, 0)
            with pool.Fori(0, IT - 1) as i:
                gather(1, i)
                scatter(0, i)
                gather(0, i + 1)
                scatter(1, i)
            gather(1, IT - 1)
            scatter(0, IT - 1)
            scatter(1, IT - 1)
            for h in range(2):
                pool.wait_ge(scattered[h], 16 * B * IT)

        @block.scalar
        def _(act):
            def stage(h, at):
                nc.scalar.activation(keep[h][:], edge["keep"][:, bass.ds(at, B)], ACT.Copy)
                nc.scalar.activation(rank[h][:], edge["rank"][:, bass.ds(at, B)], ACT.Copy)
                nc.scalar.activation(key[h][:], edge["src"][:, bass.ds(at, B)], ACT.Copy)
                nc.scalar.copy(index[h][:], edge["src"][:, bass.ds(at, B)]).then_inc(staged[h], 1)

            def attention(h, i):
                act.wait_ge(labelled, 2 * i + h + 1)
                nc.scalar.activation(label_score[h][:], p_score[h][:, 0:B], ACT.Copy).then_inc(activated, 1)
                act.wait_ge(stepped, INIT + per * (2 * i + h) + 1 + B + 5)
                nc.scalar.activation(att[h][:], score[h][:], ACT.Sigmoid).then_inc(activated, 1)

            stage(0, 0)
            with act.Fori(0, IT) as i:
                act.wait_ge(stepped, INIT + per * (2 * i))
                stage(1, (2 * i + 1) * B)
                attention(0, i)
                act.wait_ge(stepped, INIT + per * (2 * i + 1))
                stage(0, (2 * i + 2) * B)
                attention(1, i)

        @block.tensor
        def _(pe):
            with pe.Fori(0, IT) as i:
                for h in range(2):
                    pe.wait_ge(loaded[h], 48 * (i + 1))
                    pe.wait_ge(stepped, INIT + per * (2 * i + h - 1))
                    for k in range(B):
                        edges = label[h][:, k * P:(k + 1) * P]
                        nc.tensor.matmul(p_label[h][:, k, :], edges, w_label, start=True, stop=True)
                        ins = nc.tensor.matmul(p_score[h][:, k:k + 1], edges, w_label_att, start=True, stop=True)
                    ins.then_inc(labelled, 1)

        @block.vector
        def _(dve):
            nc.vector.memset(run[1][:, B - 1, 0:SUMS], 0.0).then_inc(stepped, 1)
            nc.vector.memset(run[1][:, B - 1, SUMS:RUN], -BIG).then_inc(stepped, 1)
            nc.vector.tensor_copy(xdst[1][:, B - 1, :], first_rows[:, C:2 * C]).then_inc(stepped, INIT - 2)
            def both_halves(i, first):
                for h in range(2):
                    n = [0]

                    def step(ins):
                        ins.then_inc(stepped, 1)
                        n[0] += 1

                    def after(back=0):
                        dve.wait_ge(stepped, INIT + per * (2 * i + h) + n[0] - back)

                    dve.wait_ge(staged[h], i + 1)
                    step(nc.vector.tensor_scalar(pen[h][:], keep[h][:], BIG, -BIG, ALU.mult, ALU.add))
                    dve.wait_ge(loaded[h], 48 * (i + 1))
                    for k in range(B):
                        before = xdst[h][:, k - 1, :] if k else xdst[1 - h][:, B - 1, :]
                        after()
                        step(nc.vector.scalar_tensor_tensor(xdst[h][:, k, :], before, keep[h][:, k:k + 1], begun[h][:, k, :], ALU.mult, ALU.add))
                    dve.wait_ge(gathered[h], 16 * B * (i + 1))
                    after()
                    step(nc.vector.tensor_tensor(product[:], rows[h][:, :, 0:C], xdst[h][:], ALU.mult))
                    after()
                    step(nc.vector.tensor_reduce(score[h][:], product[:], AX.X, ALU.add))
                    after()
                    step(nc.vector.scalar_tensor_tensor(score[h][:], score[h][:], 0.01, score[h][:], ALU.mult, ALU.max))
                    dve.wait_ge(activated, 2 * (2 * i + h) + 1)
                    step(nc.vector.scalar_tensor_tensor(label_score[h][:], label_score[h][:], 0.01, label_score[h][:], ALU.mult, ALU.max))
                    after()
                    step(nc.vector.tensor_tensor(score[h][:], score[h][:], label_score[h][:], ALU.add))
                    dve.wait_ge(activated, 2 * (2 * i + h) + 2)
                    if not first:
                        dve.wait_ge(scattered[h], 16 * B * i)
                    step(nc.vector.tensor_tensor(msg[h][:, :, OUT0:LABEL0], xdst[h][:], spread(att[h][:], C), ALU.mult))
                    step(nc.vector.tensor_tensor(msg[h][:, :, LABEL0:IN0], label_row[h][:], spread(att[h][:], LABELS), ALU.mult))
                    step(nc.vector.tensor_tensor(msg[h][:, :, EF0:WIDE], p_label[h][:], spread(att[h][:], C), ALU.mult))
                    step(nc.vector.tensor_tensor(msg[h][:, :, IN0:EF0], rows[h][:, :, C:2 * C], spread(att[h][:], C), ALU.mult))
                    step(nc.vector.tensor_copy(msg[h][:, :, KEY], key[h][:]))
                    step(nc.vector.tensor_tensor(place[h][:], rows[h][:, :, 2 * C], rank[h][:], ALU.add))
                    dve.wait_ge(stored[h], 16 * (i + 1))
                    after(1)
                    for k in range(B):
                        before = run[h][:, k - 1, :] if k else run[1 - h][:, B - 1, :]
                        if k:
                            after(1)
                        step(nc.vector.scalar_tensor_tensor(run[h][:, k, 0:SUMS], before[:, 0:SUMS], keep[h][:, k:k + 1],
                                                            msg[h][:, k, LABEL0:EF0], ALU.mult, ALU.add))
                        if k:
                            after(1)
                        step(nc.vector.scalar_tensor_tensor(run[h][:, k, SUMS:RUN], before[:, SUMS:RUN], pen[h][:, k:k + 1],
                                                            msg[h][:, k, IN0:WIDE], ALU.add, ALU.max))
                    assert n[0] == per, n

            both_halves(0, True)
            with dve.Fori(1, IT) as i:
                both_halves(i, False)
            dve.wait_ge(stepped, INIT + per * 2 * IT)
            nc.vector.tensor_copy(final[:], run[1][:, B - 1, :]).then_inc(stepped, 1)


def source_pass(nc, sig, block, ctx, sent, w_labels, running, final, first_last, zeros):
    SUMS = C + LABELS
    per = 4 + 2 * B

    def sb(name, shape, dt=F32):
        return ctx.enter_context(nc.sbuf_tensor(name, shape, dt))

    def pair(name, shape, dt=F32):
        return [sb(f"{name}{h}", shape, dt) for h in range(2)]

    def sem(name):
        return ctx.enter_context(nc.semaphore(name))

    rows = pair("s_rows", [P, B, SENT])
    peak = pair("s_peak", [P, B, 2 * C])
    run = pair("s_run", [P, B, RUN])
    keep, pen = pair("s_keep", [P, B]), pair("s_pen", [P, B])
    label, label_t = sb("s_label", [P, B, LABELS]), sb("s_label_t", [B * LABELS, P])
    last_key = sb("s_last_key", [P, 1])
    p_turn = ctx.enter_context(nc.psum_tensor("s_p_turn", [P, 512], F32))
    p_ef = ctx.enter_context(nc.psum_tensor("s_p_ef", [P, B, C], F32))
    loaded, stored = ([sem(f"s_{n}{h}") for h in range(2)] for n in ("loaded", "stored"))
    stepped, ends_loaded, taken, turned, turned_sb, projected, peaked = (
        sem(f"s_{n}") for n in ("stepped", "ends_loaded", "taken", "turned", "turned_sb", "projected", "peaked"))
    running_v = running[0:EP, :].rearrange("(p t) c -> p t c", p=P)
    sent_v = sent.rearrange("(p t) c -> p t c", p=P)
    INIT = 2 * per

    @block.sync
    def _(sp):
        def load(h, n):
            sp.dma_start(rows[h][:], sent_v[:, bass.ds(n * B, B), :]).then_inc(loaded[h], 16)

        def store(h, i, more):
            sp.wait_ge(stepped, INIT + per * (2 * i + h + 1))
            if more:
                load(h, 2 * i + 2 + h)
            sp.dma_start(running_v[:, bass.ds((2 * i + h) * B, B), :], run[h][:]).then_inc(stored[h], 16)

        load(0, 0)
        load(1, 1)
        sp.dma_start(first_last[:, 0:2], sent_v[:, 0, 0:2]).then_inc(ends_loaded, 16)
        sp.dma_start(first_last[:, 2:4], sent_v[:, T - 1, 0:2]).then_inc(ends_loaded, 16)
        for h in range(2):
            cut = slice(h * RUN // 2, (h + 1) * RUN // 2)
            sp.dma_start(running[EP:EP + 1, cut], zeros[0:1, cut]).then_inc(stored[h], 16)
        with sp.Fori(0, IT - 1) as i:
            for h in range(2):
                store(h, i, True)
        for h in range(2):
            store(h, IT - 1, False)
        for h in range(2):
            sp.wait_ge(stored[h], 16 * (IT + 1))
        sp.wait_ge(ends_loaded, 32)

    @block.scalar
    def _(act):
        act.sem_inc(turned, 1)
        with act.Fori(0, IT) as i:
            for h in range(2):
                n = 2 * i + h
                act.wait_ge(loaded[h], 16 * (i + 1))
                act.wait_ge(turned, n + 1)
                nc.scalar.activation(label[:], rows[h][:, :, 1 + C:SENT], ACT.Copy).then_inc(taken, 1)
                act.wait_ge(stepped, INIT + per * (n - 1))
                nc.scalar.activation(peak[h][:, :, 0:C], rows[h][:, :, 1:1 + C], ACT.Copy)
                act.wait_ge(turned, n + 2)
                nc.scalar.activation(label_t[:], p_turn[:, 0:P], ACT.Copy).then_inc(turned_sb, 1)
                act.wait_ge(projected, n + 1)
                nc.scalar.activation(peak[h][:, :, C:2 * C], p_ef[:], ACT.Copy).then_inc(peaked, 1)

    @block.tensor
    def _(pe):
        pe.sem_inc(peaked, 1)
        with pe.Fori(0, IT) as i:
            for h in range(2):
                n = 2 * i + h
                pe.wait_ge(taken, n + 1)
                pe.wait_ge(peaked, n + 1)
                pe.sem_inc(sig["rounds"].sem, 1)
                nc.tensor.transpose(p_turn[:, 0:P], flat(label[:]), sig["ident"][:]).then_inc(turned, 1)
                pe.wait_ge(turned_sb, n + 1)
                for k in range(0, B, 512 // C):
                    ins = nc.tensor.matmul(flat(p_ef[:, k:k + 512 // C, :]), label_t[:], flat(w_labels[:, k:k + 512 // C, :]), start=True, stop=True)
                ins.then_inc(projected, 1)

    @block.vector
    def _(dve):
        nc.vector.memset(run[1][:, B - 1, 0:SUMS], 0.0).then_inc(stepped, 1)
        nc.vector.memset(run[1][:, B - 1, SUMS:RUN], -BIG).then_inc(stepped, 1)
        nc.vector.memset(last_key[:], -1.0).then_inc(stepped, INIT - 2)
        with dve.Fori(0, IT) as i:
            for h in range(2):
                n = [0]

                def step(ins):
                    ins.then_inc(stepped, 1)
                    n[0] += 1

                def after(back=0):
                    dve.wait_ge(stepped, INIT + per * (2 * i + h) + n[0] - back)

                dve.wait_ge(loaded[h], 16 * (i + 1))
                after()
                step(nc.vector.tensor_tensor(keep[h][:, 0:1], rows[h][:, 0, 0:1], last_key[:], ALU.is_equal))
                step(nc.vector.tensor_tensor(keep[h][:, 1:B], rows[h][:, 1:B, 0], rows[h][:, 0:B - 1, 0], ALU.is_equal))
                after()
                step(nc.vector.tensor_copy(last_key[:], rows[h][:, B - 1, 0:1]))
                step(nc.vector.tensor_scalar(pen[h][:], keep[h][:], BIG, -BIG, ALU.mult, ALU.add))
                dve.wait_ge(stored[h], 16 * (i + 1))
                dve.wait_ge(peaked, 2 * i + h + 2)
                after()
                for k in range(B):
                    before = run[h][:, k - 1, :] if k else run[1 - h][:, B - 1, :]
                    if k:
                        after(1)
                    step(nc.vector.scalar_tensor_tensor(run[h][:, k, 0:SUMS], before[:, 0:SUMS], keep[h][:, k:k + 1], rows[h][:, k, 1:SENT], ALU.mult, ALU.add))
                    if k:
                        after(1)
                    step(nc.vector.scalar_tensor_tensor(run[h][:, k, SUMS:RUN], before[:, SUMS:RUN], pen[h][:, k:k + 1], peak[h][:, k, :], ALU.add, ALU.max))
                assert n[0] == per, n
        dve.wait_ge(stepped, INIT + per * 2 * IT)
        nc.vector.tensor_copy(final[:, 0:RUN], run[1][:, B - 1, :]).then_inc(stepped, 1)


def softmax_pass(nc, sig, table, edge, attrs, w_edge, w_edge_att, running, final, zeros):
    per = 13 + B + 1
    S, W = C + 1, C + 2
    with ExitStack() as ctx:
        def sb(name, shape, dt=F32):
            return ctx.enter_context(nc.sbuf_tensor(name, shape, dt))

        def pair(name, shape, dt=F32):
            return [sb(f"{name}{h}", shape, dt) for h in range(2)]

        def sem(name):
            return ctx.enter_context(nc.semaphore(name))

        index = pair("e_index", [P, B], I32)
        keep, pen, at_dst = pair("e_keep", [P, B]), pair("e_pen", [P, B]), pair("e_at_dst", [P, B])
        rows = pair("e_rows", [P, B, W])
        attr = pair("e_attr", [EDIM, B * P])
        edge_score, score, bounded = pair("e_edge_score", [P, B]), pair("e_score", [P, B]), pair("e_bounded", [P, B])
        top = pair("e_top", [P, 1 + B])
        exps = pair("e_exps", [P, 2 * B])
        factor = pair("e_factor", [P, 2 * B])
        msg = pair("e_msg", [P, B, S])
        run = pair("e_run", [P, B, W])
        p_edge = [ctx.enter_context(nc.psum_tensor(f"e_p_edge{h}", [P, B, C], F32)) for h in range(2)]
        p_score = [ctx.enter_context(nc.psum_tensor(f"e_p_score{h}", [P, 512], F32)) for h in range(2)]
        gathered, stored, staged, loaded = ([sem(f"e_{n}{h}") for h in range(2)] for n in ("gathered", "stored", "staged", "loaded"))
        stepped, projected, activated = sem("e_stepped"), sem("e_projected"), sem("e_activated")
        block = ctx.enter_context(nc.Block())
        running_v = running[0:EP, :].rearrange("(p t) c -> p t c", p=P)
        INIT = per

        @block.sync
        def _(sp):
            def load(h, n):
                sp.dma_start(attr[h][:], attrs[:, bass.ds(n * (B * P), B * P)]).then_inc(loaded[h], 16)

            def store(h, i):
                sp.wait_ge(stepped, INIT + per * (2 * i + h + 1))
                sp.dma_start(running_v[:, bass.ds((2 * i + h) * B, B), :], run[h][:]).then_inc(stored[h], 16)

            sp.dma_start(running[EP:EP + 1, :], zeros[0:1, 0:W]).then_inc(stored[0], 16)
            load(0, 0)
            load(1, 1)
            with sp.Fori(0, IT - 1) as i:
                for h in range(2):
                    store(h, i)
                    load(h, 2 * i + 2 + h)
            for h in range(2):
                store(h, IT - 1)
            for h in range(2):
                sp.wait_ge(stored[h], 16 * IT + 16 * (h == 0))

        @block.gpsimd
        def _(pool):
            with pool.Fori(0, IT) as i:
                for h in range(2):
                    pool.wait_ge(staged[h], i + 1)
                    pool.sem_inc(sig["rounds"].sem, 1)
                    for k in range(B):
                        pool.indirect_dma_start(out=rows[h][:, k, :], out_offset=None, in_=table,
                                                in_offset=offsets(index[h][:, k:k + 1])).then_inc(gathered[h], 16)

        @block.scalar
        def _(act):
            def stage(h, at):
                nc.scalar.activation(keep[h][:], edge["keep"][:, bass.ds(at, B)], ACT.Copy)
                nc.scalar.activation(at_dst[h][:], edge["at_dst"][:, bass.ds(at, B)], ACT.Copy)
                nc.scalar.copy(index[h][:], edge["src"][:, bass.ds(at, B)]).then_inc(staged[h], 1)

            def activate(h, i):
                act.wait_ge(projected, 2 * i + h + 1)
                nc.scalar.activation(edge_score[h][:], p_score[h][:, 0:B], ACT.Copy).then_inc(activated, 1)
                act.wait_ge(stepped, INIT + per * (2 * i + h) + 10)
                nc.scalar.activation(factor[h][:], exps[h][:], ACT.Exp).then_inc(activated, 1)

            stage(0, 0)
            with act.Fori(0, IT) as i:
                act.wait_ge(stepped, INIT + per * (2 * i))
                stage(1, (2 * i + 1) * B)
                activate(0, i)
                act.wait_ge(stepped, INIT + per * (2 * i + 1))
                stage(0, (2 * i + 2) * B)
                activate(1, i)

        @block.tensor
        def _(pe):
            with pe.Fori(0, IT) as i:
                for h in range(2):
                    pe.wait_ge(loaded[h], 16 * (i + 1))
                    pe.wait_ge(stepped, per * (2 * i + h))
                    for k in range(B):
                        edges = attr[h][:, k * P:(k + 1) * P]
                        nc.tensor.matmul(p_edge[h][:, k, :], edges, w_edge, start=True, stop=True)
                        ins = nc.tensor.matmul(p_score[h][:, k:k + 1], edges, w_edge_att, start=True, stop=True)
                    ins.then_inc(projected, 1)

        @block.vector
        def _(dve):
            nc.vector.memset(run[1][:, B - 1, :], 0.0).then_inc(stepped, 1)
            nc.vector.memset(top[1][:, B:B + 1], -BIG).then_inc(stepped, INIT - 1)
            with dve.Fori(0, IT) as i:
                for h in range(2):
                    n = [0]

                    def step(ins):
                        ins.then_inc(stepped, 1)
                        n[0] += 1

                    def after(back=0):
                        dve.wait_ge(stepped, INIT + per * (2 * i + h) + n[0] - back)

                    dve.wait_ge(staged[h], i + 1)
                    step(nc.vector.tensor_scalar(pen[h][:], keep[h][:], BIG, -BIG, ALU.mult, ALU.add))
                    after()
                    step(nc.vector.tensor_copy(top[h][:, 0:1], top[1 - h][:, B:B + 1]))
                    dve.wait_ge(gathered[h], 16 * B * (i + 1))
                    dve.wait_ge(activated, 2 * (2 * i + h) + 1)
                    step(nc.vector.tensor_tensor(score[h][:], rows[h][:, :, C], at_dst[h][:], ALU.add))
                    after()
                    step(nc.vector.tensor_tensor(score[h][:], score[h][:], edge_score[h][:], ALU.add))
                    after()
                    step(nc.vector.scalar_tensor_tensor(score[h][:], score[h][:], 0.2, score[h][:], ALU.mult, ALU.max))
                    after()
                    step(nc.vector.tensor_scalar(bounded[h][:], score[h][:], -1.0e9, None, ALU.max))
                    after()
                    step(nc.vector.tensor_tensor_scan(top[h][:, 1:1 + B], pen[h][:], bounded[h][:], top[h][:, 0:1], ALU.add, ALU.max))
                    after()
                    step(nc.vector.tensor_tensor(exps[h][:, 0:B], score[h][:], top[h][:, 1:1 + B], ALU.subtract))
                    step(nc.vector.tensor_tensor(exps[h][:, B:2 * B], top[h][:, 0:B], top[h][:, 1:1 + B], ALU.subtract))
                    after()
                    step(nc.vector.scalar_tensor_tensor(exps[h][:, B:2 * B], exps[h][:, B:2 * B], 0.0, pen[h][:], ALU.min, ALU.add))
                    step(nc.vector.tensor_tensor(msg[h][:, :, 0:C], rows[h][:, :, 0:C], p_edge[h][:], ALU.add))
                    dve.wait_ge(activated, 2 * (2 * i + h) + 2)
                    after()
                    step(nc.vector.tensor_tensor(msg[h][:, :, 0:C], msg[h][:, :, 0:C], spread(factor[h][:, 0:B], C), ALU.mult))
                    step(nc.vector.tensor_copy(msg[h][:, :, C], factor[h][:, 0:B]))
                    dve.wait_ge(stored[h], 16 * i + 16 * (h == 0))
                    for k in range(B):
                        before = run[h][:, k - 1, 0:S] if k else run[1 - h][:, B - 1, 0:S]
                        after()
                        step(nc.vector.scalar_tensor_tensor(run[h][:, k, 0:S], before, factor[h][:, B + k:B + k + 1], msg[h][:, k, :], ALU.mult, ALU.add))
                    step(nc.vector.tensor_copy(run[h][:, :, S], top[h][:, 1:1 + B]))
                    assert n[0] == per, n
            dve.wait_ge(stepped, INIT + per * 2 * IT)
            nc.vector.tensor_copy(final[:], run[1][:, B - 1, :]).then_inc(stepped, 1)


def complete_softmax(nc, sig, link, final, fix_at, running, ends, agg):
    S, W = C + 1, C + 2
    with ExitStack() as ctx:
        def sb(name, shape):
            return ctx.enter_context(nc.sbuf_tensor(name, shape, F32))

        fixed, diag, tops, weight_t, weight = sb("m_fixed", [P, W]), sb("m_diag", [P, P]), sb("m_tops", [P, P]), sb("m_weight_t", [P, P]), sb("m_weight", [P, P])
        top, neg, scale = sb("m_top", [P, 1]), sb("m_neg", [P, 1]), sb("m_scale", [P, 1])
        ps = ctx.enter_context(nc.psum_tensor("m_ps", [P, 512], F32))
        pt = ctx.enter_context(nc.psum_tensor("m_pt", [P, 512], F32))
        block = ctx.enter_context(nc.Block())
        fetched, pe_s, act_s, dve_s = sig["fetched"], sig["pe_step"], sig["act_step"], sig["dve_step"]

        @block.gpsimd
        def _(pool):
            pool.indirect_dma_start(out=fixed[:], out_offset=None, in_=running, in_offset=offsets(fix_at[:])).then_inc(fetched.sem, 16)
            pool.wait_ge(dve_s.sem, dve_s.base + 8)
            pool.indirect_dma_start(out=running, out_offset=offsets(fix_at[:]), in_=fixed[:], in_offset=None).then_inc(fetched.sem, 16)
            pool.wait_ge(fetched.sem, fetched.base + 32)
            for j in range(J):
                pool.indirect_dma_start(out=agg[:, j, :], out_offset=None, in_=running, in_offset=offsets(ends[:, j:j + 1])).then_inc(fetched.sem, 16)
            pool.wait_ge(fetched.sem, fetched.base + 32 + 16 * J)

        @block.tensor
        def _(pe):
            nc.tensor.transpose(pt[:, 0:P], link[:], sig["ident"][:]).then_inc(pe_s.sem, 1)
            pe.wait_ge(dve_s.sem, dve_s.base + 1)
            nc.tensor.matmul(ps[:, 0:P], sig["ones"][:], diag[:], start=True, stop=True).then_inc(pe_s.sem, 1)
            pe.wait_ge(act_s.sem, act_s.base + 1)
            nc.tensor.transpose(pt[:, P:2 * P], weight_t[:], sig["ident"][:]).then_inc(pe_s.sem, 1)
            pe.wait_ge(dve_s.sem, dve_s.base + 7)
            nc.tensor.matmul(ps[:, P:P + S], weight[:], final[:, 0:S], start=True, stop=True).then_inc(pe_s.sem, 1)

        @block.scalar
        def _(act):
            act.wait_ge(dve_s.sem, dve_s.base + 6)
            nc.scalar.activation(weight_t[:], tops[:], ACT.Exp, bias=neg[:]).then_inc(act_s.sem, 1)
            nc.scalar.activation(scale[:], fixed[:, S:W], ACT.Exp, bias=neg[:]).then_inc(act_s.sem, 1)

        @block.vector
        def _(dve):
            step = Chain(dve, dve_s.sem, dve_s.base)
            step(nc.vector.tensor_scalar(diag[:], sig["ident"][:], final[:, S:W], None, ALU.mult))
            dve.wait_ge(pe_s.sem, pe_s.base + 2)
            step(nc.vector.tensor_scalar(tops[:], pt[:, 0:P], BIG, -BIG, ALU.mult, ALU.add))
            step(nc.vector.tensor_tensor(tops[:], tops[:], ps[:, 0:P], ALU.add))
            step(nc.vector.tensor_reduce(top[:], tops[:], AX.X, ALU.max))
            dve.wait_ge(fetched.sem, fetched.base + 16)
            step(nc.vector.tensor_tensor(top[:], top[:], fixed[:, S:W], ALU.max))
            step(nc.vector.tensor_scalar(neg[:], top[:], -1.0, None, ALU.mult))
            dve.wait_ge(pe_s.sem, pe_s.base + 3)
            step(nc.vector.tensor_copy(weight[:], pt[:, P:2 * P]))
            dve.wait_ge(pe_s.sem, pe_s.base + 4)
            dve.wait_ge(act_s.sem, act_s.base + 2)
            step(nc.vector.scalar_tensor_tensor(fixed[:, 0:S], fixed[:, 0:S], scale[:], ps[:, P:P + S], ALU.mult, ALU.add))

        fetched.base += 32 + 16 * J
        pe_s.base += 4
        act_s.base += 2
        dve_s.base += 8


def on_vector(nc, sig, body, block=None):
    with ExitStack() as ctx:
        block = block or ctx.enter_context(nc.Block())

        @block.vector
        def _(dve):
            step = Chain(dve, sig["dve_step"].sem, sig["dve_step"].base)
            body(step)
            sig["dve_step"].base = step.n


def moves(nc, sig, copies):
    with nc.Block() as block:
        moved = sig["moved"]

        @block.sync
        def _(sp):
            for to, of in copies:
                sp.dma_start(to, of).then_inc(moved.sem, 16)
            sp.wait_ge(moved.sem, moved.base + 16 * len(copies))

        moved.base += 16 * len(copies)


def gnn(nc, out, x, src, dst, u, ew, labels, label_rows, attrs, spline1, root1, bias01, spline2, root2, bias02,
        w_att, bias1, trans, trans_t, att, edge_att, agg_weights, gw1, gb1, gw2, gb2, gw3, gb3, lw, lb,
        wn, wn_t, we, we_t, att_src, att_dst, att_edge, stop=None):
    V = nc.vector
    with ExitStack() as ctx:
        def dram(name, shape):
            return nc.dram_tensor(name, shape, F32, kind="Internal").ap()

        def sb(name, shape, dt=F32, scope=ctx):
            return scope.enter_context(nc.sbuf_tensor(name, shape, dt))

        sig = {n: Signal(ctx.enter_context(nc.semaphore(n))) for n in
               ("copied", "turned", "turned_sb", "product", "saved", "fetched", "pe_step", "act_step", "dve_step", "pool_step", "moved", "rounds")}

        spline_table = dram("spline_table", [NP, 2 * C])
        att_table = dram("att_table", [NP, 2 * C + 1])
        gcn_table = [dram(f"gcn_table{k}", [NP, c]) for k, c in enumerate((16, 16, 32))]
        soft_table = dram("soft_table", [NP, C + 2])
        range_table = dram("range_table", [NP, 1])
        running = {w: dram(f"running{w}", [EP + 1, w]) for w in (C + 1, C, 16, 32, C + 2)}
        running_dst, running_src = dram("running_dst", [EP + 1, RUN]), dram("running_src", [EP + 1, RUN])
        begun_x, begun_s, sent = dram("begun_x", [EP, C]), dram("begun_s", [EP, 1]), dram("sent", [EP, SENT])

        def nodes(table):
            return table.rearrange("(p j) c -> p j c", p=P)

        def steps(rows):
            return rows.rearrange("(p t) c -> p t c", p=P)

        with nc.Block() as block:
            @block.sync
            def _(sp):
                for name in ("copied", "turned", "turned_sb", "product", "saved"):
                    sp.sem_inc(sig[name].sem, 2)
                    sig[name].base = 2

        for name in ("ident", "ones", "upper", "shift1", "shift2", "iota"):
            sig[name] = sb(name, [P, P])
        sig["ident_b"], sig["not_earlier"] = sb("ident_b", [P, P], BF16), sb("not_earlier", [P, P], BF16)
        chunk_row = sb("chunk_row", [P, 1])
        zeros = sb("zeros", [P, max(B, J - REST) * C])
        src_i = sb("src_i", [P, T + B], I32)
        keep = sb("keep", [P, T + B])
        ew_s = sb("ew_s", [P, T + B])
        rank = sb("rank", [P, T + B])
        src_lo, src_hi = (sb(n, [P, T + B], BF16) for n in ("src_lo", "src_hi"))
        first_dst, first_dst_f, last_dst_f, fix_dst = sb("first_dst", [P, 1], I32), sb("first_dst_f", [P, 1]), sb("last_dst_f", [P, 1]), sb("fix_dst", [P, 1], I32)
        link, step_pen, use_pen = sb("link", [P, P]), sb("step_pen", [P, P]), sb("use_pen", [P, P])
        xs = sb("xs", [P, J, C])
        y = sb("y", [P, J, C])
        final = sb("final", [P, 4 * C])
        cnt_dst, cnt_src, begin_dst, begin_src = (sb(n, [P, J]) for n in ("cnt_dst", "cnt_src", "begin_dst", "begin_src"))
        end_dst, first_at, end_src = (sb(n, [P, J], I32) for n in ("end_dst", "first_at", "end_src"))
        r_dst, r_src, ew_sum, dinv = (sb(n, [P, J]) for n in ("r_dst", "r_src", "ew_sum", "dinv"))

        l0 = ctx.enter_context(ExitStack())
        u_s = sb("u_s", [P, T + B], F32, l0)
        dst_lo, dst_hi = (sb(n, [P, T + B], BF16, l0) for n in ("dst_lo", "dst_hi"))
        w0 = [sb(f"w0_{k}", [C, 3 * C], F32, l0) for k in range(2)]
        b0 = [sb(f"b0_{k}", [P, C], F32, l0) for k in range(2)]

        with ExitStack() as tmp:
            dst_i, prev_i = sb("dst_i", [P, T], I32, tmp), sb("prev_i", [P, T], I32, tmp)
            dst_f, prev_f = sb("dst_f", [P, T], F32, tmp), sb("prev_f", [P, T], F32, tmp)
            many = sb("many", [P, 1], F32, tmp)
            blank_node = zeros[0:1, 0:(J - REST) * C]
            with nc.Block() as block:
                pool_s, moved, dve_s = sig["pool_step"], sig["moved"], sig["dve_step"]
                dst_flat = dst.rearrange("p t -> (p t)")

                @block.sync
                def _(sp):
                    sp.wait_ge(dve_s.sem, 1)
                    n = 0
                    for to, of in (
                        (src_i[:, 0:T], src), (dst_i[:], dst),
                        (prev_i[1:P, :], dst_flat[T - 1:EP - 1].rearrange("(p t) -> p t", t=T)), (prev_i[0:1, 1:T], dst[0:1, 0:T - 1]),
                        (ew_s[:, 0:T], ew), (u_s[:, 0:T], u),
                        (xs[0:LAST, :, :], x[0:LAST * J, :].rearrange("(p j) c -> p j c", j=J)),
                        (xs[LAST:LAST + 1, 0:REST, :], x[LAST * J:N, :].unsqueeze(0)),
                        (xs[LAST:LAST + 1, REST:J, :], blank_node.rearrange("p (j c) -> p j c", c=C)),
                        *((w0[k][:, n0 * C:(n0 + 1) * C], w) for k, ws in enumerate(((spline1[0], spline1[1], root1), (spline2[0], spline2[1], root2)))
                          for n0, w in enumerate(ws)),
                        *((b0[k][:], b.broadcast_to([P, C])) for k, b in enumerate((bias01, bias02))),
                    ):
                        sp.dma_start(to, of).then_inc(moved.sem, 16)
                        n += 1
                    sp.wait_ge(moved.sem, 16 * n)
                    moved.base += 16 * n

                @block.gpsimd
                def _(pool):
                    step = Chain(pool, pool_s.sem)
                    step(pool.iota(sig["iota"][:], [[1, P]], base=0, channel_multiplier=0, allow_small_or_imprecise_dtypes=True))
                    step(pool.iota(chunk_row[:], [[0, 1]], base=-1, channel_multiplier=T, allow_small_or_imprecise_dtypes=True))
                    step(pool.memset(sig["ones"][:], 1.0))
                    for name in ("ident", "shift1", "shift2", "ident_b", "not_earlier"):
                        step(pool.memset(sig[name][:], 0.0))

                    def select(name, of, op, base, fill):
                        step(pool.affine_select(out=sig[name][:], in_=sig[of][:], compare_op=op, fill=fill, base=base, pattern=[[1, P]], channel_multiplier=-1))

                    select("ident", "ident", ALU.not_equal, 0, 1.0)
                    select("ident_b", "ident_b", ALU.not_equal, 0, 1.0)
                    select("shift1", "shift1", ALU.not_equal, -1, 1.0)
                    select("shift2", "shift2", ALU.not_equal, -2, 1.0)
                    select("upper", "ones", ALU.is_gt, 0, 0.0)
                    select("not_earlier", "not_earlier", ALU.is_gt, 0, -1.0)

                @block.vector
                def _(dve):
                    step = Chain(dve, dve_s.sem)
                    step(V.memset(zeros[:], 0.0))
                    step(V.memset(prev_i[0:1, 0:1], -1))
                    step(V.memset(cnt_src[:], 0.0))
                    for t in (src_i, keep, ew_s, rank, u_s, dst_lo, dst_hi, src_lo, src_hi):
                        step(V.memset(t[:, T:T + B], 0))
                    dve.wait_ge(moved.sem, 16 * 17)
                    step(V.tensor_copy(dst_f[:], dst_i[:]))
                    step(V.tensor_copy(prev_f[:], prev_i[:]))
                    step(V.tensor_tensor(keep[:, 0:T], dst_f[:], prev_f[:], ALU.is_equal))
                    step(V.tensor_copy(first_dst[:], dst_i[:, 0:1]))
                    step(V.tensor_copy(first_dst_f[:], dst_f[:, 0:1]))
                    step(V.tensor_copy(last_dst_f[:], dst_f[:, T - 1:T]))
                    step(V.tensor_scalar(prev_f[:], dst_f[:], first_dst_f[:], None, ALU.is_equal))
                    step(V.tensor_reduce(many[:], prev_f[:], AX.X, ALU.add))
                    dve.wait_ge(pool_s.sem, 2)
                    step(V.tensor_tensor(fix_dst[:], many[:], chunk_row[:], ALU.add))

                    def split(key, lo, lo_b, hi):
                        step(V.tensor_scalar(lo, key, -float(J // 2), 1.0 / J, ALU.add, ALU.mult))
                        step(V.tensor_scalar(lo, lo, ROUND, None, ALU.add))
                        step(V.tensor_scalar(lo, lo, -ROUND, None, ALU.add))
                        step(V.scalar_tensor_tensor(hi, lo, -float(J), key, ALU.mult, ALU.add))
                        step(V.tensor_copy(lo_b, lo))

                    split(dst_f[:], prev_f[:], dst_lo[:, 0:T], dst_hi[:, 0:T])
                    step(V.tensor_copy(prev_f[:], src_i[:, 0:T]))
                    split(prev_f[:], dst_f[:], src_lo[:, 0:T], src_hi[:, 0:T])
                    for k in range(2):
                        step(V.tensor_tensor(w0[k][:, C:2 * C], w0[k][:, C:2 * C], w0[k][:, 0:C], ALU.subtract))
                    dve_s.base = step.n

        carry_masks(nc, sig, first_dst_f[:], last_dst_f[:], link, step_pen, use_pen)
        carries = (link, step_pen, use_pen)

        with ExitStack() as tmp:
            d, own = sb("d", [P, J, 2 * C], F32, tmp), sb("own", [P, J, C], F32, tmp)
            h = sb("h0", [P, J, C], F32, tmp)
            for k in range(2):
                width = C + 1 if k == 0 else C
                node_rows = xs if k == 0 else h
                dense(nc, sig, [node_rows], [w0[k][:, 0:2 * C]], d, 2 * C, nodes(spline_table))
                edge = {"src": src_i, "keep": keep, "weight": u_s, "src_lo": src_lo, "src_hi": src_hi, "rank": rank, "seen": cnt_src, "ranked": k * RANKED}
                if k == 0:
                    edge |= {"extra": ew_s, "dst_lo": dst_lo, "dst_hi": dst_hi, "count": cnt_dst}
                spline_pass(nc, sig, spline_table, width, edge, running[width], final, zeros,
                              cleared=() if k == 0 else (steps(begun_x), steps(begun_s)))
                if k == 0:
                    node_ranges(nc, sig, cnt_dst, begin_dst, end_dst, first_at)
                else:
                    node_ranges(nc, sig, cnt_src, begin_src, end_src, None)
                agg_scope = tmp.enter_context(ExitStack())
                agg_k = sb(f"agg0_{k}", [P, J, width], F32, agg_scope)
                complete_and_fetch(nc, sig, carries, final, width, width, fix_dst, running[width], end_dst, agg_k,
                                   beside=lambda block, _: dense(nc, sig, [node_rows], [w0[k][:, 2 * C:3 * C]], own, C, bias=b0[k][:], block=block))

                def mean_and_own(step):
                    if k == 0:
                        step(V.tensor_scalar(r_dst[:], cnt_dst[:], 1.0, None, ALU.max))
                        step(V.reciprocal(r_dst[:], r_dst[:]))
                        step(V.tensor_copy(ew_sum[:], agg_k[:, :, C]))
                    to = h if k == 0 else y
                    step(V.tensor_tensor(to[:], agg_k[:, :, 0:C], spread(r_dst[:], C), ALU.mult))
                    step(V.tensor_tensor(to[:], to[:], own[:], ALU.add))

                on_vector(nc, sig, mean_and_own)
                agg_scope.close()
            layer_norm(nc, sig, xs, y, xs)
        l0.close()

        def finish():
            moves(nc, sig, [(out[0:LAST * J, :].rearrange("(p j) c -> p j c", j=J), xs[0:LAST, :, :]),
                            (out[LAST * J:N, :].unsqueeze(0), xs[LAST:LAST + 1, 0:REST, :])])

        if stop == 0:
            return finish()

        with ExitStack() as tmp:
            w_src, w_dst, b1 = sb("w_src", [P, C], F32, tmp), sb("w_dst", [P, C], F32, tmp), sb("b1", [P, C], F32, tmp)
            w_ef, w_lab, twt = sb("w_ef", [C, 2, C], F32, tmp), sb("w_lab", [2 * LABELS, C], F32, tmp), sb("twt", [C, 3 * LABELS], F32, tmp)
            tw, ea, tw_att = sb("tw", [LABELS, C], F32, tmp), sb("ea", [C, 1], F32, tmp), sb("tw_att", [LABELS, 1], F32, tmp)
            w_labels = sb("w_labels", [B * LABELS, B, C], F32, tmp)
            att_b, mix = sb("att_b", [P, C], F32, tmp), sb("mix", [P, 3], F32, tmp)
            mix_sum = sb("mix_sum", [P, 1], F32, tmp)
            share = sb("share", [P, J], F32, tmp)
            first_rows = sb("first_rows", [P, 2 * C + 1], F32, tmp)
            on_vector(nc, sig, lambda step: step(V.memset(w_labels[:], 0.0)))
            moves(nc, sig, [(w_src[:], w_att[0:2 * C, :]), (w_dst[:], w_att[2 * C:4 * C, :]), (w_ef[:, 0, :], w_att[C:2 * C, :]), (w_ef[:, 1, :], w_att[3 * C:4 * C, :]),
                            (b1[:], bias1.broadcast_to([P, C])), (tw[:], trans), (twt[:, 0:LABELS], trans_t), (twt[:, LABELS:2 * LABELS], zeros[0:C, 0:LABELS]),
                            (twt[:, 2 * LABELS:3 * LABELS], trans_t), (ea[:], edge_att),
                            (att_b[:], att.broadcast_to([P, C])), (mix[:], agg_weights.broadcast_to([P, 3])),
                            *((w_labels[k * LABELS:(k + 1) * LABELS, k, :], trans) for k in range(B))])
            with ExitStack() as rows:
                t1 = sb("t1", [P, J, 2 * C + 1], F32, rows)

                def table_rows(step):
                    step(V.tensor_tensor(t1[:, :, 0:C], xs[:], repeat(att_b[:], J), ALU.mult))
                    step(V.tensor_copy(t1[:, :, C:2 * C], xs[:]))
                    step(V.tensor_copy(t1[:, :, 2 * C], begin_src[:]))
                    step(V.tensor_reduce(mix_sum[:], mix[:], AX.X, ALU.max))
                    step(V.tensor_scalar(mix[:], mix[:], mix_sum[:], None, ALU.subtract))
                    step(V.tensor_copy(begin_dst[:], end_src[:]))
                    step(V.tensor_scalar(r_src[:], cnt_src[:], 1.0, None, ALU.max))
                    step(V.reciprocal(r_src[:], r_src[:]))

                on_vector(nc, sig, table_rows)
                with ExitStack() as c2:
                    ps = c2.enter_context(nc.psum_tensor("p_label_att", [P, 512], F32))
                    block = c2.enter_context(nc.Block())
                    act_s, pe_s, dve_s = sig["act_step"], sig["pe_step"], sig["dve_step"]

                    @block.scalar
                    def _(act):
                        nc.scalar.activation(mix[:], mix[:], ACT.Exp).then_inc(act_s.sem, 1)

                    @block.tensor
                    def _(pe):
                        nc.tensor.matmul(ps[0:LABELS, 0:1], twt[:, 0:LABELS], ea[:], start=True, stop=True).then_inc(pe_s.sem, 1)
                        nc.tensor.matmul(ps[0:2 * LABELS, C:2 * C], twt[:, 0:2 * LABELS], w_ef[:, 0, :], start=True, stop=False)
                        nc.tensor.matmul(ps[0:2 * LABELS, C:2 * C], twt[:, LABELS:3 * LABELS], w_ef[:, 1, :], start=False, stop=True).then_inc(pe_s.sem, 1)

                    @block.vector
                    def _(dve):
                        step = Chain(dve, dve_s.sem, dve_s.base)
                        dve.wait_ge(pe_s.sem, pe_s.base + 2)
                        step(V.tensor_copy(tw_att[:], ps[0:LABELS, 0:1]))
                        step(V.tensor_copy(w_lab[:], ps[0:2 * LABELS, C:2 * C]))
                        dve.wait_ge(act_s.sem, act_s.base + 1)
                        step(V.tensor_reduce(mix_sum[:], mix[:], AX.X, ALU.add))
                        step(V.reciprocal(mix_sum[:], mix_sum[:]))
                        step(V.tensor_scalar(mix[:], mix[:], mix_sum[:], None, ALU.mult))
                        dve_s.base = step.n

                    act_s.base += 1
                    pe_s.base += 2
                moves(nc, sig, [(nodes(att_table), t1[:]), (nodes(range_table), begin_dst[:].unsqueeze(2))])
            spread_to_edges(nc, sig, xs, first_at, begun_x, att_table, first_dst[:], first_rows)
            attention_pass(nc, sig, att_table, {"src": src_i, "keep": keep, "rank": rank}, labels, label_rows, begun_x, first_rows, tw[:], tw_att[:],
                           running_dst, final[:, 0:RUN], sent, zeros)

            def combine(agg, side, x0, lab0, cnt_r, to, block=None):
                def body(step):
                    step(V.tensor_scalar(share[:], cnt_r[:], mix[:, 0:1], mix[:, 2:3], ALU.mult, ALU.add))
                    step(V.tensor_tensor(to[:, :, 0:C], agg[:, :, x0:x0 + C], spread(share[:], C), ALU.mult))
                    step(V.scalar_tensor_tensor(to[:, :, 0:C], agg[:, :, SUMS:SUMS + C], mix[:, 1:2], to[:, :, 0:C], ALU.mult, ALU.add))
                    step(V.tensor_scalar(to[:, :, C:2 * C], agg[:, :, SUMS + C:RUN], mix[:, 1:2], None, ALU.mult))
                    step(V.tensor_tensor(comb_lab[:, :, side * LABELS:(side + 1) * LABELS], agg[:, :, lab0:lab0 + LABELS], spread(share[:], LABELS), ALU.mult))

                on_vector(nc, sig, body, block)

            SUMS = C + LABELS
            agg_dst = sb("agg_dst", [P, J, RUN], F32, tmp)
            ends = sb("ends", [P, 4], F32, tmp)
            complete_and_fetch(nc, sig, carries, final, SUMS, RUN, fix_dst, running_dst, end_dst, agg_dst,
                               beside=lambda block, scope: source_pass(nc, sig, block, scope, sent, w_labels, running_src, final, ends, zeros))
            first_src, fix_src, end_first = sb("first_src", [P, 1], I32, tmp), sb("fix_src", [P, 1], I32, tmp), sb("end_first", [P, 1], F32, tmp)
            link_s, step_pen_s, use_pen_s = sb("link_s", [P, P], F32, tmp), sb("step_pen_s", [P, P], F32, tmp), sb("use_pen_s", [P, P], F32, tmp)
            carry_masks(nc, sig, ends[:, 0:1], ends[:, 2:3], link_s, step_pen_s, use_pen_s)
            chunk_end = sb("chunk_end", [P, 1], F32, tmp)
            with nc.Block() as block:
                fetched, dve_s = sig["fetched"], sig["dve_step"]

                @block.gpsimd
                def _(pool):
                    pool.wait_ge(dve_s.sem, dve_s.base + 1)
                    pool.indirect_dma_start(out=end_first[:], out_offset=None, in_=range_table, in_offset=offsets(first_src[:])).then_inc(fetched.sem, 16)

                @block.vector
                def _(dve):
                    step = Chain(dve, dve_s.sem, dve_s.base)
                    step(V.tensor_copy(first_src[:], ends[:, 0:1]))
                    step(V.tensor_scalar(chunk_end[:], chunk_row[:], float(T), None, ALU.add))
                    dve.wait_ge(fetched.sem, fetched.base + 16)
                    step(V.tensor_tensor(fix_src[:], end_first[:], chunk_end[:], ALU.min))
                    dve_s.base = step.n

                fetched.base += 16
            comb_dst, comb_lab = sb("comb_dst", [P, J, 2 * C], F32, tmp), sb("comb_lab", [P, J, 2 * LABELS], F32, tmp)
            with ExitStack() as rows:
                agg_src = sb("agg_src", [P, J, RUN], F32, rows)
                complete_and_fetch(nc, sig, (link_s, step_pen_s, use_pen_s), final, SUMS, RUN, fix_src, running_src, end_src, agg_src,
                                   beside=lambda block, _: combine(agg_dst, 1, LABELS, 0, r_dst, comb_dst, block))
                comb_src = agg_dst[:, :, 0:2 * C]
                combine(agg_src, 0, 0, C, r_src, comb_src)
            dense(nc, sig, [comb_src, comb_dst, comb_lab], [w_src[:], w_dst[:], w_lab[:]], y, C, bias=b1[:])
            layer_norm(nc, sig, xs, y, xs)
        if stop == 1:
            return finish()

        with ExitStack() as tmp:
            widths = (16, 16, 32)
            w1, w2, w3 = sb("gw1s", [C, 16], F32, tmp), sb("gw2s", [16, 32], F32, tmp), sb("gw3s", [32, C], F32, tmp)
            gb = [sb(f"gb{k}", [P, c], F32, tmp) for k, c in enumerate((16, 32, C))]
            lws = [sb(f"lws{k}", [C, C], F32, tmp) for k in range(2)]
            lbs = sb("lbs", [P, C], F32, tmp)
            t = [sb(f"gt{k}", [P, J, c], F32, tmp) for k, c in enumerate(widths)]
            agg = [sb(f"gagg{k}", [P, J, c], F32, tmp) for k, c in enumerate(widths)]
            x2, x3, x4 = sb("x2", [P, J, 16], F32, tmp), sb("x3", [P, J, 32], F32, tmp), sb("x4", [P, J, C], F32, tmp)
            moves(nc, sig, [(w1[:], gw1), (w2[:], gw2), (w3[:], gw3), (gb[0][:], gb1.broadcast_to([P, 16])), (gb[1][:], gb2.broadcast_to([P, 32])),
                            (gb[2][:], gb3.broadcast_to([P, C])), (lws[0][:], lw[0:C, :]), (lws[1][:], lw[C:2 * C, :]), (lbs[:], lb.broadcast_to([P, C]))])
            some = sb("some", [P, J], F32, tmp)

            def degrees(step):
                step(V.tensor_scalar(ew_sum[:], ew_sum[:], 1.0, None, ALU.add))
                step(V.tensor_scalar(some[:], ew_sum[:], 0.0, None, ALU.is_gt))
                step(V.tensor_scalar(ew_sum[:], ew_sum[:], 1.0e-30, None, ALU.max))

            on_vector(nc, sig, degrees)
            with nc.Block() as block:
                act_s, dve_s = sig["act_step"], sig["dve_step"]

                @block.scalar
                def _(act):
                    nc.scalar.activation(dinv[:], ew_sum[:], ACT.Sqrt).then_inc(act_s.sem, 1)

                @block.vector
                def _(dve):
                    step = Chain(dve, dve_s.sem, dve_s.base)
                    dve.wait_ge(act_s.sem, act_s.base + 1)
                    step(V.reciprocal(dinv[:], dinv[:]))
                    step(V.tensor_tensor(dinv[:], dinv[:], some[:], ALU.mult))
                    dve_s.base = step.n

                act_s.base += 1

            def convolve(k):
                c = widths[k]
                moves(nc, sig, [(nodes(gcn_table[k]), t[k][:])])
                with ExitStack() as split:
                    parts = [sb(f"part{k}_{n}", [P, c // SLICE, J, SLICE], BF16, split) for n in range(3)]
                    split_rows(nc, sig, t[k], c, parts)
                    edge = {"src": src_i, "src_lo": src_lo, "src_hi": src_hi, "keep": keep, "weight": ew_s}
                    graph_pass(nc, sig, gcn_table[k], c, edge, parts, running[c], final, zeros)
                complete_and_fetch(nc, sig, carries, final, c, c, fix_dst, running[c], end_dst, agg[k])

                def body(step):
                    step(V.tensor_tensor(agg[k][:], agg[k][:], t[k][:], ALU.add))
                    step(V.tensor_tensor(agg[k][:], agg[k][:], spread(dinv[:], c), ALU.mult))

                on_vector(nc, sig, body)

            def relu(step, h):
                step(V.tensor_scalar(flat(h[:]), flat(h[:]), 0.0, None, ALU.max))

            def scaled(step, to, h, c):
                step(V.tensor_tensor(to[:], h[:], spread(dinv[:], c), ALU.mult))

            dense(nc, sig, [xs], [w1[:]], x2, 16)
            on_vector(nc, sig, lambda step: scaled(step, t[0], x2, 16))
            convolve(0)
            on_vector(nc, sig, lambda step: (step(V.tensor_tensor(agg[0][:], agg[0][:], repeat(gb[0][:], J), ALU.add)), relu(step, agg[0]), scaled(step, t[1], agg[0], 16)))
            convolve(1)
            dense(nc, sig, [agg[1]], [w2[:]], x3, 32, bias=gb[1][:])
            on_vector(nc, sig, lambda step: (relu(step, x3), scaled(step, t[2], x3, 32)))
            convolve(2)
            dense(nc, sig, [agg[2]], [w3[:]], x4, C, bias=gb[2][:])
            on_vector(nc, sig, lambda step: relu(step, x4))
            dense(nc, sig, [xs, x4], [lws[0][:], lws[1][:]], y, C, bias=lbs[:])
            layer_norm(nc, sig, xs, y, xs)
        if stop == 2:
            return finish()

        with ExitStack() as tmp:
            wns, wnt, a_cols = sb("wns", [C, C + 2], F32, tmp), sb("wnt", [C, C], F32, tmp), sb("a_cols", [C, 2], F32, tmp)
            wes, wet, ae, w_edge_att = sb("wes", [EDIM, C], F32, tmp), sb("wet", [C, EDIM], F32, tmp), sb("ae", [C, 1], F32, tmp), sb("w_edge_att", [EDIM, 1], F32, tmp)
            t3, s_dst = sb("t3", [P, J, C + 2], F32, tmp), sb("s_dst", [P, J, 1], F32, tmp)
            first_rows = sb("first_rows3", [P, C + 2], F32, tmp)
            at_dst, begun = sb("at_dst", [P, T + B], F32, tmp), sb("begun3", [P, T], F32, tmp)
            moves(nc, sig, [(wns[:, 0:C], wn), (wnt[:], wn_t), (wes[:], we), (wet[:], we_t), (ae[:], att_edge), (a_cols[:, 0:1], att_src), (a_cols[:, 1:2], att_dst)])

            with ExitStack() as c2:
                ps = c2.enter_context(nc.psum_tensor("p_edge_att", [P, 512], F32))
                block = c2.enter_context(nc.Block())
                pe_s, dve_s = sig["pe_step"], sig["dve_step"]

                @block.tensor
                def _(pe):
                    nc.tensor.matmul(ps[0:EDIM, 0:1], wet[:], ae[:], start=True, stop=True).then_inc(pe_s.sem, 1)
                    nc.tensor.matmul(ps[0:C, 1:3], wnt[:], a_cols[:], start=True, stop=True).then_inc(pe_s.sem, 1)

                @block.vector
                def _(dve):
                    step = Chain(dve, dve_s.sem, dve_s.base)
                    dve.wait_ge(pe_s.sem, pe_s.base + 2)
                    step(V.tensor_copy(w_edge_att[:], ps[0:EDIM, 0:1]))
                    step(V.tensor_copy(wns[:, C:C + 2], ps[0:C, 1:3]))
                    dve_s.base = step.n

                pe_s.base += 2
            dense(nc, sig, [xs], [wns[:]], t3, C + 2, nodes(soft_table))
            on_vector(nc, sig, lambda step: step(V.tensor_copy(s_dst[:, :, 0], t3[:, :, C + 1])))
            spread_to_edges(nc, sig, s_dst, first_at, begun_s, soft_table, first_dst[:], first_rows)
            moves(nc, sig, [(begun[:], begun_s.rearrange("(p t) c -> p (t c)", p=P))])

            def held(step):
                step(V.memset(at_dst[:, T:T + B], 0.0))
                step(V.tensor_tensor_scan(at_dst[:, 0:T], keep[:, 0:T], begun[:], first_rows[:, C + 1:C + 2], ALU.mult, ALU.add))

            on_vector(nc, sig, held)
            softmax_pass(nc, sig, soft_table, {"src": src_i, "keep": keep, "at_dst": at_dst}, attrs, wes[:], w_edge_att[:], running[C + 2], final[:, 0:C + 2], zeros)
            agg = sb("agg3", [P, J, C + 2], F32, tmp)
            complete_softmax(nc, sig, link, final, fix_dst, running[C + 2], end_dst, agg)

            def normalised(step):
                step(V.tensor_scalar(r_src[:], agg[:, :, C], 1.0e-8, None, ALU.add))
                step(V.reciprocal(r_src[:], r_src[:]))
                step(V.tensor_tensor(y[:], agg[:, :, 0:C], spread(r_src[:], C), ALU.mult))
                step(V.tensor_tensor(flat(y[:]), flat(y[:]), flat(xs[:]), ALU.add))

            on_vector(nc, sig, normalised)
            layer_norm(nc, sig, xs, y, xs)
        finish()


def kernel(**inputs):
    import concourse.bacc as bacc
    from concourse.bass_utils import run_bass_kernel_spmd

    def chunks(name, fill):
        a = np.asarray(inputs[name]).reshape(E)
        return np.concatenate([a, np.full(EP - E, fill, a.dtype)]).reshape(P, T)

    def steps(name):
        a = np.asarray(inputs[name])
        a = np.concatenate([a, np.zeros((EP - E, a.shape[1]), a.dtype)])
        return np.ascontiguousarray(a.reshape(P, T, -1).transpose(2, 1, 0)).reshape(a.shape[1], T * P)

    def rows(name):
        a = np.asarray(inputs[name])
        return np.concatenate([a, np.zeros((EP - E, a.shape[1]), a.dtype)]).reshape(P, T, -1)

    def plain(name):
        return np.ascontiguousarray(inputs[name])

    def row(name):
        return plain(name).reshape(1, -1)

    def turned(name):
        return np.ascontiguousarray(np.asarray(inputs[name]).T)

    arrays = {
        "x": plain("x"), "src": chunks("src", NP - 1), "dst": chunks("dst", NP - 1),
        "u": chunks("edge_weight1", 0), "ew": chunks("edge_weight", 0),
        "labels": steps("edge_attr_8"), "label_rows": rows("edge_attr_8"), "attrs": steps("edge_attr_16"),
        "spline1": plain("L0_gnn_w1"), "root1": plain("L0_gnn_root1"), "bias01": row("L0_gnn_b1"),
        "spline2": plain("L0_gnn_w2"), "root2": plain("L0_gnn_root2"), "bias02": row("L0_gnn_b2"),
        "w_att": plain("L1_gnn_weight"), "bias1": row("L1_gnn_bias"), "trans": plain("L1_gnn_trans_weight"), "trans_t": turned("L1_gnn_trans_weight"),
        "att": row("L1_gnn_attention_weight"), "edge_att": plain("L1_gnn_edge_attention_weight"), "agg_weights": row("L1_gnn_agg_weights"),
        "gw1": plain("L2_gnn_w1"), "gb1": row("L2_gnn_b1"), "gw2": plain("L2_gnn_w2"), "gb2": row("L2_gnn_b2"),
        "gw3": plain("L2_gnn_w3"), "gb3": row("L2_gnn_b3"), "lw": plain("L2_gnn_lw"), "lb": row("L2_gnn_lb"),
        "wn": plain("L3_gnn_Wn"), "wn_t": turned("L3_gnn_Wn"), "we": plain("L3_gnn_We"), "we_t": turned("L3_gnn_We"),
        "att_src": plain("L3_gnn_att_src").reshape(C, 1), "att_dst": plain("L3_gnn_att_dst").reshape(C, 1), "att_edge": plain("L3_gnn_att_edge").reshape(C, 1),
    }
    nc = bacc.Bacc("TRN2", target_bir_lowering=False, num_devices=1)
    args = {n: nc.dram_tensor(f"in_{n}", a.shape, mybir.dt.from_np(a.dtype), kind="ExternalInput").ap() for n, a in arrays.items()}
    out = nc.dram_tensor("out", [N, C], F32, kind="ExternalOutput").ap()
    gnn(nc, out, **args)
    r = run_bass_kernel_spmd(nc, [{f"in_{n}": a for n, a in arrays.items()}], core_ids=[0])
    return r.results[0]["out"]
```

```python
from contextlib import ExitStack

import numpy as np

import concourse.bass as bass
from concourse import mybir
from concourse.alu_op_type import AluOpType as ALU

F32 = mybir.dt.float32
BF16 = mybir.dt.bfloat16
I32 = mybir.dt.int32
ACT = mybir.ActivationFunctionType
AX = mybir.AxisListType

P = 128
N = 6250
C = 64
E = 200000
J = -(-N // P)
NP = P * J
B = 16
T = -(-E // (P * 2 * B)) * 2 * B
EP = P * T
IT = T // (2 * B)
LAST = (N - 1) // J
REST = N - LAST * J
LABELS, EDIM = 8, 16
BIG = 1.0e30
ROUND = 12582912.0
GROUP = 4
PAIR = (0, 4, 8, 7)
PAIRS = GROUP * (GROUP + 1) // 2
RANKED = B // 2
SENT = 1 + C + LABELS
RUN = C + LABELS + 2 * C
SLICE = 16
GROUP_SLOTS = 7
PICKS = {16: 5, 32: 6}
CLASSES = 4
CLASS = -(-J // CLASSES)


class Chain:

    def __init__(self, eng, sem, base=0):
        self.eng, self.sem, self.n = eng, sem, base

    def __call__(self, ins):
        self.n += 1
        ins.then_inc(self.sem, 1)
        self.eng.wait_ge(self.sem, self.n)


class Signal:

    def __init__(self, sem):
        self.sem, self.base = sem, 0


def flat(ap):
    return ap.rearrange("p a b -> p (a b)")


def offsets(ap):
    return bass.IndirectOffsetOnAxis(ap=ap, axis=0)


def dense(nc, sig, xs, weights, out, width, store=None, bias=None, block=None, scope=None, prepare=None, ready=0):
    G = GROUP_SLOTS
    GROUPS = J // G
    with ExitStack() as ctx:
        ctx = scope or ctx
        uid = nc.next_id()
        K = len(xs)
        k_dims = [w.shape[0] for w in weights]

        def sb(name, shape):
            return [ctx.enter_context(nc.sbuf_tensor(f"{name}{uid}_{b}", shape, F32)) for b in range(2)]

        xin = [sb(f"xin{k}_", [P, G, d]) for k, d in enumerate(k_dims)]
        xt = [sb(f"xt{k}_", [d, G, P]) for k, d in enumerate(k_dims)]
        tp = [ctx.enter_context(nc.psum_tensor(f"tp{uid}_{k}", [P, 8, P], F32)) for k in range(K)]
        slot = next(s for s in (64, 128, 256) if width <= s)
        ACCS = 2 if 2 * K + slot // 32 <= 8 and block is None else 1
        acc = [ctx.enter_context(nc.psum_tensor(f"acc{uid}_{b}", [P, 8, slot], F32)) for b in range(ACCS)]
        block = block or ctx.enter_context(nc.Block())
        dve_s = sig["dve_step"]
        dve_base, prepared = dve_s.base, [0]
        copied, turned, turned_sb, product, saved, moved = (sig[n] for n in ("copied", "turned", "turned_sb", "product", "saved", "moved"))

        def each_group(eng, body):
            with eng.Fori(0, GROUPS // 2) as j:
                body(2 * j, 0)
                body(2 * j + 1, 1)
            body(GROUPS - 1, 0)

        @block.vector
        def _(dve):
            def copy_out(i, b):
                dve.wait_ge(turned.sem, turned.base + i + 1)
                dve.wait_ge(product.sem, product.base + i - 1)
                for k in range(K):
                    ins = nc.vector.tensor_copy(flat(xt[k][b][:]), flat(tp[k][0:k_dims[k], 0:G, :]))
                ins.then_inc(turned_sb.sem, 1)

            def add_bias(i, b):
                if bias is None:
                    return
                dve.wait_ge(product.sem, product.base + i + 1)
                rows = repeat(bias, G) if len(bias.shape) == 2 else bias[:, bass.ds(i * G, G), :]
                nc.vector.tensor_tensor(out[:, bass.ds(i * G, G), 0:width], acc[b % ACCS][:, 0:G, 0:width], rows, ALU.add).then_inc(saved.sem, 1)

            if prepare:
                step = Chain(dve, dve_s.sem, dve_base)
                for i in range(GROUPS):
                    prepare(dve, step, i, slice(i * G, (i + 1) * G))
                    prepared[0] = (step.n - dve_base) // (i + 1)
                    copy_out(i, i % 2)
                    if i:
                        add_bias(i - 1, (i - 1) % 2)
                add_bias(GROUPS - 1, 0)
                if bias is not None:
                    dve.wait_ge(saved.sem, saved.base + GROUPS)
                dve_s.base = step.n
                return
            copy_out(0, 0)
            with dve.Fori(0, GROUPS // 2) as j:
                for b in range(2):
                    copy_out(2 * j + b + 1, 1 - b)
                    add_bias(2 * j + b, b)
            add_bias(GROUPS - 1, 0)
            if bias is not None:
                dve.wait_ge(saved.sem, saved.base + GROUPS)

        @block.scalar
        def _(act):
            if ready:
                act.wait_ge(dve_s.sem, ready)

            def copy(i, b):
                act.wait_ge(turned.sem, turned.base + i - 1)
                if prepare:
                    act.wait_ge(dve_s.sem, dve_base + prepared[0] * (i + 1))
                for k in range(K):
                    ins = nc.scalar.activation(xin[k][b][:], xs[k][:, bass.ds(i * G, G), :], ACT.Copy)
                ins.then_inc(copied.sem, 1)

            def save(i, b):
                if bias is not None:
                    return
                act.wait_ge(product.sem, product.base + i + 1)
                nc.scalar.activation(out[:, bass.ds(i * G, G), 0:width], acc[b % ACCS][:, 0:G, 0:width], ACT.Copy).then_inc(saved.sem, 1)

            if prepare:
                copy(0, 0)
                with act.Fori(0, GROUPS // 2) as j:
                    for b in range(2):
                        copy(2 * j + b + 1, 1 - b)
                        save(2 * j + b, b)
                save(GROUPS - 1, 0)
                return
            copy(0, 0)
            copy(1, 1)
            with act.Fori(0, GROUPS // 2 - 1) as j:
                for b in range(2):
                    copy(2 * j + b + 2, b)
                    save(2 * j + b, b)
            copy(GROUPS - 1, 0)
            save(GROUPS - 3, 0)
            save(GROUPS - 2, 1)
            save(GROUPS - 1, 0)

        @block.tensor
        def _(pe):
            def turn(i, b):
                pe.wait_ge(copied.sem, copied.base + i + 1)
                pe.wait_ge(turned_sb.sem, turned_sb.base + i)
                pe.sem_inc(sig["rounds"].sem, 1)
                for k in range(K):
                    for g in range(G):
                        ins = nc.tensor.transpose(tp[k][0:k_dims[k], g, :], xin[k][b][:, g, :], sig["ident"][:])
                ins.then_inc(turned.sem, 1)

            def multiply(i, b):
                pe.wait_ge(turned_sb.sem, turned_sb.base + i + 1)
                pe.wait_ge(saved.sem, saved.base + i + 1 - ACCS)
                for g in range(G):
                    for k in range(K):
                        ins = nc.tensor.matmul(acc[b % ACCS][:, g, 0:width], xt[k][b][:, g, :], weights[k], start=(k == 0), stop=(k == K - 1))
                ins.then_inc(product.sem, 1)

            turn(0, 0)
            with pe.Fori(0, GROUPS // 2) as j:
                for b in range(2):
                    turn(2 * j + b + 1, 1 - b)
                    multiply(2 * j + b, b)
            multiply(GROUPS - 1, 0)

        if store is not None:
            @block.sync
            def _(sp):
                def send(i, b):
                    sp.wait_ge(saved.sem, saved.base + i + 1)
                    sp.dma_start(store[:, bass.ds(i * G, G), :], out[:, bass.ds(i * G, G), 0:store.shape[2]]).then_inc(moved.sem, 16)

                each_group(sp, send)
                sp.wait_ge(moved.sem, moved.base + 16 * GROUPS)

            moved.base += 16 * GROUPS

        for s in (copied, turned, turned_sb, product, saved):
            s.base += GROUPS


def complete_and_fetch(nc, sig, carries, final, n_sum, width, fix_at, running, ends, agg, beside=None, groups=()):
    link, step_pen, use_pen = carries
    n_max = width - n_sum
    with ExitStack() as ctx:
        uid = nc.next_id()
        fixed = ctx.enter_context(nc.sbuf_tensor(f"fixed{uid}", [P, width], F32))
        ps = ctx.enter_context(nc.psum_tensor(f"pcarry{uid}", [P, 512], F32))
        if n_max:
            pt = ctx.enter_context(nc.psum_tensor(f"pcarry_t{uid}", [P, 512], F32))
        run = ctx.enter_context(nc.sbuf_tensor(f"run{uid}", [P, P + 1], F32))
        block = ctx.enter_context(nc.Block())
        fetched, pe_s, dve_s = sig["fetched"], sig["pe_step"], sig["dve_step"]

        @block.gpsimd
        def _(pool):
            pool.indirect_dma_start(out=fixed[:], out_offset=None, in_=running, in_offset=offsets(fix_at[:])).then_inc(fetched.sem, 16)
            pool.wait_ge(dve_s.sem, dve_s.base + (5 if n_max else 1))
            pool.indirect_dma_start(out=running, out_offset=offsets(fix_at[:]), in_=fixed[:], in_offset=None).then_inc(fetched.sem, 16)
            pool.wait_ge(fetched.sem, fetched.base + 32)
            for j in range(J):
                pool.indirect_dma_start(out=agg[:, j, :], out_offset=None, in_=running, in_offset=offsets(ends[:, j:j + 1])).then_inc(
                    groups[j // GROUP_SLOTS].sem if groups else fetched.sem, 16)
            if groups:
                for group in groups:
                    pool.wait_ge(group.sem, group.base + 16 * GROUP_SLOTS)
            else:
                pool.wait_ge(fetched.sem, fetched.base + 32 + 16 * J)

        @block.tensor
        def _(pe):
            nc.tensor.matmul(ps[:, 0:n_sum], link[:], final[:, 0:n_sum], start=True, stop=True).then_inc(pe_s.sem, 1)
            if n_max:
                nc.tensor.transpose(pt[0:n_max, 0:P], final[:, n_sum:width], sig["ident"][:]).then_inc(pe_s.sem, 1)
                pe.wait_ge(dve_s.sem, dve_s.base + 4)
                nc.tensor.transpose(pt[:, P:P + n_max], run[0:n_max, 0:P], sig["ident"][0:n_max, 0:n_max]).then_inc(pe_s.sem, 1)

        @block.vector
        def _(dve):
            step = Chain(dve, dve_s.sem, dve_s.base)
            if n_max:
                dve.wait_ge(pe_s.sem, pe_s.base + 2)
                step(nc.vector.memset(run[0:n_max, 0:1], -BIG))
                step(nc.vector.tensor_tensor_scan(run[0:n_max, 1:P], step_pen[0:n_max, 1:P], pt[0:n_max, 0:P - 1], -BIG, ALU.add, ALU.max))
                step(nc.vector.tensor_tensor(run[0:n_max, 1:P], run[0:n_max, 1:P], use_pen[0:n_max, 1:P], ALU.add))
                step(nc.vector.tensor_scalar(run[0:n_max, 0:P], run[0:n_max, 0:P], -BIG, None, ALU.max))
                dve.wait_ge(pe_s.sem, pe_s.base + 3)
                dve.wait_ge(fetched.sem, fetched.base + 16)
                nc.vector.tensor_tensor(fixed[:, n_sum:width], fixed[:, n_sum:width], pt[:, P:P + n_max], ALU.max)
            dve.wait_ge(pe_s.sem, pe_s.base + 1)
            dve.wait_ge(fetched.sem, fetched.base + 16)
            step(nc.vector.tensor_tensor(fixed[:, 0:n_sum], fixed[:, 0:n_sum], ps[:, 0:n_sum], ALU.add))

        fetched.base += 32 + (0 if groups else 16 * J)
        for group in groups:
            group.base += 16 * GROUP_SLOTS
        pe_s.base += 3 if n_max else 1
        dve_s.base += 5 if n_max else 1
        if beside:
            beside(block, ctx)


def spread(ap, n):
    return ap.unsqueeze(2).broadcast_to([ap.shape[0], ap.shape[1], n])


def repeat(ap, n):
    return ap.unsqueeze(1).broadcast_to([ap.shape[0], n, ap.shape[1]])


def carry_masks(nc, sig, first, last, link, step_pen, use_pen, block=None, scope=None, ready=None):
    with ExitStack() as ctx:
        uid = nc.next_id()
        ctx = scope or ctx
        diag = ctx.enter_context(nc.sbuf_tensor(f"diag{uid}", [P, P], F32))
        near = ctx.enter_context(nc.sbuf_tensor(f"near{uid}", [P, 2 * P], F32))
        ps = ctx.enter_context(nc.psum_tensor(f"pmask{uid}", [P, 512], F32))
        block = block or ctx.enter_context(nc.Block())
        pe_s, dve_s = sig["pe_step"], sig["dve_step"]

        @block.tensor
        def _(pe):
            pe.wait_ge(dve_s.sem, dve_s.base + 1)
            nc.tensor.matmul(ps[:, 0:P], sig["ones"][:], diag[:], start=True, stop=True).then_inc(pe_s.sem, 1)
            pe.wait_ge(dve_s.sem, dve_s.base + 4)
            nc.tensor.matmul(ps[:, P:3 * P], sig["ones"][:], near[:], start=True, stop=True).then_inc(pe_s.sem, 1)

        @block.vector
        def _(dve):
            step = Chain(dve, dve_s.sem, dve_s.base)
            if ready:
                ready(dve)
            step(nc.vector.tensor_scalar(diag[:], sig["ident"][:], first, None, ALU.mult))
            dve.wait_ge(pe_s.sem, pe_s.base + 1)
            step(nc.vector.scalar_tensor_tensor(link[:], ps[:, 0:P], last, sig["upper"][:], ALU.is_equal, ALU.mult))
            step(nc.vector.tensor_tensor(near[:, 0:P], link[:], sig["shift2"][:], ALU.mult))
            step(nc.vector.tensor_tensor(near[:, P:2 * P], link[:], sig["shift1"][:], ALU.mult))
            dve.wait_ge(pe_s.sem, pe_s.base + 2)
            step(nc.vector.tensor_scalar(step_pen[:], ps[:, P:2 * P], BIG, -BIG, ALU.mult, ALU.add))
            step(nc.vector.tensor_scalar(use_pen[:], ps[:, 2 * P:3 * P], BIG, -BIG, ALU.mult, ALU.add))

        pe_s.base += 2
        dve_s.base += 6


def node_ranges(nc, sig, cnt, begin, end_row, begin_row, block=None, scope=None):
    with ExitStack() as ctx:
        uid = nc.next_id()
        ctx = scope or ctx
        upto = ctx.enter_context(nc.sbuf_tensor(f"upto{uid}", [P, J], F32))
        has = ctx.enter_context(nc.sbuf_tensor(f"has{uid}", [P, J], F32))
        tmp = ctx.enter_context(nc.sbuf_tensor(f"rtmp{uid}", [P, J], F32))
        ps = ctx.enter_context(nc.psum_tensor(f"pbefore{uid}", [P, 512], F32))
        block = block or ctx.enter_context(nc.Block())
        pe_s, dve_s = sig["pe_step"], sig["dve_step"]

        @block.tensor
        def _(pe):
            pe.wait_ge(dve_s.sem, dve_s.base + 1)
            nc.tensor.matmul(ps[:, 0:1], sig["upper"][:], upto[:, J - 1:J], start=True, stop=True).then_inc(pe_s.sem, 1)

        @block.vector
        def _(dve):
            step = Chain(dve, dve_s.sem, dve_s.base)
            step(nc.vector.tensor_tensor_scan(upto[:], sig["ones"][:, 0:J], cnt[:], 0.0, ALU.mult, ALU.add))
            dve.wait_ge(pe_s.sem, pe_s.base + 1)
            step(nc.vector.tensor_scalar(upto[:], upto[:], ps[:, 0:1], None, ALU.add))
            step(nc.vector.tensor_tensor(begin[:], upto[:], cnt[:], ALU.subtract))
            step(nc.vector.tensor_scalar(has[:], cnt[:], 0.0, None, ALU.is_gt))
            for ahead, rows, offset in ((upto, end_row, -1.0), (begin, begin_row, 0.0)):
                if rows is not None:
                    step(nc.vector.scalar_tensor_tensor(tmp[:], ahead[:], offset - EP, has[:], ALU.add, ALU.mult))
                    step(nc.vector.tensor_scalar(rows[:], tmp[:], float(EP), None, ALU.add))

        pe_s.base += 1
        dve_s.base += 4 + 2 * ((end_row is not None) + (begin_row is not None))


def layer_norm(nc, sig, y, out, block=None, scope=None, prepare=None):
    with ExitStack() as ctx:
        uid = nc.next_id()
        ctx = scope or ctx
        s = ctx.enter_context(nc.sbuf_tensor(f"lnsum{uid}", [P, J], F32))
        sq = ctx.enter_context(nc.sbuf_tensor(f"lnsq{uid}", [P, J, C], F32))
        std = ctx.enter_context(nc.sbuf_tensor(f"lnstd{uid}", [P, J], F32))
        block = block or ctx.enter_context(nc.Block())
        act_s, dve_s = sig["act_step"], sig["dve_step"]
        cuts = [slice(g, g + GROUP_SLOTS) for g in range(0, J, GROUP_SLOTS)] if prepare else [slice(0, J)]
        variances = []

        @block.vector
        def _(dve):
            step = Chain(dve, dve_s.sem, dve_s.base)
            for g, cut in enumerate(cuts):
                if prepare:
                    prepare(dve, step, g, cut)
                step(nc.vector.tensor_reduce(s[:, cut], y[:, cut, :], AX.X, ALU.add))
                step(nc.vector.tensor_scalar(s[:, cut], s[:, cut], 1.0 / C, None, ALU.mult))
                step(nc.vector.tensor_tensor(y[:, cut, :], y[:, cut, :], spread(s[:, cut], C), ALU.subtract))
                step(nc.vector.tensor_tensor(sq[:, cut, :], y[:, cut, :], y[:, cut, :], ALU.mult))
                step(nc.vector.tensor_reduce(s[:, cut], sq[:, cut, :], AX.X, ALU.add))
                step(nc.vector.tensor_scalar(s[:, cut], s[:, cut], 1.0 / C, 1e-5, ALU.mult, ALU.add))
                variances.append(step.n)
                dve.wait_ge(act_s.sem, act_s.base + g + 1)
                step(nc.vector.reciprocal(s[:, cut], std[:, cut]))
                step(nc.vector.tensor_tensor(out[:, cut, :], y[:, cut, :], spread(s[:, cut], C), ALU.mult))
            dve_s.base = step.n

        @block.scalar
        def _(act):
            for cut, made in zip(cuts, variances):
                act.wait_ge(dve_s.sem, made)
                nc.scalar.activation(std[:, cut], s[:, cut], ACT.Sqrt).then_inc(act_s.sem, 1)

        act_s.base += len(cuts)


def spline_pass(nc, sig, table, width, edge, running, final, zeros, cleared=()):
    count, ranked, extra = "count" in edge, edge.get("ranked"), "extra" in edge
    rank = ranked is not None
    per = 2 + B + 2 * count + 4 * rank
    with ExitStack() as ctx:
        uid = nc.next_id()

        def sb(name, shape, dt=F32):
            return ctx.enter_context(nc.sbuf_tensor(f"{name}{uid}", shape, dt))

        def pair(name, shape, dt=F32):
            return [sb(f"{name}{h}_", shape, dt) for h in range(2)]

        def sem(name):
            return ctx.enter_context(nc.semaphore(f"{name}{uid}"))

        index = pair("index", [P, B], I32)
        weight = pair("weight", [P, B])
        keep = pair("keep", [P, B])
        rows = pair("rows", [P, B, 2 * C])
        msg = pair("msg", [P, B, width])
        run = pair("run", [P, B, width])
        gathered = [sem(f"gathered{h}_") for h in range(2)]
        stored = [sem(f"stored{h}_") for h in range(2)]
        staged, indexed = ([sem(f"{n}{h}_") for h in range(2)] for n in ("staged", "indexed"))
        stepped = sem("stepped")
        if count:
            dst_lo, dst_hi = pair("dst_lo", [P, B]), pair("dst_hi", [P, B])
            at_lo, at_hi = pair("at_lo", [P, B, P], BF16), pair("at_hi", [P, B, J], BF16)
            blank = sb("blank", [P, P], BF16)
            p_count = ctx.enter_context(nc.psum_tensor(f"p_count{uid}", [P, 512], F32))
            counted = sem("counted")
        if rank:
            lo, hi = pair("lo", [P, RANKED]), pair("hi", [P, RANKED])
            one_lo, one_hi = pair("one_lo", [P, RANKED, P], BF16), pair("one_hi", [P, RANKED, J], BF16)
            lo_t, lo_tf = pair("lo_t", [P, GROUP, P], BF16), pair("lo_tf", [P, GROUP, P])
            earlier = pair("earlier", [P, PAIRS, P], BF16)
            seen = pair("seen", [P, J])
            picked = sb("picked", [P, RANKED, J])
            p_seen = ctx.enter_context(nc.psum_tensor(f"p_seen{uid}", [P, 512], F32))
            p_turn = ctx.enter_context(nc.psum_tensor(f"p_turn{uid}", [P, 8, P], BF16))
            p_same = ctx.enter_context(nc.psum_tensor(f"p_same{uid}", [P, 12, P], F32))
            p_look = ctx.enter_context(nc.psum_tensor(f"p_look{uid}", [P, RANKED, C], F32))
            turned, turned_sb, same, same_sb, summed, seen_sb, looked = (sem(n) for n in ("turned", "turned_sb", "same", "same_sb", "summed", "seen_sb", "looked"))
        block = ctx.enter_context(nc.Block())
        running_v = running[0:EP, :].rearrange("(p t) c -> p t c", p=P)
        INIT = per
        Q = RANKED // GROUP

        @block.sync
        def _(sp):
            for h, cut in enumerate((slice(0, C // 2), slice(C // 2, width))):
                sp.dma_start(running[EP:EP + 1, cut], zeros[0:1, cut]).then_inc(stored[h], 16)
            with sp.Fori(0, IT) as i:
                for h in range(2):
                    sp.wait_ge(stepped, INIT + per * (2 * i + h + 1))
                    sp.dma_start(running_v[:, bass.ds((2 * i + h) * B, B), :], run[h][:]).then_inc(stored[h], 16)
                    for dst in cleared:
                        sp.dma_start(dst[:, bass.ds((2 * i + h) * B, B), :], zeros[:, 0:B * dst.shape[2]].rearrange("p (t c) -> p t c", t=B)).then_inc(stored[h], 16)
            for h in range(2):
                sp.wait_ge(stored[h], 16 * IT * (1 + len(cleared)) + 16)

        @block.gpsimd
        def _(pool):
            with pool.Fori(0, IT) as i:
                for h in range(2):
                    pool.wait_ge(indexed[h], i + 1)
                    pool.sem_inc(sig["rounds"].sem, 1)
                    for k in range(B):
                        pool.indirect_dma_start(out=rows[h][:, k, :], out_offset=None, in_=table,
                                                in_offset=offsets(index[h][:, k:k + 1])).then_inc(gathered[h], 16)

        @block.scalar
        def _(act):
            def stage(h, at):
                nc.scalar.activation(weight[h][:], edge["weight"][:, bass.ds(at, B)], ACT.Copy)
                if extra:
                    nc.scalar.activation(msg[h][:, :, C], edge["extra"][:, bass.ds(at, B)], ACT.Copy)
                if count:
                    nc.scalar.activation(dst_lo[h][:], edge["dst_lo"][:, bass.ds(at, B)], ACT.Copy)
                    nc.scalar.activation(dst_hi[h][:], edge["dst_hi"][:, bass.ds(at, B)], ACT.Copy)
                if rank:
                    nc.scalar.activation(lo[h][:], edge["src_lo"][:, bass.ds(at + ranked, RANKED)], ACT.Copy)
                    nc.scalar.activation(hi[h][:], edge["src_hi"][:, bass.ds(at + ranked, RANKED)], ACT.Copy)
                nc.scalar.activation(keep[h][:], edge["keep"][:, bass.ds(at, B)], ACT.Copy).then_inc(staged[h], 1)

            def stage_index(h, at):
                nc.scalar.copy(index[h][:], edge["src"][:, bass.ds(at, B)]).then_inc(indexed[h], 1)

            def ranks(i, h):
                n = (2 * i + h) * Q
                turn_out(n, 0)
                for q in range(Q):
                    act.wait_ge(same, n + q + 1)
                    nc.scalar.activation(flat(earlier[q % 2][:]), flat(p_same[:, 0:PAIRS, :]), ACT.Relu).then_inc(same_sb, 1)
                    if q + 1 < Q:
                        turn_out(n + q + 1, q + 1)
                    act.wait_ge(summed, n + q + 1)
                    nc.scalar.activation(seen[(q + 1) % 2][:], p_seen[:, 0:J], ACT.Copy).then_inc(seen_sb, 1)

            def turn_out(n, q):
                act.wait_ge(turned, n + 1)
                nc.scalar.activation(flat(lo_t[q % 2][:]), flat(p_turn[:, 0:GROUP, :]), ACT.Copy)
                nc.scalar.activation(flat(lo_tf[q % 2][:]), flat(p_turn[:, 0:GROUP, :]), ACT.Copy).then_inc(turned_sb, 1)

            stage_index(0, 0)
            stage(0, 0)
            with act.Fori(0, IT) as i:
                for h in range(2):
                    n = 2 * i + h
                    act.wait_ge(stepped, INIT + per * n - (per - 2))
                    stage_index(1 - h, (n + 1) * B)
                    act.wait_ge(stepped, INIT + per * n)
                    stage(1 - h, (n + 1) * B)
                    if rank:
                        ranks(i, h)
            if count:
                act.wait_ge(counted, T + 2)
                nc.scalar.activation(edge["count"][:], p_count[:, 0:J], ACT.Copy).then_inc(staged[0], 1)
            if rank:
                act.wait_ge(summed, 2 * IT * Q)
                nc.scalar.activation(edge["seen"][:], p_seen[:, 0:J], ACT.Copy).then_inc(staged[0], 1)

        if count or rank:
            @block.tensor
            def _(pe):
                pe.wait_ge(stepped, INIT)
                if rank:
                    for s in (turned_sb, same_sb, seen_sb):
                        pe.sem_inc(s, 1)
                if count:
                    nc.tensor.matmul(p_count[:, 0:J], blank[:], blank[:, 0:J], start=True, stop=False).then_inc(counted, 1)

                def turn(n, h, q):
                    pe.wait_ge(turned_sb, n + 1)
                    for k in range(GROUP):
                        ins = nc.tensor.transpose(p_turn[:, k, :], one_lo[h][:, q * GROUP + k, :], sig["ident_b"][:])
                    ins.then_inc(turned, 1)

                def ranks(i, h):
                    n = (2 * i + h) * Q
                    turn(n, h, 0)
                    for q in range(Q):
                        pe.wait_ge(turned_sb, n + q + 2)
                        pe.wait_ge(same_sb, n + q + 1)
                        low = lo_t[q % 2]
                        for j in range(GROUP):
                            nc.tensor.matmul(p_same[:, PAIR[j], :], low[:, j, :], low[:, j, :], start=True, stop=False)
                            ins = nc.tensor.matmul(p_same[:, PAIR[j], :], sig["ident_b"][:], sig["not_earlier"][:], start=False, stop=True)
                            if j + 1 < GROUP:
                                ins = nc.tensor.matmul(p_same[:, PAIR[j] + 1:PAIR[j] + GROUP - j, :], low[:, j, :], low[:, j + 1:GROUP, :], start=True, stop=True)
                        ins.then_inc(same, 1)
                        if q + 1 < Q:
                            turn(n + q + 1, h, q + 1)
                        pe.wait_ge(seen_sb, n + q + 1)
                        nc.tensor.matmul(p_seen[:, 0:J], sig["ident"][:], seen[q % 2][:], start=True, stop=False)
                        for k in range(GROUP):
                            kk = q * GROUP + k
                            ins = nc.tensor.matmul(p_seen[:, 0:J], one_lo[h][:, kk, :], one_hi[h][:, kk, :], start=False, stop=k == GROUP - 1)
                        ins.then_inc(summed, 1)
                        pe.wait_ge(same_sb, n + q + 2)
                        for k in range(GROUP):
                            kk = q * GROUP + k
                            nc.tensor.matmul(p_look[:, kk, 0:J], lo_tf[q % 2][:, k, :], seen[q % 2][:], start=True, stop=False)
                            for j in range(k + 1):
                                ins = nc.tensor.matmul(p_look[:, kk, 0:J], earlier[q % 2][:, PAIR[j] + k - j, :], one_hi[h][:, q * GROUP + j, :], start=False, stop=j == k)
                        ins.then_inc(looked, 1)

                with pe.Fori(0, IT) as i:
                    for h in range(2):
                        pe.wait_ge(stepped, INIT + per * (2 * i + h))
                        if rank:
                            ranks(i, h)
                        if count:
                            for k in range(B):
                                nc.tensor.matmul(p_count[:, 0:J], at_lo[h][:, k, :], at_hi[h][:, k, :], start=False, stop=False).then_inc(counted, 1)
                if count:
                    nc.tensor.matmul(p_count[:, 0:J], blank[:], blank[:, 0:J], start=False, stop=True).then_inc(counted, 1)

        @block.vector
        def _(dve):
            def one_hots(h, step):
                if count:
                    step(nc.vector.tensor_tensor(at_lo[h][:], repeat(sig["iota"][:, 0:P], B), spread(dst_lo[h][:], P), ALU.is_equal))
                    step(nc.vector.tensor_tensor(at_hi[h][:], repeat(sig["iota"][:, 0:J], B), spread(dst_hi[h][:], J), ALU.is_equal))
                if rank:
                    step(nc.vector.tensor_tensor(one_lo[h][:], repeat(sig["iota"][:, 0:P], RANKED), spread(lo[h][:], P), ALU.is_equal))
                    step(nc.vector.tensor_tensor(one_hi[h][:], repeat(sig["iota"][:, 0:J], RANKED), spread(hi[h][:], J), ALU.is_equal))

            nc.vector.memset(run[1][:, B - 1, :], 0.0).then_inc(stepped, INIT - 3 * count - 3 * rank)
            if count:
                nc.vector.memset(blank[:], 0.0).then_inc(stepped, 1)
            if rank:
                nc.vector.tensor_copy(seen[0][:], edge["seen"][:]).then_inc(stepped, 1)
            if count or rank:
                dve.wait_ge(staged[0], 1)
                one_hots(0, lambda ins: ins.then_inc(stepped, 1))
            with dve.Fori(0, IT) as i:
                for h in range(2):
                    n = [0]

                    def step(ins):
                        ins.then_inc(stepped, 1)
                        n[0] += 1

                    def after():
                        dve.wait_ge(stepped, INIT + per * (2 * i + h) + n[0])

                    dve.wait_ge(staged[h], i + 1)
                    dve.wait_ge(gathered[h], 16 * B * (i + 1))
                    step(nc.vector.tensor_tensor(msg[h][:, :, 0:C], rows[h][:, :, C:2 * C], spread(weight[h][:], C), ALU.mult))
                    after()
                    step(nc.vector.tensor_tensor(msg[h][:, :, 0:C], msg[h][:, :, 0:C], rows[h][:, :, 0:C], ALU.add))
                    dve.wait_ge(stored[h], 16 * (1 + len(cleared)) * i + 16)
                    for k in range(B):
                        before = run[h][:, k - 1, :] if k else run[1 - h][:, B - 1, :]
                        after()
                        step(nc.vector.scalar_tensor_tensor(run[h][:, k, :], before, keep[h][:, k:k + 1], msg[h][:, k, :], ALU.mult, ALU.add))
                    if count or rank:
                        dve.wait_ge(staged[1 - h], i + 1 + h)
                    if count:
                        dve.wait_ge(counted, 1 + B * (2 * i + h))
                    if count or rank:
                        one_hots(1 - h, step)
                    if rank:
                        dve.wait_ge(looked, Q * (2 * i + h + 1))
                        step(nc.vector.tensor_tensor(picked[:], p_look[:, :, 0:J], one_hi[h][:], ALU.mult))
                        after()
                        step(nc.vector.tensor_reduce(edge["rank"][:, bass.ds((2 * i + h) * B + ranked, RANKED)], picked[:], AX.X, ALU.add))
                    assert n[0] == per
            dve.wait_ge(stepped, INIT + per * 2 * IT)
            nc.vector.tensor_copy(final[:, 0:width], run[1][:, B - 1, :]).then_inc(stepped, 1)


def store_and_split(nc, sig, make, rows, width, table, parts):
    with ExitStack() as ctx:
        rest = ctx.enter_context(nc.sbuf_tensor(f"rest{nc.next_id()}", [P, J, width], F32))
        block = ctx.enter_context(nc.Block())
        on_vector(nc, sig, make, block)

        def body(step):
            for part in parts:
                for c in range(width // SLICE):
                    step(nc.vector.memset(part[:, c, J:CLASSES * CLASS, :], 0.0))
            left = rows
            for k, part in enumerate(parts):
                for c in range(width // SLICE):
                    cut = slice(c * SLICE, (c + 1) * SLICE)
                    step(nc.vector.tensor_copy(part[:, c, 0:J, :], left[:, :, cut]))
                    if k + 1 < len(parts):
                        step(nc.vector.tensor_tensor(rest[:, :, cut], left[:, :, cut], part[:, c, 0:J, :], ALU.subtract))
                left = rest

        moves(nc, sig, [(table, rows[:])], block, sig["dve_step"].base)
        on_vector(nc, sig, body, block)


def graph_pass(nc, sig, table, width, edge, parts, running, final, zeros):
    SLICES = width // SLICE
    N_PICKS = PICKS[width]
    ON_CHIP = N_PICKS // SLICES
    GATHERED = B - ON_CHIP
    CHAIN = B // 2 + 6
    per = 2 + 2 * N_PICKS + 1 + CHAIN
    INIT = 2 * per
    PICK_ORDER = [(0, 0)] + [step for m in range(1, N_PICKS) for step in ((0, m), (1, m - 1))] + [(1, N_PICKS - 1)]

    def picked_at(kind, m):
        return 2 + PICK_ORDER.index((kind, m)) + 1

    with ExitStack() as ctx:
        uid = nc.next_id()

        def sb(name, shape, dt=F32):
            return ctx.enter_context(nc.sbuf_tensor(f"{name}{uid}", shape, dt))

        def pair(name, shape, dt=F32):
            return [sb(f"{name}{h}_", shape, dt) for h in range(2)]

        def sem(name):
            return ctx.enter_context(nc.semaphore(f"{name}{uid}"))

        index = pair("index", [P, GATHERED], I32)
        weight, keep = pair("weight", [P, B]), pair("keep", [P, B])
        lo, hi = pair("lo", [P, ON_CHIP]), pair("hi", [P, ON_CHIP])
        one_lo, one_hi = pair("one_lo", [P, ON_CHIP, CLASSES * P], BF16), pair("one_hi", [P, ON_CHIP, CLASS])
        lo_t = pair("lo_t", [P, ON_CHIP, CLASSES, P], BF16)
        rows, msg = (pair(n, [P, B, width]) for n in ("rows", "msg"))
        run = pair("run", [P, 1 + B, width])
        both, two, held = sb("both", [P, B // 2]), sb("two", [P, B // 2, width]), sb("held", [P, B // 2, width])
        picked = [sb(f"picked{k}_", [P, SLICE, CLASS]) for k in range(3)]
        p_turn = ctx.enter_context(nc.psum_tensor(f"p_turn{uid}", [P, 2, 8, P], BF16))
        p_slots = ctx.enter_context(nc.psum_tensor(f"p_slots{uid}", [P, N_PICKS, 512], F32))
        gathered, stored, indexed, staged = ([sem(f"{n}{h}_") for h in range(2)] for n in ("gathered", "stored", "indexed", "staged"))
        stepped, turned, turned_sb, looked = (sem(n) for n in ("stepped", "turned", "turned_sb", "looked"))
        block = ctx.enter_context(nc.Block())
        running_v = running[0:EP, :].rearrange("(p t) c -> p t c", p=P)

        @block.sync
        def _(sp):
            for h in range(2):
                cut = slice(h * width // 2, (h + 1) * width // 2)
                sp.dma_start(running[EP:EP + 1, cut], zeros[0:1, cut]).then_inc(stored[h], 16)
            with sp.Fori(0, IT) as i:
                for h in range(2):
                    sp.wait_ge(stepped, INIT + per * (2 * i + h + 1))
                    sp.dma_start(running_v[:, bass.ds((2 * i + h) * B, B), :], run[h][:, 1:1 + B, :]).then_inc(stored[h], 16)
            for h in range(2):
                sp.wait_ge(stored[h], 16 * (IT + 1))

        @block.gpsimd
        def _(pool):
            with pool.Fori(0, IT) as i:
                for h in range(2):
                    pool.wait_ge(indexed[h], i + 1)
                    pool.sem_inc(sig["rounds"].sem, 1)
                    for k in range(GATHERED):
                        pool.indirect_dma_start(out=rows[h][:, ON_CHIP + k, :], out_offset=None, in_=table,
                                                in_offset=offsets(index[h][:, k:k + 1])).then_inc(gathered[h], 16)

        @block.scalar
        def _(act):
            def stage_index(h, at):
                nc.scalar.activation(lo[h][:], edge["src_key"][:, bass.ds(at, ON_CHIP)], ACT.Copy)
                nc.scalar.activation(hi[h][:], edge["src_slot"][:, bass.ds(at, ON_CHIP)], ACT.Copy)
                nc.scalar.copy(index[h][:], edge["src"][:, bass.ds(at + ON_CHIP, GATHERED)]).then_inc(indexed[h], 1)

            def stage(h, at):
                nc.scalar.activation(weight[h][:], edge["weight"][:, bass.ds(at, B)], ACT.Copy)
                nc.scalar.activation(keep[h][:], edge["keep"][:, bass.ds(at, B)], ACT.Copy).then_inc(staged[h], 1)

            def turn_out(n, h):
                for k in range(ON_CHIP):
                    act.wait_ge(turned, ON_CHIP * n + k + 1)
                    nc.scalar.activation(flat(lo_t[h][:, k, :, :]), flat(p_turn[:, k % 2, 0:CLASSES, :]), ACT.Copy).then_inc(turned_sb, 1)

            stage_index(0, 0)
            stage(0, 0)
            turn_out(0, 0)
            with act.Fori(0, IT) as i:
                for h in range(2):
                    n = 2 * i + h
                    act.wait_ge(stepped, INIT + per * n - CHAIN)
                    stage_index(1 - h, (n + 1) * B)
                    act.wait_ge(stepped, INIT + per * n)
                    stage(1 - h, (n + 1) * B)
                    turn_out(n + 1, 1 - h)

        @block.tensor
        def _(pe):
            def turn(n, h, k):
                if k == 0:
                    pe.wait_ge(stepped, INIT + per * (n - 1) + 2)
                elif k >= 2:
                    pe.wait_ge(turned_sb, ON_CHIP * n + k - 1)
                pe.sem_inc(sig["rounds"].sem, 1)
                for q in range(CLASSES):
                    ins = nc.tensor.transpose(p_turn[:, k % 2, q, :], one_lo[h][:, k, q * P:(q + 1) * P], sig["ident_b"][:])
                ins.then_inc(turned, 1)

            def multiply(n, h, k):
                pe.wait_ge(turned_sb, ON_CHIP * n + k + 1)
                for c in range(SLICES):
                    m = k * SLICES + c
                    pe.wait_ge(stepped, INIT + per * (n - 1) + picked_at(0, m))
                    for q in range(CLASSES):
                        for part_no, part in enumerate(parts):
                            ins = nc.tensor.matmul(p_slots[:, m, 0:CLASS * SLICE], lo_t[h][:, k, q, :], flat(part[:, c, q * CLASS:(q + 1) * CLASS, :]),
                                                   start=q == 0 and part_no == 0, stop=q == CLASSES - 1 and part_no == len(parts) - 1)
                    ins.then_inc(looked, 1)

            with pe.Fori(0, IT) as i:
                for h in range(2):
                    turn(2 * i + h, h, 0)
                    for k in range(ON_CHIP):
                        if k + 1 < ON_CHIP:
                            turn(2 * i + h, h, k + 1)
                        multiply(2 * i + h, h, k)
            for k in range(ON_CHIP):
                turn(2 * IT, 0, k)

        @block.vector
        def _(dve):
            def one_hots(h, step):
                step(nc.vector.tensor_tensor(one_lo[h][:], repeat(sig["iota"][:], ON_CHIP), spread(lo[h][:], CLASSES * P), ALU.is_equal))
                step(nc.vector.tensor_tensor(one_hi[h][:], repeat(sig["iota"][:, 0:CLASS], ON_CHIP), spread(hi[h][:], CLASS), ALU.is_equal))

            dve.wait_ge(indexed[0], 1)
            one_hots(0, lambda ins: ins.then_inc(stepped, (per + 2) // 2))
            nc.vector.memset(run[1][:, B, :], 0.0).then_inc(stepped, INIT - 2 * ((per + 2) // 2))
            with dve.Fori(0, IT) as i:
                for h in range(2):
                    n = [0]

                    def step(ins):
                        ins.then_inc(stepped, 1)
                        n[0] += 1

                    def after(back=0):
                        dve.wait_ge(stepped, INIT + per * (2 * i + h) + n[0] - back)

                    dve.wait_ge(indexed[1 - h], i + 1 + h)
                    one_hots(1 - h, step)
                    for kind, m in PICK_ORDER:
                        k, c = m // SLICES, m % SLICES
                        if kind == 0:
                            dve.wait_ge(looked, N_PICKS * (2 * i + h) + m + 1)
                            if m >= 3:
                                dve.wait_ge(stepped, INIT + per * (2 * i + h) + picked_at(1, m - 3))
                            slots = p_slots[:, m, 0:CLASS * SLICE].rearrange("p (j c) -> p c j", c=SLICE)
                            step(nc.vector.tensor_tensor(picked[m % 3][:], slots, one_hi[h][:, k:k + 1, :].broadcast_to([P, SLICE, CLASS]), ALU.mult))
                        else:
                            dve.wait_ge(stepped, INIT + per * (2 * i + h) + picked_at(0, m))
                            step(nc.vector.tensor_reduce(rows[h][:, k, c * SLICE:(c + 1) * SLICE], picked[m % 3][:], AX.X, ALU.add))
                    dve.wait_ge(gathered[h], 16 * GATHERED * (i + 1))
                    dve.wait_ge(staged[h], i + 1)
                    after()
                    step(nc.vector.tensor_tensor(msg[h][:], rows[h][:], spread(weight[h][:], width), ALU.mult))
                    step(nc.vector.tensor_tensor(both[:], keep[h][:, 0:B:2], keep[h][:, 1:B:2], ALU.mult))
                    after(1)
                    step(nc.vector.tensor_tensor(two[:], msg[h][:, 0:B:2, :], spread(keep[h][:, 1:B:2], width), ALU.mult))
                    dve.wait_ge(stored[h], 16 * (i + 1))
                    step(nc.vector.tensor_copy(run[h][:, 0, :], run[1 - h][:, B, :]))
                    after(1)
                    step(nc.vector.tensor_tensor(two[:], two[:], msg[h][:, 1:B:2, :], ALU.add))
                    for k in range(B // 2):
                        after()
                        step(nc.vector.scalar_tensor_tensor(run[h][:, 2 * k + 2, :], run[h][:, 2 * k, :], both[:, k:k + 1], two[:, k, :], ALU.mult, ALU.add))
                    after(1)
                    step(nc.vector.tensor_tensor(held[:], run[h][:, 0:B:2, :], spread(keep[h][:, 0:B:2], width), ALU.mult))
                    after()
                    step(nc.vector.tensor_tensor(run[h][:, 1:B:2, :], held[:], msg[h][:, 0:B:2, :], ALU.add))
                    assert n[0] == per
            dve.wait_ge(stepped, INIT + per * 2 * IT)
            nc.vector.tensor_copy(final[:, 0:width], run[1][:, B, :]).then_inc(stepped, 1)


def spread_to_edges(nc, sig, block, node_rows, begin_row, edge_rows, table, first_key, first_rows, saved=0):
    with ExitStack() as ctx:
        fetched, moved = sig["fetched"], sig["moved"]

        @block.gpsimd
        def _(pool):
            for j in range(J):
                if saved and j % 7 == 0:
                    pool.wait_ge(sig["saved"].sem, saved + j // 7 + 1)
                pool.indirect_dma_start(out=edge_rows, out_offset=offsets(begin_row[:, j:j + 1]), in_=node_rows[:, j, :], in_offset=None,
                                        bounds_check=EP - 1, oob_is_err=False).then_inc(fetched.sem, 16)
            pool.wait_ge(moved.sem, moved.base)
            pool.indirect_dma_start(out=first_rows[:], out_offset=None, in_=table, in_offset=offsets(first_key)).then_inc(fetched.sem, 16)
            pool.wait_ge(fetched.sem, fetched.base + 16 * (J + 1))

        fetched.base += 16 * (J + 1)


def attention_pass(nc, sig, table, edge, labels, label_rows, node_rows, first_rows, w_label, w_label_att, running, final, sent, zeros):
    KEY, OUT0, LABEL0, IN0, EF0, WIDE = 0, 1, 1 + C, SENT, SENT + C, SENT + 2 * C
    SUMS = LABELS + C
    per = 1 + B + 11 + 2 * B
    with ExitStack() as ctx:
        def sb(name, shape, dt=F32):
            return ctx.enter_context(nc.sbuf_tensor(name, shape, dt))

        def pair(name, shape, dt=F32):
            return [sb(f"{name}{h}", shape, dt) for h in range(2)]

        def sem(name):
            return ctx.enter_context(nc.semaphore(name))

        index, place = pair("a_index", [P, B], I32), pair("a_place", [P, B], I32)
        keep, pen, rank, key = pair("a_keep", [P, B]), pair("a_pen", [P, B]), pair("a_rank", [P, B]), pair("a_key", [P, B])
        rows = pair("a_rows", [P, B, 2 * C + 1])
        begun, xdst = pair("a_begun", [P, B, C]), pair("a_xdst", [P, B, C])
        label, label_row = pair("a_label", [LABELS, B * P]), pair("a_label_row", [P, B, LABELS])
        product = sb("a_product", [P, B, C])
        score = pair("a_score", [P, B])
        label_score, att = pair("a_label_score", [P, B]), pair("a_att", [P, B])
        msg = pair("a_msg", [P, B, WIDE])
        run = pair("a_run", [P, B, RUN])
        p_label = [ctx.enter_context(nc.psum_tensor(f"a_p_label{h}", [P, B, C], F32)) for h in range(2)]
        p_score = [ctx.enter_context(nc.psum_tensor(f"a_p_score{h}", [P, 512], F32)) for h in range(2)]
        gathered, stored, staged, indexed, loaded, scattered = ([sem(f"a_{n}{h}") for h in range(2)] for n in ("gathered", "stored", "staged", "indexed", "loaded", "scattered"))
        stepped, labelled, activated = sem("a_stepped"), sem("a_labelled"), sem("a_activated")
        block = ctx.enter_context(nc.Block())
        running_v = running[0:EP, :].rearrange("(p t) c -> p t c", p=P)
        node_rows_v = node_rows[0:EP, :].rearrange("(p t) c -> p t c", p=P)
        INIT = 2 * per
        PLACED = 1 + B + 11

        @block.sync
        def _(sp):
            def load(h, n):
                sp.dma_start(begun[h][:], node_rows_v[:, bass.ds(n * B, B), :]).then_inc(loaded[h], 16)
                sp.dma_start(label[h][:], labels[:, bass.ds(n * (B * P), B * P)]).then_inc(loaded[h], 16)
                sp.dma_start(label_row[h][:], label_rows[:, bass.ds(n * B, B), :]).then_inc(loaded[h], 16)

            def store(h, i):
                sp.wait_ge(stepped, INIT + per * (2 * i + h + 1))
                sp.dma_start(running_v[:, bass.ds((2 * i + h) * B, B), :], run[h][:]).then_inc(stored[h], 16)

            for h in range(2):
                cut = slice(h * RUN // 2, (h + 1) * RUN // 2)
                sp.dma_start(running[EP:EP + 1, cut], zeros[0:1, cut]).then_inc(stored[h], 16)
            load(0, 0)
            load(1, 1)
            with sp.Fori(0, IT - 1) as i:
                for h in range(2):
                    store(h, i)
                    load(h, 2 * i + 2 + h)
            for h in range(2):
                store(h, IT - 1)
            for h in range(2):
                sp.wait_ge(stored[h], 16 * (IT + 1))

        @block.gpsimd
        def _(pool):
            def gather(h, i):
                pool.wait_ge(indexed[h], i + 1)
                pool.sem_inc(sig["rounds"].sem, 1)
                for k in range(B):
                    pool.indirect_dma_start(out=rows[h][:, k, :], out_offset=None, in_=table,
                                            in_offset=offsets(index[h][:, k:k + 1])).then_inc(gathered[h], 16)

            def scatter(h, i):
                pool.wait_ge(stepped, INIT + per * (2 * i + h) + PLACED)
                pool.sem_inc(sig["rounds"].sem, 1)
                for k in range(B):
                    pool.indirect_dma_start(out=sent, out_offset=offsets(place[h][:, k:k + 1]), in_=msg[h][:, k, 0:SENT],
                                            in_offset=None).then_inc(scattered[h], 16)

            gather(0, 0)
            with pool.Fori(0, IT - 1) as i:
                gather(1, i)
                scatter(0, i)
                gather(0, i + 1)
                scatter(1, i)
            gather(1, IT - 1)
            scatter(0, IT - 1)
            scatter(1, IT - 1)
            for h in range(2):
                pool.wait_ge(scattered[h], 16 * B * IT)

        @block.scalar
        def _(act):
            def stage(h, at):
                nc.scalar.activation(rank[h][:], edge["rank"][:, bass.ds(at, B)], ACT.Copy)
                nc.scalar.activation(key[h][:], edge["src"][:, bass.ds(at, B)], ACT.Copy)
                nc.scalar.activation(keep[h][:], edge["keep"][:, bass.ds(at, B)], ACT.Copy).then_inc(staged[h], 1)

            def stage_index(h, at):
                nc.scalar.copy(index[h][:], edge["src"][:, bass.ds(at, B)]).then_inc(indexed[h], 1)

            def attention(h, i):
                act.wait_ge(labelled, 2 * i + h + 1)
                nc.scalar.activation(label_score[h][:], p_score[h][:, 0:B], ACT.Copy).then_inc(activated, 1)
                act.wait_ge(stepped, INIT + per * (2 * i + h) + 1 + B + 5)
                nc.scalar.activation(att[h][:], score[h][:], ACT.Sigmoid).then_inc(activated, 1)

            stage_index(0, 0)
            stage(0, 0)
            with act.Fori(0, IT) as i:
                for h in range(2):
                    n = 2 * i + h
                    act.wait_ge(stepped, INIT + per * (n - 1) + PLACED)
                    stage_index(1 - h, (n + 1) * B)
                    act.wait_ge(stepped, INIT + per * n)
                    stage(1 - h, (n + 1) * B)
                    attention(h, i)

        @block.tensor
        def _(pe):
            with pe.Fori(0, IT) as i:
                for h in range(2):
                    pe.wait_ge(loaded[h], 48 * (i + 1))
                    pe.wait_ge(stepped, INIT + per * (2 * i + h - 1))
                    for k in range(B):
                        edges = label[h][:, k * P:(k + 1) * P]
                        nc.tensor.matmul(p_label[h][:, k, :], edges, w_label, start=True, stop=True)
                        ins = nc.tensor.matmul(p_score[h][:, k:k + 1], edges, w_label_att, start=True, stop=True)
                    ins.then_inc(labelled, 1)

        @block.vector
        def _(dve):
            nc.vector.memset(run[1][:, B - 1, 0:SUMS], 0.0).then_inc(stepped, 1)
            nc.vector.memset(run[1][:, B - 1, SUMS:RUN], -BIG).then_inc(stepped, 1)
            nc.vector.tensor_copy(xdst[1][:, B - 1, :], first_rows[:, C:2 * C]).then_inc(stepped, INIT - 2)
            def both_halves(i, first):
                for h in range(2):
                    n = [0]

                    def step(ins):
                        ins.then_inc(stepped, 1)
                        n[0] += 1

                    def after(back=0):
                        dve.wait_ge(stepped, INIT + per * (2 * i + h) + n[0] - back)

                    dve.wait_ge(staged[h], i + 1)
                    step(nc.vector.tensor_scalar(pen[h][:], keep[h][:], BIG, -BIG, ALU.mult, ALU.add))
                    dve.wait_ge(loaded[h], 48 * (i + 1))
                    for k in range(B):
                        before = xdst[h][:, k - 1, :] if k else xdst[1 - h][:, B - 1, :]
                        after()
                        step(nc.vector.scalar_tensor_tensor(xdst[h][:, k, :], before, keep[h][:, k:k + 1], begun[h][:, k, :], ALU.mult, ALU.add))
                    dve.wait_ge(gathered[h], 16 * B * (i + 1))
                    after()
                    step(nc.vector.tensor_tensor(product[:], rows[h][:, :, 0:C], xdst[h][:], ALU.mult))
                    after()
                    step(nc.vector.tensor_reduce(score[h][:], product[:], AX.X, ALU.add))
                    after()
                    step(nc.vector.scalar_tensor_tensor(score[h][:], score[h][:], 0.01, score[h][:], ALU.mult, ALU.max))
                    dve.wait_ge(activated, 2 * (2 * i + h) + 1)
                    step(nc.vector.scalar_tensor_tensor(label_score[h][:], label_score[h][:], 0.01, label_score[h][:], ALU.mult, ALU.max))
                    after()
                    step(nc.vector.tensor_tensor(score[h][:], score[h][:], label_score[h][:], ALU.add))
                    dve.wait_ge(activated, 2 * (2 * i + h) + 2)
                    if not first:
                        dve.wait_ge(scattered[h], 16 * B * i)
                    step(nc.vector.tensor_tensor(msg[h][:, :, OUT0:LABEL0], xdst[h][:], spread(att[h][:], C), ALU.mult))
                    step(nc.vector.tensor_tensor(msg[h][:, :, LABEL0:IN0], label_row[h][:], spread(att[h][:], LABELS), ALU.mult))
                    step(nc.vector.tensor_tensor(msg[h][:, :, EF0:WIDE], p_label[h][:], spread(att[h][:], C), ALU.mult))
                    step(nc.vector.tensor_tensor(msg[h][:, :, IN0:EF0], rows[h][:, :, C:2 * C], spread(att[h][:], C), ALU.mult))
                    step(nc.vector.tensor_copy(msg[h][:, :, KEY], key[h][:]))
                    step(nc.vector.tensor_tensor(place[h][:], rows[h][:, :, 2 * C], rank[h][:], ALU.add))
                    dve.wait_ge(stored[h], 16 * (i + 1))
                    after(1)
                    for k in range(B):
                        before = run[h][:, k - 1, :] if k else run[1 - h][:, B - 1, :]
                        if k:
                            after(1)
                        step(nc.vector.scalar_tensor_tensor(run[h][:, k, 0:SUMS], before[:, 0:SUMS], keep[h][:, k:k + 1],
                                                            msg[h][:, k, LABEL0:EF0], ALU.mult, ALU.add))
                        if k:
                            after(1)
                        step(nc.vector.scalar_tensor_tensor(run[h][:, k, SUMS:RUN], before[:, SUMS:RUN], pen[h][:, k:k + 1],
                                                            msg[h][:, k, IN0:WIDE], ALU.add, ALU.max))
                    assert n[0] == per, n

            both_halves(0, True)
            with dve.Fori(1, IT) as i:
                both_halves(i, False)
            dve.wait_ge(stepped, INIT + per * 2 * IT)
            nc.vector.tensor_copy(final[:], run[1][:, B - 1, :]).then_inc(stepped, 1)


def source_pass(nc, sig, block, ctx, sent, w_labels, running, final, zeros):
    SUMS = C + LABELS
    PRODUCTS = B * C // 512
    per = 4 + 2 * B
    KEPT = 4

    def sb(name, shape, dt=F32):
        return ctx.enter_context(nc.sbuf_tensor(name, shape, dt))

    def pair(name, shape, dt=F32):
        return [sb(f"{name}{h}", shape, dt) for h in range(2)]

    def sem(name):
        return ctx.enter_context(nc.semaphore(name))

    rows = pair("s_rows", [P, B, SENT])
    msg = pair("s_msg", [P, B, LABELS + 2 * C])
    run = pair("s_run", [P, B, RUN])
    keep, pen = pair("s_keep", [P, B]), pair("s_pen", [P, B])
    label, label_t = sb("s_label", [P, B, LABELS]), sb("s_label_t", [B * LABELS, P])
    last_key = sb("s_last_key", [P, 1])
    p_turn = ctx.enter_context(nc.psum_tensor("s_p_turn", [P, 512], F32))
    p_ef = ctx.enter_context(nc.psum_tensor("s_p_ef", [P, B, C], F32))
    loaded, stored = ([sem(f"s_{n}{h}") for h in range(2)] for n in ("loaded", "stored"))
    stepped, copied, taken, turned, turned_sb, projected, peaked = (
        sem(f"s_{n}") for n in ("stepped", "copied", "taken", "turned", "turned_sb", "projected", "peaked"))
    running_v = running[0:EP, :].rearrange("(p t) c -> p t c", p=P)
    sent_v = sent.rearrange("(p t) c -> p t c", p=P)
    INIT = 2 * per

    @block.sync
    def _(sp):
        for h in range(2):
            cut = slice(h * RUN // 2, (h + 1) * RUN // 2)
            sp.dma_start(running[EP:EP + 1, cut], zeros[0:1, cut]).then_inc(stored[h], 16)
        with sp.Fori(0, IT) as i:
            for h in range(2):
                sp.wait_ge(stepped, INIT + per * (2 * i + h + 1))
                sp.dma_start(running_v[:, bass.ds((2 * i + h) * B, B), :], run[h][:]).then_inc(stored[h], 16)
        for h in range(2):
            sp.wait_ge(stored[h], 16 * (IT + 1))

    @block.scalar
    def _(act):
        def load(h, n):
            act.dma_start(rows[h][:], sent_v[:, bass.ds(n * B, B), :]).then_inc(loaded[h], 16)

        def messages(h, i):
            n = 2 * i + h
            act.wait_ge(loaded[h], 16 * (i + 1))
            act.wait_ge(turned, n + 1)
            nc.scalar.activation(label[:], rows[h][:, :, 1 + C:SENT], ACT.Copy).then_inc(taken, 1)
            act.wait_ge(turned, n + 2)
            nc.scalar.activation(label_t[:], p_turn[:, 0:P], ACT.Copy).then_inc(turned_sb, 1)
            act.wait_ge(stepped, INIT + per * (n - 1))
            nc.scalar.activation(msg[h][:, :, 0:LABELS], rows[h][:, :, 1 + C:SENT], ACT.Copy).then_inc(copied, 1)
            nc.scalar.activation(msg[h][:, :, LABELS:SUMS], rows[h][:, :, 1:1 + C], ACT.Copy).then_inc(copied, 1)
            for m in range(PRODUCTS):
                act.wait_ge(projected, PRODUCTS * n + m + 1)
                cut = slice(m * B // PRODUCTS, (m + 1) * B // PRODUCTS)
                nc.scalar.activation(msg[h][:, cut, SUMS:SUMS + C], p_ef[:, cut, :], ACT.Copy).then_inc(peaked, 1)

        act.sem_inc(turned, 1)
        load(0, 0)
        load(1, 1)
        with act.Fori(0, IT - 1) as i:
            for h in range(2):
                messages(h, i)
                act.wait_ge(copied, 2 * (2 * i + h + 1))
                act.wait_ge(stepped, INIT + per * (2 * i + h) + KEPT)
                load(h, 2 * i + 2 + h)
        for h in range(2):
            messages(h, IT - 1)

    @block.tensor
    def _(pe):
        pe.sem_inc(peaked, PRODUCTS)
        with pe.Fori(0, IT) as i:
            for h in range(2):
                n = 2 * i + h
                pe.wait_ge(taken, n + 1)
                pe.wait_ge(peaked, PRODUCTS * (n + 1))
                pe.sem_inc(sig["rounds"].sem, 1)
                nc.tensor.transpose(p_turn[:, 0:P], flat(label[:]), sig["ident"][:]).then_inc(turned, 1)
                pe.wait_ge(turned_sb, n + 1)
                for m in range(PRODUCTS):
                    cut = slice(m * B // PRODUCTS, (m + 1) * B // PRODUCTS)
                    nc.tensor.matmul(flat(p_ef[:, cut, :]), label_t[:], flat(w_labels[:, cut, :]), start=True, stop=True).then_inc(projected, 1)

    @block.vector
    def _(dve):
        nc.vector.memset(run[1][:, B - 1, 0:SUMS], 0.0).then_inc(stepped, 1)
        nc.vector.memset(run[1][:, B - 1, SUMS:RUN], -BIG).then_inc(stepped, 1)
        nc.vector.memset(last_key[:], -1.0).then_inc(stepped, INIT - 2)
        with dve.Fori(0, IT) as i:
            for h in range(2):
                n = [0]

                def step(ins):
                    ins.then_inc(stepped, 1)
                    n[0] += 1

                def after(back=0):
                    dve.wait_ge(stepped, INIT + per * (2 * i + h) + n[0] - back)

                dve.wait_ge(loaded[h], 16 * (i + 1))
                after()
                step(nc.vector.tensor_tensor(keep[h][:, 0:1], rows[h][:, 0, 0:1], last_key[:], ALU.is_equal))
                step(nc.vector.tensor_tensor(keep[h][:, 1:B], rows[h][:, 1:B, 0], rows[h][:, 0:B - 1, 0], ALU.is_equal))
                after()
                step(nc.vector.tensor_copy(last_key[:], rows[h][:, B - 1, 0:1]))
                step(nc.vector.tensor_scalar(pen[h][:], keep[h][:], BIG, -BIG, ALU.mult, ALU.add))
                dve.wait_ge(stored[h], 16 * (i + 1))
                dve.wait_ge(peaked, PRODUCTS * (2 * i + h + 2))
                after()
                for k in range(B):
                    before = run[h][:, k - 1, :] if k else run[1 - h][:, B - 1, :]
                    if k:
                        after(1)
                    step(nc.vector.scalar_tensor_tensor(run[h][:, k, 0:SUMS], before[:, 0:SUMS], keep[h][:, k:k + 1], msg[h][:, k, 0:SUMS], ALU.mult, ALU.add))
                    if k:
                        after(1)
                    step(nc.vector.scalar_tensor_tensor(run[h][:, k, SUMS:RUN], before[:, SUMS:RUN], pen[h][:, k:k + 1], msg[h][:, k, LABELS:LABELS + 2 * C], ALU.add, ALU.max))
                assert n[0] == per, n
        dve.wait_ge(stepped, INIT + per * 2 * IT)
        nc.vector.tensor_copy(final[:, 0:RUN], run[1][:, B - 1, :]).then_inc(stepped, 1)


def softmax_pass(nc, sig, table, edge, attrs, w_edge, w_edge_att, running, final, zeros):
    per = 13 + B + 1
    S, W = C + 1, C + 2
    with ExitStack() as ctx:
        def sb(name, shape, dt=F32):
            return ctx.enter_context(nc.sbuf_tensor(name, shape, dt))

        def pair(name, shape, dt=F32):
            return [sb(f"{name}{h}", shape, dt) for h in range(2)]

        def sem(name):
            return ctx.enter_context(nc.semaphore(name))

        index = pair("e_index", [P, B], I32)
        keep, pen, at_dst = pair("e_keep", [P, B]), pair("e_pen", [P, B]), pair("e_at_dst", [P, B])
        rows = pair("e_rows", [P, B, W])
        attr = pair("e_attr", [EDIM, B * P])
        edge_score, score, bounded = pair("e_edge_score", [P, B]), pair("e_score", [P, B]), pair("e_bounded", [P, B])
        top = pair("e_top", [P, 1 + B])
        exps = pair("e_exps", [P, 2 * B])
        factor = pair("e_factor", [P, 2 * B])
        msg = pair("e_msg", [P, B, S])
        run = pair("e_run", [P, B, W])
        p_edge = [ctx.enter_context(nc.psum_tensor(f"e_p_edge{h}", [P, B, C], F32)) for h in range(2)]
        p_score = [ctx.enter_context(nc.psum_tensor(f"e_p_score{h}", [P, 512], F32)) for h in range(2)]
        gathered, stored, staged, loaded = ([sem(f"e_{n}{h}") for h in range(2)] for n in ("gathered", "stored", "staged", "loaded"))
        stepped, projected, activated = sem("e_stepped"), sem("e_projected"), sem("e_activated")
        block = ctx.enter_context(nc.Block())
        running_v = running[0:EP, :].rearrange("(p t) c -> p t c", p=P)
        INIT = per

        @block.sync
        def _(sp):
            def load(h, n):
                sp.dma_start(attr[h][:], attrs[:, bass.ds(n * (B * P), B * P)]).then_inc(loaded[h], 16)

            def store(h, i):
                sp.wait_ge(stepped, INIT + per * (2 * i + h + 1))
                sp.dma_start(running_v[:, bass.ds((2 * i + h) * B, B), :], run[h][:]).then_inc(stored[h], 16)

            sp.dma_start(running[EP:EP + 1, :], zeros[0:1, 0:W]).then_inc(stored[0], 16)
            load(0, 0)
            load(1, 1)
            with sp.Fori(0, IT - 1) as i:
                for h in range(2):
                    store(h, i)
                    load(h, 2 * i + 2 + h)
            for h in range(2):
                store(h, IT - 1)
            for h in range(2):
                sp.wait_ge(stored[h], 16 * IT + 16 * (h == 0))

        @block.gpsimd
        def _(pool):
            with pool.Fori(0, IT) as i:
                for h in range(2):
                    pool.wait_ge(staged[h], i + 1)
                    pool.sem_inc(sig["rounds"].sem, 1)
                    for k in range(B):
                        pool.indirect_dma_start(out=rows[h][:, k, :], out_offset=None, in_=table,
                                                in_offset=offsets(index[h][:, k:k + 1])).then_inc(gathered[h], 16)

        @block.scalar
        def _(act):
            def stage(h, at):
                nc.scalar.activation(keep[h][:], edge["keep"][:, bass.ds(at, B)], ACT.Copy)
                nc.scalar.activation(at_dst[h][:], edge["at_dst"][:, bass.ds(at, B)], ACT.Copy)
                nc.scalar.copy(index[h][:], edge["src"][:, bass.ds(at, B)]).then_inc(staged[h], 1)

            def activate(h, i):
                act.wait_ge(projected, 2 * i + h + 1)
                nc.scalar.activation(edge_score[h][:], p_score[h][:, 0:B], ACT.Copy).then_inc(activated, 1)
                act.wait_ge(stepped, INIT + per * (2 * i + h) + 10)
                nc.scalar.activation(factor[h][:], exps[h][:], ACT.Exp).then_inc(activated, 1)

            stage(0, 0)
            with act.Fori(0, IT) as i:
                act.wait_ge(stepped, INIT + per * (2 * i))
                stage(1, (2 * i + 1) * B)
                activate(0, i)
                act.wait_ge(stepped, INIT + per * (2 * i + 1))
                stage(0, (2 * i + 2) * B)
                activate(1, i)

        @block.tensor
        def _(pe):
            with pe.Fori(0, IT) as i:
                for h in range(2):
                    pe.wait_ge(loaded[h], 16 * (i + 1))
                    pe.wait_ge(stepped, per * (2 * i + h))
                    for k in range(B):
                        edges = attr[h][:, k * P:(k + 1) * P]
                        nc.tensor.matmul(p_edge[h][:, k, :], edges, w_edge, start=True, stop=True)
                        ins = nc.tensor.matmul(p_score[h][:, k:k + 1], edges, w_edge_att, start=True, stop=True)
                    ins.then_inc(projected, 1)

        @block.vector
        def _(dve):
            nc.vector.memset(run[1][:, B - 1, :], 0.0).then_inc(stepped, 1)
            nc.vector.memset(top[1][:, B:B + 1], -BIG).then_inc(stepped, INIT - 1)
            with dve.Fori(0, IT) as i:
                for h in range(2):
                    n = [0]

                    def step(ins):
                        ins.then_inc(stepped, 1)
                        n[0] += 1

                    def after(back=0):
                        dve.wait_ge(stepped, INIT + per * (2 * i + h) + n[0] - back)

                    dve.wait_ge(staged[h], i + 1)
                    step(nc.vector.tensor_scalar(pen[h][:], keep[h][:], BIG, -BIG, ALU.mult, ALU.add))
                    after()
                    step(nc.vector.tensor_copy(top[h][:, 0:1], top[1 - h][:, B:B + 1]))
                    dve.wait_ge(gathered[h], 16 * B * (i + 1))
                    dve.wait_ge(activated, 2 * (2 * i + h) + 1)
                    step(nc.vector.tensor_tensor(score[h][:], rows[h][:, :, C], at_dst[h][:], ALU.add))
                    after()
                    step(nc.vector.tensor_tensor(score[h][:], score[h][:], edge_score[h][:], ALU.add))
                    after()
                    step(nc.vector.scalar_tensor_tensor(score[h][:], score[h][:], 0.2, score[h][:], ALU.mult, ALU.max))
                    after()
                    step(nc.vector.tensor_scalar(bounded[h][:], score[h][:], -1.0e9, None, ALU.max))
                    after()
                    step(nc.vector.tensor_tensor_scan(top[h][:, 1:1 + B], pen[h][:], bounded[h][:], top[h][:, 0:1], ALU.add, ALU.max))
                    after()
                    step(nc.vector.tensor_tensor(exps[h][:, 0:B], score[h][:], top[h][:, 1:1 + B], ALU.subtract))
                    step(nc.vector.tensor_tensor(exps[h][:, B:2 * B], top[h][:, 0:B], top[h][:, 1:1 + B], ALU.subtract))
                    after()
                    step(nc.vector.scalar_tensor_tensor(exps[h][:, B:2 * B], exps[h][:, B:2 * B], 0.0, pen[h][:], ALU.min, ALU.add))
                    step(nc.vector.tensor_tensor(msg[h][:, :, 0:C], rows[h][:, :, 0:C], p_edge[h][:], ALU.add))
                    dve.wait_ge(activated, 2 * (2 * i + h) + 2)
                    after()
                    step(nc.vector.tensor_tensor(msg[h][:, :, 0:C], msg[h][:, :, 0:C], spread(factor[h][:, 0:B], C), ALU.mult))
                    step(nc.vector.tensor_copy(msg[h][:, :, C], factor[h][:, 0:B]))
                    dve.wait_ge(stored[h], 16 * i + 16 * (h == 0))
                    for k in range(B):
                        before = run[h][:, k - 1, 0:S] if k else run[1 - h][:, B - 1, 0:S]
                        after()
                        step(nc.vector.scalar_tensor_tensor(run[h][:, k, 0:S], before, factor[h][:, B + k:B + k + 1], msg[h][:, k, :], ALU.mult, ALU.add))
                    step(nc.vector.tensor_copy(run[h][:, :, S], top[h][:, 1:1 + B]))
                    assert n[0] == per, n
            dve.wait_ge(stepped, INIT + per * 2 * IT)
            nc.vector.tensor_copy(final[:], run[1][:, B - 1, :]).then_inc(stepped, 1)


def complete_softmax(nc, sig, link, final, fix_at, running, ends, agg, groups, beside):
    S, W = C + 1, C + 2
    with ExitStack() as ctx:
        def sb(name, shape):
            return ctx.enter_context(nc.sbuf_tensor(name, shape, F32))

        fixed, diag, tops, weight_t, weight = sb("m_fixed", [P, W]), sb("m_diag", [P, P]), sb("m_tops", [P, P]), sb("m_weight_t", [P, P]), sb("m_weight", [P, P])
        top, neg, scale = sb("m_top", [P, 1]), sb("m_neg", [P, 1]), sb("m_scale", [P, 1])
        ps = ctx.enter_context(nc.psum_tensor("m_ps", [P, 512], F32))
        pt = ctx.enter_context(nc.psum_tensor("m_pt", [P, 512], F32))
        block = ctx.enter_context(nc.Block())
        fetched, pe_s, act_s, dve_s = sig["fetched"], sig["pe_step"], sig["act_step"], sig["dve_step"]

        @block.gpsimd
        def _(pool):
            pool.indirect_dma_start(out=fixed[:], out_offset=None, in_=running, in_offset=offsets(fix_at[:])).then_inc(fetched.sem, 16)
            pool.wait_ge(dve_s.sem, dve_s.base + 8)
            pool.indirect_dma_start(out=running, out_offset=offsets(fix_at[:]), in_=fixed[:], in_offset=None).then_inc(fetched.sem, 16)
            pool.wait_ge(fetched.sem, fetched.base + 32)
            for j in range(J):
                pool.indirect_dma_start(out=agg[:, j, :], out_offset=None, in_=running, in_offset=offsets(ends[:, j:j + 1])).then_inc(groups[j // GROUP_SLOTS].sem, 16)
            for group in groups:
                pool.wait_ge(group.sem, group.base + 16 * GROUP_SLOTS)

        @block.tensor
        def _(pe):
            nc.tensor.transpose(pt[:, 0:P], link[:], sig["ident"][:]).then_inc(pe_s.sem, 1)
            pe.wait_ge(dve_s.sem, dve_s.base + 1)
            nc.tensor.matmul(ps[:, 0:P], sig["ones"][:], diag[:], start=True, stop=True).then_inc(pe_s.sem, 1)
            pe.wait_ge(act_s.sem, act_s.base + 1)
            nc.tensor.transpose(pt[:, P:2 * P], weight_t[:], sig["ident"][:]).then_inc(pe_s.sem, 1)
            pe.wait_ge(dve_s.sem, dve_s.base + 7)
            nc.tensor.matmul(ps[:, P:P + S], weight[:], final[:, 0:S], start=True, stop=True).then_inc(pe_s.sem, 1)

        @block.scalar
        def _(act):
            act.wait_ge(dve_s.sem, dve_s.base + 6)
            nc.scalar.activation(weight_t[:], tops[:], ACT.Exp, bias=neg[:]).then_inc(act_s.sem, 1)
            nc.scalar.activation(scale[:], fixed[:, S:W], ACT.Exp, bias=neg[:]).then_inc(act_s.sem, 1)

        @block.vector
        def _(dve):
            step = Chain(dve, dve_s.sem, dve_s.base)
            step(nc.vector.tensor_scalar(diag[:], sig["ident"][:], final[:, S:W], None, ALU.mult))
            dve.wait_ge(pe_s.sem, pe_s.base + 2)
            step(nc.vector.tensor_scalar(tops[:], pt[:, 0:P], BIG, -BIG, ALU.mult, ALU.add))
            step(nc.vector.tensor_tensor(tops[:], tops[:], ps[:, 0:P], ALU.add))
            step(nc.vector.tensor_reduce(top[:], tops[:], AX.X, ALU.max))
            dve.wait_ge(fetched.sem, fetched.base + 16)
            step(nc.vector.tensor_tensor(top[:], top[:], fixed[:, S:W], ALU.max))
            step(nc.vector.tensor_scalar(neg[:], top[:], -1.0, None, ALU.mult))
            dve.wait_ge(pe_s.sem, pe_s.base + 3)
            step(nc.vector.tensor_copy(weight[:], pt[:, P:2 * P]))
            dve.wait_ge(pe_s.sem, pe_s.base + 4)
            dve.wait_ge(act_s.sem, act_s.base + 2)
            step(nc.vector.scalar_tensor_tensor(fixed[:, 0:S], fixed[:, 0:S], scale[:], ps[:, P:P + S], ALU.mult, ALU.add))

        fetched.base += 32
        for group in groups:
            group.base += 16 * GROUP_SLOTS
        pe_s.base += 4
        act_s.base += 2
        dve_s.base += 8
        beside(block, ctx)


def on_vector(nc, sig, body, block=None):
    with ExitStack() as ctx:
        block = block or ctx.enter_context(nc.Block())

        @block.vector
        def _(dve):
            step = Chain(dve, sig["dve_step"].sem, sig["dve_step"].base)
            body(step)
            sig["dve_step"].base = step.n


def on_groups(nc, sig, prepare, block):
    @block.vector
    def _(dve):
        step = Chain(dve, sig["dve_step"].sem, sig["dve_step"].base)
        for g in range(J // GROUP_SLOTS):
            prepare(dve, step, g, slice(g * GROUP_SLOTS, (g + 1) * GROUP_SLOTS))
        sig["dve_step"].base = step.n


def moves(nc, sig, copies, block=None, after=0):
    with ExitStack() as ctx:
        block = block or ctx.enter_context(nc.Block())
        moved = sig["moved"]

        @block.sync
        def _(sp):
            if after:
                sp.wait_ge(sig["dve_step"].sem, after)
            for to, of in copies:
                sp.dma_start(to, of).then_inc(moved.sem, 16)
            sp.wait_ge(moved.sem, moved.base + 16 * len(copies))

        moved.base += 16 * len(copies)


def gnn(nc, out, x, src, dst, u, ew, labels, label_rows, attrs, spline1, root1, bias01, spline2, root2, bias02,
        w_att, bias1, trans, trans_t, att, edge_att, agg_weights, gw1, gb1, gw2, gb2, gw3, gb3, lw, lb,
        wn, wn_t, we, we_t, att_src, att_dst, att_edge, stop=None):
    V = nc.vector
    with ExitStack() as ctx:
        def dram(name, shape):
            return nc.dram_tensor(name, shape, F32, kind="Internal").ap()

        def sb(name, shape, dt=F32, scope=ctx):
            return scope.enter_context(nc.sbuf_tensor(name, shape, dt))

        sig = {n: Signal(ctx.enter_context(nc.semaphore(n))) for n in
               ("copied", "turned", "turned_sb", "product", "saved", "fetched", "pe_step", "act_step", "dve_step", "pool_step", "moved", "rounds")}

        groups = [Signal(ctx.enter_context(nc.semaphore(f"fetched_group{g}"))) for g in range(J // GROUP_SLOTS)]

        spline_table = dram("spline_table", [NP, 2 * C])
        att_table = dram("att_table", [NP, 2 * C + 1])
        gcn_table = [dram(f"gcn_table{k}", [NP, c]) for k, c in enumerate((16, 16, 32))]
        soft_table = dram("soft_table", [NP, C + 2])
        range_table = dram("range_table", [NP, 1])
        running = {w: dram(f"running{w}", [EP + 1, w]) for w in (C + 1, C, 16, 32, C + 2)}
        running_dst, running_src = dram("running_dst", [EP + 1, RUN]), dram("running_src", [EP + 1, RUN])
        begun_x, begun_s, sent = dram("begun_x", [EP, C]), dram("begun_s", [EP, 1]), dram("sent", [EP, SENT])

        def nodes(table):
            return table.rearrange("(p j) c -> p j c", p=P)

        def steps(rows):
            return rows.rearrange("(p t) c -> p t c", p=P)

        with nc.Block() as block:
            @block.sync
            def _(sp):
                for name in ("copied", "turned", "turned_sb", "product", "saved"):
                    sp.sem_inc(sig[name].sem, 2)
                    sig[name].base = 2

        for name in ("ident", "ones", "upper", "shift1", "shift2"):
            sig[name] = sb(name, [P, P])
        sig["iota"] = sb("iota", [P, CLASSES * P])
        sig["ident_b"], sig["not_earlier"] = sb("ident_b", [P, P], BF16), sb("not_earlier", [P, P], BF16)
        chunk_row = sb("chunk_row", [P, 1])
        zeros = sb("zeros", [P, max(B, J - REST) * C])
        src_i = sb("src_i", [P, T + B], I32)
        keep = sb("keep", [P, T + B])
        ew_s = sb("ew_s", [P, T + B])
        rank = sb("rank", [P, T + B])
        src_lo, src_hi = (sb(n, [P, T + B], BF16) for n in ("src_lo", "src_hi"))
        first_dst, first_dst_f, last_dst_f, fix_dst = sb("first_dst", [P, 1], I32), sb("first_dst_f", [P, 1]), sb("last_dst_f", [P, 1]), sb("fix_dst", [P, 1], I32)
        link, step_pen, use_pen = sb("link", [P, P]), sb("step_pen", [P, P]), sb("use_pen", [P, P])
        xs = sb("xs", [P, J, C])
        y = sb("y", [P, J, C])
        final = sb("final", [P, 4 * C])
        cnt_dst, cnt_src, begin_dst, begin_src = (sb(n, [P, J]) for n in ("cnt_dst", "cnt_src", "begin_dst", "begin_src"))
        end_dst, first_at, end_src = (sb(n, [P, J], I32) for n in ("end_dst", "first_at", "end_src"))
        r_dst, r_src, ew_sum, dinv = (sb(n, [P, J]) for n in ("r_dst", "r_src", "ew_sum", "dinv"))

        w_src, w_dst, b1 = sb("w_src", [P, C]), sb("w_dst", [P, C]), sb("b1", [P, C])
        w_ef, w_lab, twt = sb("w_ef", [C, 2, C]), sb("w_lab", [2 * LABELS, C]), sb("twt", [C, 3 * LABELS])
        tw, ea, tw_att = sb("tw", [LABELS, C]), sb("ea", [C, 1]), sb("tw_att", [LABELS, 1])
        w_labels = sb("w_labels", [B * LABELS, B, C])
        att_b, mix = sb("att_b", [P, C]), sb("mix", [P, 3])
        w1, w2, w3 = sb("gw1s", [C, 16]), sb("gw2s", [16, 32]), sb("gw3s", [32, C])
        gb = [sb(f"gb{k}", [P, c]) for k, c in enumerate((16, 32, C))]
        lws = [sb(f"lws{k}", [C, C]) for k in range(2)]
        lbs = sb("lbs", [P, C])
        wns, wnt, a_cols = sb("wns", [C, C + 2]), sb("wnt", [C, C]), sb("a_cols", [C, 2])
        wes, wet, ae, w_edge_att = sb("wes", [EDIM, C]), sb("wet", [C, EDIM]), sb("ae", [C, 1]), sb("w_edge_att", [EDIM, 1])
        later_weights = [
            (w_src[:], w_att[0:2 * C, :]), (w_dst[:], w_att[2 * C:4 * C, :]), (w_ef[:, 0, :], w_att[C:2 * C, :]), (w_ef[:, 1, :], w_att[3 * C:4 * C, :]),
            (b1[:], bias1.broadcast_to([P, C])), (tw[:], trans), (twt[:, 0:LABELS], trans_t), (twt[:, LABELS:2 * LABELS], zeros[0:C, 0:LABELS]),
            (twt[:, 2 * LABELS:3 * LABELS], trans_t), (ea[:], edge_att), (att_b[:], att.broadcast_to([P, C])), (mix[:], agg_weights.broadcast_to([P, 3])),
            *((w_labels[k * LABELS:(k + 1) * LABELS, k, :], trans) for k in range(B)),
            (w1[:], gw1), (w2[:], gw2), (w3[:], gw3), (gb[0][:], gb1.broadcast_to([P, 16])), (gb[1][:], gb2.broadcast_to([P, 32])),
            (gb[2][:], gb3.broadcast_to([P, C])), (lws[0][:], lw[0:C, :]), (lws[1][:], lw[C:2 * C, :]), (lbs[:], lb.broadcast_to([P, C])),
            (wns[:, 0:C], wn), (wnt[:], wn_t), (wes[:], we), (wet[:], we_t), (ae[:], att_edge), (a_cols[:, 0:1], att_src), (a_cols[:, 1:2], att_dst)]

        l0 = ctx.enter_context(ExitStack())
        u_s = sb("u_s", [P, T + B], F32, l0)
        dst_lo, dst_hi = (sb(n, [P, T + B], BF16, l0) for n in ("dst_lo", "dst_hi"))
        w0 = [sb(f"w0_{k}", [C, 3 * C], F32, l0) for k in range(2)]
        b0 = [sb(f"b0_{k}", [P, C], F32, l0) for k in range(2)]

        with ExitStack() as tmp:
            dst_i, prev_i = sb("dst_i", [P, T], I32, tmp), sb("prev_i", [P, T], I32, tmp)
            dst_f, prev_f = sb("dst_f", [P, T], F32, tmp), sb("prev_f", [P, T], F32, tmp)
            many = sb("many", [P, 1], F32, tmp)
            blank_node = zeros[0:1, 0:(J - REST) * C]
            with nc.Block() as block:
                pool_s, moved, dve_s = sig["pool_step"], sig["moved"], sig["dve_step"]
                dst_flat = dst.rearrange("p t -> (p t)")

                @block.sync
                def _(sp):
                    sp.wait_ge(dve_s.sem, 1)
                    n = 0
                    for to, of in (
                        (src_i[:, 0:T], src), (dst_i[:], dst),
                        (prev_i[1:P, :], dst_flat[T - 1:EP - 1].rearrange("(p t) -> p t", t=T)), (prev_i[0:1, 1:T], dst[0:1, 0:T - 1]),
                        (ew_s[:, 0:T], ew), (u_s[:, 0:T], u),
                        (xs[0:LAST, :, :], x[0:LAST * J, :].rearrange("(p j) c -> p j c", j=J)),
                        (xs[LAST:LAST + 1, 0:REST, :], x[LAST * J:N, :].unsqueeze(0)),
                        (xs[LAST:LAST + 1, REST:J, :], blank_node.rearrange("p (j c) -> p j c", c=C)),
                        *((w0[k][:, n0 * C:(n0 + 1) * C], w) for k, ws in enumerate(((spline1[0], spline1[1], root1), (spline2[0], spline2[1], root2)))
                          for n0, w in enumerate(ws)),
                        *((b0[k][:], b.broadcast_to([P, C])) for k, b in enumerate((bias01, bias02))),
                    ):
                        sp.dma_start(to, of).then_inc(moved.sem, 16)
                        n += 1
                    sp.wait_ge(moved.sem, 16 * n)
                    moved.base += 16 * n

                @block.gpsimd
                def _(pool):
                    step = Chain(pool, pool_s.sem)
                    step(pool.iota(sig["iota"][:], [[1, CLASSES * P]], base=0, channel_multiplier=0, allow_small_or_imprecise_dtypes=True))
                    step(pool.iota(chunk_row[:], [[0, 1]], base=-1, channel_multiplier=T, allow_small_or_imprecise_dtypes=True))
                    step(pool.memset(sig["ones"][:], 1.0))
                    for name in ("ident", "shift1", "shift2", "ident_b", "not_earlier"):
                        step(pool.memset(sig[name][:], 0.0))

                    def select(name, of, op, base, fill):
                        step(pool.affine_select(out=sig[name][:], in_=sig[of][:], compare_op=op, fill=fill, base=base, pattern=[[1, P]], channel_multiplier=-1))

                    select("ident", "ident", ALU.not_equal, 0, 1.0)
                    select("ident_b", "ident_b", ALU.not_equal, 0, 1.0)
                    select("shift1", "shift1", ALU.not_equal, -1, 1.0)
                    select("shift2", "shift2", ALU.not_equal, -2, 1.0)
                    select("upper", "ones", ALU.is_gt, 0, 0.0)
                    select("not_earlier", "not_earlier", ALU.is_gt, 0, -1.0)

                @block.vector
                def _(dve):
                    step = Chain(dve, dve_s.sem)
                    step(V.memset(zeros[:], 0.0))
                    step(V.memset(prev_i[0:1, 0:1], -1))
                    step(V.memset(cnt_src[:], 0.0))
                    step(V.memset(w_labels[:], 0.0))
                    for t in (src_i, keep, ew_s, rank, u_s, dst_lo, dst_hi, src_lo, src_hi):
                        step(V.memset(t[:, T:T + B], 0))
                    dve.wait_ge(moved.sem, 16 * 17)
                    step(V.tensor_copy(dst_f[:], dst_i[:]))
                    step(V.tensor_copy(prev_f[:], prev_i[:]))
                    step(V.tensor_tensor(keep[:, 0:T], dst_f[:], prev_f[:], ALU.is_equal))
                    step(V.tensor_copy(first_dst[:], dst_i[:, 0:1]))
                    step(V.tensor_copy(first_dst_f[:], dst_f[:, 0:1]))
                    step(V.tensor_copy(last_dst_f[:], dst_f[:, T - 1:T]))
                    step(V.tensor_scalar(prev_f[:], dst_f[:], first_dst_f[:], None, ALU.is_equal))
                    step(V.tensor_reduce(many[:], prev_f[:], AX.X, ALU.add))
                    dve.wait_ge(pool_s.sem, 2)
                    step(V.tensor_tensor(fix_dst[:], many[:], chunk_row[:], ALU.add))

                    def split(key, lo, lo_b, hi):
                        step(V.tensor_scalar(lo, key, -float(J // 2), 1.0 / J, ALU.add, ALU.mult))
                        step(V.tensor_scalar(lo, lo, ROUND, None, ALU.add))
                        step(V.tensor_scalar(lo, lo, -ROUND, None, ALU.add))
                        step(V.scalar_tensor_tensor(hi, lo, -float(J), key, ALU.mult, ALU.add))
                        step(V.tensor_copy(lo_b, lo))

                    split(dst_f[:], prev_f[:], dst_lo[:, 0:T], dst_hi[:, 0:T])
                    step(V.tensor_copy(prev_f[:], src_i[:, 0:T]))
                    split(prev_f[:], dst_f[:], src_lo[:, 0:T], src_hi[:, 0:T])
                    for k in range(2):
                        step(V.tensor_tensor(w0[k][:, C:2 * C], w0[k][:, C:2 * C], w0[k][:, 0:C], ALU.subtract))
                    dve_s.base = step.n

        carry_masks(nc, sig, first_dst_f[:], last_dst_f[:], link, step_pen, use_pen)
        carries = (link, step_pen, use_pen)

        with ExitStack() as tmp:
            d, own = sb("d", [P, J, 2 * C], F32, tmp), sb("own", [P, J, C], F32, tmp)
            h = sb("h0", [P, J, C], F32, tmp)
            dense(nc, sig, [xs], [w0[0][:, 0:2 * C]], d, 2 * C, nodes(spline_table))
            for k in range(2):
                node_rows, to = (xs, h) if k == 0 else (h, y)
                width = C + 1 if k == 0 else C
                edge = {"src": src_i, "keep": keep, "weight": u_s, "src_lo": src_lo, "src_hi": src_hi, "rank": rank, "seen": cnt_src, "ranked": k * RANKED}
                if k == 0:
                    edge |= {"extra": ew_s, "dst_lo": dst_lo, "dst_hi": dst_hi, "count": cnt_dst}
                spline_pass(nc, sig, spline_table, width, edge, running[width], final, zeros,
                            cleared=() if k == 0 else (steps(begun_x), steps(begun_s)))
                with ExitStack() as fetch:
                    if k == 0:
                        node_ranges(nc, sig, cnt_dst, begin_dst, end_dst, first_at)
                    agg_k = sb(f"agg0_{k}", [P, J, width], F32, fetch)

                    def mean_and_own(dve, step, g, cut):
                        dve.wait_ge(groups[g].sem, groups[g].base)
                        step(V.tensor_tensor(to[:, cut, :], agg_k[:, cut, 0:C], spread(r_dst[:, cut], C), ALU.mult))
                        step(V.tensor_tensor(to[:, cut, :], to[:, cut, :], own[:, cut, :], ALU.add))

                    def inverse_degree(step):
                        step(V.tensor_scalar(r_dst[:], cnt_dst[:], 1.0, None, ALU.max))
                        step(V.reciprocal(r_dst[:], r_dst[:]))

                    def beside(block, scope):
                        dense(nc, sig, [node_rows], [w0[k][:, 2 * C:3 * C]], own, C, bias=b0[0][:] if k == 0 else y, block=block, scope=scope)
                        if k == 0:
                            on_vector(nc, sig, inverse_degree, block)
                            dense(nc, sig, [h], [w0[1][:, 0:2 * C]], d, 2 * C, nodes(spline_table), block=block, scope=scope, prepare=mean_and_own)

                            def keep_and_residual(step):
                                step(V.tensor_copy(ew_sum[:], agg_k[:, :, C]))
                                step(V.tensor_tensor(y[:], xs[:], repeat(b0[1][:], J), ALU.add))

                            on_vector(nc, sig, keep_and_residual, block)
                        else:
                            node_ranges(nc, sig, cnt_src, begin_src, end_src, None, block, scope)
                            moves(nc, sig, later_weights, block)
                            layer_norm(nc, sig, y, xs, block, scope, mean_and_own)

                    complete_and_fetch(nc, sig, carries, final, width, width, fix_dst, running[width], end_dst, agg_k, beside=beside, groups=groups)
        l0.close()
        src_key = rank

        def finish():
            moves(nc, sig, [(out[0:LAST * J, :].rearrange("(p j) c -> p j c", j=J), xs[0:LAST, :, :]),
                            (out[LAST * J:N, :].unsqueeze(0), xs[LAST:LAST + 1, 0:REST, :])])

        if stop == 0:
            return finish()

        with ExitStack() as tmp:
            mix_sum = sb("mix_sum", [P, 1], F32, tmp)
            share, some = sb("share", [P, J], F32, tmp), sb("some", [P, J], F32, tmp)
            first_rows = sb("first_rows", [P, 2 * C + 1], F32, tmp)
            with ExitStack() as rows:
                t1 = sb("t1", [P, J, 2 * C + 1], F32, rows)

                with ExitStack() as c2:
                    ps = c2.enter_context(nc.psum_tensor("p_label_att", [P, 512], F32))
                    block = c2.enter_context(nc.Block())
                    act_s, pe_s, dve_s = sig["act_step"], sig["pe_step"], sig["dve_step"]
                    TABLE, SHIFTED, DEGREES = dve_s.base + 4, dve_s.base + 6, dve_s.base + 9

                    @block.scalar
                    def _(act):
                        act.wait_ge(dve_s.sem, SHIFTED)
                        nc.scalar.activation(mix[:], mix[:], ACT.Exp).then_inc(act_s.sem, 1)
                        act.wait_ge(dve_s.sem, DEGREES)
                        nc.scalar.activation(dinv[:], ew_sum[:], ACT.Sqrt).then_inc(act_s.sem, 1)

                    @block.tensor
                    def _(pe):
                        nc.tensor.matmul(ps[0:LABELS, 0:1], twt[:, 0:LABELS], ea[:], start=True, stop=True).then_inc(pe_s.sem, 1)
                        nc.tensor.matmul(ps[0:2 * LABELS, C:2 * C], twt[:, 0:2 * LABELS], w_ef[:, 0, :], start=True, stop=False)
                        nc.tensor.matmul(ps[0:2 * LABELS, C:2 * C], twt[:, LABELS:3 * LABELS], w_ef[:, 1, :], start=False, stop=True).then_inc(pe_s.sem, 1)

                    @block.vector
                    def _(dve):
                        step = Chain(dve, dve_s.sem, dve_s.base)
                        step(V.tensor_tensor(t1[:, :, 0:C], xs[:], repeat(att_b[:], J), ALU.mult))
                        step(V.tensor_copy(t1[:, :, C:2 * C], xs[:]))
                        step(V.tensor_copy(t1[:, :, 2 * C], begin_src[:]))
                        step(V.tensor_copy(begin_dst[:], end_src[:]))
                        assert step.n == TABLE
                        step(V.tensor_reduce(mix_sum[:], mix[:], AX.X, ALU.max))
                        step(V.tensor_scalar(mix[:], mix[:], mix_sum[:], None, ALU.subtract))
                        assert step.n == SHIFTED
                        step(V.tensor_scalar(ew_sum[:], ew_sum[:], 1.0, None, ALU.add))
                        step(V.tensor_scalar(some[:], ew_sum[:], 0.0, None, ALU.is_gt))
                        step(V.tensor_scalar(ew_sum[:], ew_sum[:], 1.0e-30, None, ALU.max))
                        assert step.n == DEGREES
                        step(V.tensor_scalar(r_src[:], cnt_src[:], 1.0, None, ALU.max))
                        step(V.reciprocal(r_src[:], r_src[:]))
                        dve.wait_ge(pe_s.sem, pe_s.base + 2)
                        step(V.tensor_copy(tw_att[:], ps[0:LABELS, 0:1]))
                        step(V.tensor_copy(w_lab[:], ps[0:2 * LABELS, C:2 * C]))
                        dve.wait_ge(act_s.sem, act_s.base + 1)
                        step(V.tensor_reduce(mix_sum[:], mix[:], AX.X, ALU.add))
                        step(V.reciprocal(mix_sum[:], mix_sum[:]))
                        step(V.tensor_scalar(mix[:], mix[:], mix_sum[:], None, ALU.mult))
                        step(V.tensor_tensor(lws[0][:], lws[0][:], sig["ident"][0:C, 0:C], ALU.add))
                        dve.wait_ge(act_s.sem, act_s.base + 2)
                        step(V.reciprocal(dinv[:], dinv[:]))
                        step(V.tensor_tensor(dinv[:], dinv[:], some[:], ALU.mult))
                        dve_s.base = step.n

                    act_s.base += 2
                    pe_s.base += 2
                    moves(nc, sig, [(nodes(att_table), t1[:]), (nodes(range_table), begin_dst[:].unsqueeze(2))], block, TABLE)
                    spread_to_edges(nc, sig, block, xs, first_at, begun_x, att_table, first_dst[:], first_rows)
            attention_pass(nc, sig, att_table, {"src": src_i, "keep": keep, "rank": rank}, labels, label_rows, begun_x, first_rows, tw[:], tw_att[:],
                           running_dst, final[:, 0:RUN], sent, zeros)

            def combine(agg, side, x0, lab0, cnt_r, to, block=None):
                def body(step):
                    step(V.tensor_scalar(share[:], cnt_r[:], mix[:, 0:1], mix[:, 2:3], ALU.mult, ALU.add))
                    step(V.tensor_tensor(to[:, :, 0:C], agg[:, :, x0:x0 + C], spread(share[:], C), ALU.mult))
                    step(V.scalar_tensor_tensor(to[:, :, 0:C], agg[:, :, SUMS:SUMS + C], mix[:, 1:2], to[:, :, 0:C], ALU.mult, ALU.add))
                    step(V.tensor_scalar(to[:, :, C:2 * C], agg[:, :, SUMS + C:RUN], mix[:, 1:2], None, ALU.mult))
                    step(V.tensor_tensor(comb_lab[:, :, side * LABELS:(side + 1) * LABELS], agg[:, :, lab0:lab0 + LABELS], spread(share[:], LABELS), ALU.mult))

                on_vector(nc, sig, body, block)

            SUMS = C + LABELS
            agg_dst = sb("agg_dst", [P, J, RUN], F32, tmp)
            ends = sb("ends", [P, 4], F32, tmp)
            link_s, step_pen_s, use_pen_s = sb("link_s", [P, P], F32, tmp), sb("step_pen_s", [P, P], F32, tmp), sb("use_pen_s", [P, P], F32, tmp)

            def over_sources(block, scope):
                moved = sig["moved"]
                sent_v = sent.rearrange("(p t) c -> p t c", p=P)
                moves(nc, sig, [(ends[:, 0:2], sent_v[:, 0, 0:2]), (ends[:, 2:4], sent_v[:, T - 1, 0:2])], block)
                carry_masks(nc, sig, ends[:, 0:1], ends[:, 2:3], link_s, step_pen_s, use_pen_s, block, scope,
                            ready=lambda dve: dve.wait_ge(moved.sem, moved.base))
                source_pass(nc, sig, block, scope, sent, w_labels, running_src, final, zeros)

            complete_and_fetch(nc, sig, carries, final, SUMS, RUN, fix_dst, running_dst, end_dst, agg_dst, beside=over_sources)
            first_src, fix_src, end_first = sb("first_src", [P, 1], I32, tmp), sb("fix_src", [P, 1], I32, tmp), sb("end_first", [P, 1], F32, tmp)
            chunk_end = sb("chunk_end", [P, 1], F32, tmp)
            with nc.Block() as block:
                fetched, dve_s = sig["fetched"], sig["dve_step"]

                @block.gpsimd
                def _(pool):
                    pool.wait_ge(dve_s.sem, dve_s.base + 1)
                    pool.indirect_dma_start(out=end_first[:], out_offset=None, in_=range_table, in_offset=offsets(first_src[:])).then_inc(fetched.sem, 16)

                @block.vector
                def _(dve):
                    step = Chain(dve, dve_s.sem, dve_s.base)
                    step(V.tensor_copy(first_src[:], ends[:, 0:1]))
                    step(V.tensor_scalar(chunk_end[:], chunk_row[:], float(T), None, ALU.add))
                    dve.wait_ge(fetched.sem, fetched.base + 16)
                    step(V.tensor_tensor(fix_src[:], end_first[:], chunk_end[:], ALU.min))
                    dve_s.base = step.n

                fetched.base += 16
            comb_dst, comb_lab = sb("comb_dst", [P, J, 2 * C], F32, tmp), sb("comb_lab", [P, J, 2 * LABELS], F32, tmp)
            with ExitStack() as rows:
                agg_src = sb("agg_src", [P, J, RUN], F32, rows)

                def of_destinations(block, scope):
                    combine(agg_dst, 1, LABELS, 0, r_dst, comb_dst, block)
                    dense(nc, sig, [comb_dst], [w_dst[:]], y, C, bias=b1[:], block=block, scope=scope, ready=sig["dve_step"].base)
                    on_vector(nc, sig, lambda step: (step(V.tensor_tensor(y[:], y[:], xs[:], ALU.add)), class_keys(step)), block)

                def class_keys(step):
                    in_class = flat(agg_dst[:])[:, 0:T + B]
                    step(V.tensor_copy(src_key[:], src_lo[:]))
                    for q in range(CLASSES - 1, 0, -1):
                        step(V.tensor_scalar(in_class, src_hi[:], q * CLASS - 0.5, None, ALU.is_gt))
                        step(V.scalar_tensor_tensor(src_key[:], in_class, float(P * q), src_key[:], ALU.mult, ALU.add))
                        step(V.scalar_tensor_tensor(src_hi[:], in_class, -float(CLASS * q), src_hi[:], ALU.mult, ALU.add))

                complete_and_fetch(nc, sig, (link_s, step_pen_s, use_pen_s), final, SUMS, RUN, fix_src, running_src, end_src, agg_src,
                                   beside=of_destinations)
                comb_src = agg_dst[:, :, 0:2 * C]
                combine(agg_src, 0, LABELS, 0, r_src, comb_src)
            dense(nc, sig, [comb_src, comb_lab], [w_src[:], w_lab[:]], y, C, bias=y)
            layer_norm(nc, sig, y, xs)
        if stop == 1:
            return finish()

        with ExitStack() as tmp:
            widths = (16, 16, 32)
            t = [sb(f"gt{k}", [P, J, c], F32, tmp) for k, c in enumerate(widths)]
            agg = [sb(f"gagg{k}", [P, J, c], F32, tmp) for k, c in enumerate(widths)]
            x2, x3, x4 = sb("x2", [P, J, 16], F32, tmp), sb("x3", [P, J, 32], F32, tmp), sb("x4", [P, J, C], F32, tmp)
            def convolve(k, make, beside):
                c = widths[k]
                with ExitStack() as split:
                    parts = [sb(f"part{k}_{n}", [P, c // SLICE, CLASSES * CLASS, SLICE], BF16, split) for n in range(3)]
                    store_and_split(nc, sig, make, t[k], c, nodes(gcn_table[k]), parts)
                    edge = {"src": src_i, "src_key": src_key, "src_slot": src_hi, "keep": keep, "weight": ew_s}
                    graph_pass(nc, sig, gcn_table[k], c, edge, parts, running[c], final, zeros)

                def own_part(dve, step, g, cut):
                    dve.wait_ge(groups[g].sem, groups[g].base)
                    step(V.tensor_tensor(agg[k][:, cut, :], agg[k][:, cut, :], t[k][:, cut, :], ALU.add))
                    step(V.tensor_tensor(agg[k][:, cut, :], agg[k][:, cut, :], spread(dinv[:, cut], c), ALU.mult))

                complete_and_fetch(nc, sig, carries, final, c, c, fix_dst, running[c], end_dst, agg[k],
                                   beside=lambda block, scope: beside(block, scope, own_part), groups=groups)

            def relu(step, h):
                step(V.tensor_scalar(flat(h[:]), flat(h[:]), 0.0, None, ALU.max))

            def scaled(step, to, h, c):
                step(V.tensor_tensor(to[:], h[:], spread(dinv[:], c), ALU.mult))

            def second_table(step):
                step(V.tensor_tensor(agg[0][:], agg[0][:], repeat(gb[0][:], J), ALU.add))
                relu(step, agg[0])
                scaled(step, t[1], agg[0], 16)

            def third_table(step):
                relu(step, x3)
                scaled(step, t[2], x3, 32)

            def after_third(block, scope, own_part):
                dense(nc, sig, [xs], [lws[0][:]], y, C, bias=lbs[:], block=block, scope=scope)
                dense(nc, sig, [agg[2]], [w3[:]], x4, C, bias=gb[2][:], block=block, scope=scope, prepare=own_part)

            dense(nc, sig, [xs], [w1[:]], x2, 16)
            convolve(0, lambda step: scaled(step, t[0], x2, 16), lambda block, _, own_part: on_groups(nc, sig, own_part, block))
            convolve(1, second_table, lambda block, scope, own_part: dense(nc, sig, [agg[1]], [w2[:]], x3, 32, bias=gb[1][:], block=block, scope=scope, prepare=own_part))
            convolve(2, third_table, after_third)
            on_vector(nc, sig, lambda step: relu(step, x4))
            dense(nc, sig, [x4], [lws[1][:]], y, C, bias=y)
            layer_norm(nc, sig, y, xs)
        if stop == 2:
            return finish()

        with ExitStack() as tmp:
            t3 = sb("t3", [P, J, C + 2], F32, tmp)
            first_rows = sb("first_rows3", [P, C + 2], F32, tmp)
            at_dst, begun = sb("at_dst", [P, T + B], F32, tmp), sb("begun3", [P, T], F32, tmp)
            with ExitStack() as c2:
                ps = c2.enter_context(nc.psum_tensor("p_edge_att", [P, 512], F32))
                block = c2.enter_context(nc.Block())
                pe_s, dve_s = sig["pe_step"], sig["dve_step"]

                @block.tensor
                def _(pe):
                    nc.tensor.matmul(ps[0:EDIM, 0:1], wet[:], ae[:], start=True, stop=True).then_inc(pe_s.sem, 1)
                    nc.tensor.matmul(ps[0:C, 1:3], wnt[:], a_cols[:], start=True, stop=True).then_inc(pe_s.sem, 1)

                @block.vector
                def _(dve):
                    step = Chain(dve, dve_s.sem, dve_s.base)
                    dve.wait_ge(pe_s.sem, pe_s.base + 2)
                    step(V.tensor_copy(w_edge_att[:], ps[0:EDIM, 0:1]))
                    step(V.tensor_copy(wns[:, C:C + 2], ps[0:C, 1:3]))
                    dve_s.base = step.n

                pe_s.base += 2
            with ExitStack() as scope:
                block = scope.enter_context(nc.Block())
                saved = sig["saved"].base
                dense(nc, sig, [xs], [wns[:]], t3, C + 2, nodes(soft_table), block=block, scope=scope)
                spread_to_edges(nc, sig, block, t3[:, :, C + 1:C + 2], first_at, begun_s, soft_table, first_dst[:], first_rows, saved)
            moves(nc, sig, [(begun[:], begun_s.rearrange("(p t) c -> p (t c)", p=P))])

            def held(step):
                step(V.memset(at_dst[:, T:T + B], 0.0))
                step(V.tensor_tensor_scan(at_dst[:, 0:T], keep[:, 0:T], begun[:], first_rows[:, C + 1:C + 2], ALU.mult, ALU.add))

            on_vector(nc, sig, held)
            softmax_pass(nc, sig, soft_table, {"src": src_i, "keep": keep, "at_dst": at_dst}, attrs, wes[:], w_edge_att[:], running[C + 2], final[:, 0:C + 2], zeros)
            agg = sb("agg3", [P, J, C + 2], F32, tmp)

            def normalised(dve, step, g, cut):
                dve.wait_ge(groups[g].sem, groups[g].base)
                step(V.tensor_scalar(r_src[:, cut], agg[:, cut, C], 1.0e-8, None, ALU.add))
                step(V.reciprocal(r_src[:, cut], r_src[:, cut]))
                step(V.tensor_tensor(y[:, cut, :], agg[:, cut, 0:C], spread(r_src[:, cut], C), ALU.mult))
                step(V.tensor_tensor(y[:, cut, :], y[:, cut, :], twice[:, cut, :], ALU.add))

            def after(block, scope):
                on_vector(nc, sig, lambda step: step(V.tensor_tensor(twice[:], xs[:], xs[:], ALU.add)), block)
                layer_norm(nc, sig, y, xs, block, scope, normalised)

            twice = sb("twice", [P, J, C], F32, tmp)
            complete_softmax(nc, sig, link, final, fix_dst, running[C + 2], end_dst, agg, groups, after)

        finish()


def kernel(**inputs):
    import concourse.bacc as bacc
    from concourse.bass_utils import run_bass_kernel_spmd

    def chunks(name, fill):
        a = np.asarray(inputs[name]).reshape(E)
        return np.concatenate([a, np.full(EP - E, fill, a.dtype)]).reshape(P, T)

    def steps(name):
        a = np.asarray(inputs[name])
        a = np.concatenate([a, np.zeros((EP - E, a.shape[1]), a.dtype)])
        return np.ascontiguousarray(a.reshape(P, T, -1).transpose(2, 1, 0)).reshape(a.shape[1], T * P)

    def rows(name):
        a = np.asarray(inputs[name])
        return np.concatenate([a, np.zeros((EP - E, a.shape[1]), a.dtype)]).reshape(P, T, -1)

    def plain(name):
        return np.ascontiguousarray(inputs[name])

    def row(name):
        return plain(name).reshape(1, -1)

    def turned(name):
        return np.ascontiguousarray(np.asarray(inputs[name]).T)

    arrays = {
        "x": plain("x"), "src": chunks("src", NP - 1), "dst": chunks("dst", NP - 1),
        "u": chunks("edge_weight1", 0), "ew": chunks("edge_weight", 0),
        "labels": steps("edge_attr_8"), "label_rows": rows("edge_attr_8"), "attrs": steps("edge_attr_16"),
        "spline1": plain("L0_gnn_w1"), "root1": plain("L0_gnn_root1"), "bias01": row("L0_gnn_b1"),
        "spline2": plain("L0_gnn_w2"), "root2": plain("L0_gnn_root2"), "bias02": row("L0_gnn_b2"),
        "w_att": plain("L1_gnn_weight"), "bias1": row("L1_gnn_bias"), "trans": plain("L1_gnn_trans_weight"), "trans_t": turned("L1_gnn_trans_weight"),
        "att": row("L1_gnn_attention_weight"), "edge_att": plain("L1_gnn_edge_attention_weight"), "agg_weights": row("L1_gnn_agg_weights"),
        "gw1": plain("L2_gnn_w1"), "gb1": row("L2_gnn_b1"), "gw2": plain("L2_gnn_w2"), "gb2": row("L2_gnn_b2"),
        "gw3": plain("L2_gnn_w3"), "gb3": row("L2_gnn_b3"), "lw": plain("L2_gnn_lw"), "lb": row("L2_gnn_lb"),
        "wn": plain("L3_gnn_Wn"), "wn_t": turned("L3_gnn_Wn"), "we": plain("L3_gnn_We"), "we_t": turned("L3_gnn_We"),
        "att_src": plain("L3_gnn_att_src").reshape(C, 1), "att_dst": plain("L3_gnn_att_dst").reshape(C, 1), "att_edge": plain("L3_gnn_att_edge").reshape(C, 1),
    }
    nc = bacc.Bacc("TRN2", target_bir_lowering=False, num_devices=1)
    args = {n: nc.dram_tensor(f"in_{n}", a.shape, mybir.dt.from_np(a.dtype), kind="ExternalInput").ap() for n, a in arrays.items()}
    out = nc.dram_tensor("out", [N, C], F32, kind="ExternalOutput").ap()
    gnn(nc, out, **args)
    r = run_bass_kernel_spmd(nc, [{f"in_{n}": a for n, a in arrays.items()}], core_ids=[0])
    return r.results[0]["out"]
```
